# Optimizing a Trainium2 kernel written in Bass

```python
import numpy as np
import jax
import jax.numpy as jnp

def _softmax(x, axis=-1):
    return jax.nn.softmax(x, axis=axis)

def _gelu(x):
    return jax.nn.gelu(x, approximate=True)

def _silu(x):
    return jax.nn.silu(x)

def _sigmoid(x):
    return jax.nn.sigmoid(x)

def _layernorm(x, axis=-1, eps=1e-05):
    m = jnp.mean(x, axis=axis, keepdims=True)
    v = jnp.var(x, axis=axis, keepdims=True)
    return (x - m) / jnp.sqrt(v + eps)

def _scatter_add(tgt, idx, src, axis=0):
    return tgt.at[idx].add(src)

def _segment_sum(src, seg, n):
    return jax.ops.segment_sum(src, seg, n)
kernel_name = 'mk_decoder_preln_d4_seqx_r8_c14df2'

def setup_inputs(seed: int=0):
    np.random.seed(seed)
    _w = jnp.asarray

    def _rec_inputs():
        import jax
        import jax.numpy as jnp
        _rk = jax.random.key(seed)
        x = 7.22e-05 + 1 * jax.random.normal(jax.random.fold_in(_rk, 1), (8, 128, 256), jnp.float32)
        _lenS = 128 - jax.random.randint(jax.random.fold_in(_rk, 7), (8,), 0, max(1, 128 // 4) + 1, jnp.int32)
        _lenS2 = 128 - jax.random.randint(jax.random.fold_in(_rk, 8), (8,), 0, max(1, 128 // 4) + 1, jnp.int32)
        _ctx_2048P = jax.random.normal(jax.random.fold_in(_rk, 11), (8, 16, 256), jnp.float32)
        _ctx_2048c = jax.random.dirichlet(jax.random.fold_in(_rk, 511), 0.3 * jnp.ones((16,), jnp.float32), (8, 128))
        _ctx_2048t = jnp.einsum('bsk,bkd->bsd', _ctx_2048c, _ctx_2048P)
        _ctx_2048t = _ctx_2048t * jax.lax.rsqrt(jnp.mean(jnp.square(_ctx_2048t)) + 1e-12) * 0.953939
        ctx_2048 = 4.13588e-05 + 0.999923 * (_ctx_2048t + 0.3 * jax.random.normal(jax.random.fold_in(_rk, 611), (8, 128, 256), jnp.float32))
        _validS = jnp.arange(128)[None, :] < _lenS[:, None]
        _validS2 = jnp.arange(128)[None, :] < _lenS2[:, None]
        _causal = jnp.tril(jnp.ones((128, 128), dtype=bool))
        mask_SxS2_bc0 = jnp.logical_not(jnp.broadcast_to(_validS2[0:1, :], (128, 128)))
        mask_BxS2_bk0 = jnp.logical_not(jnp.broadcast_to(_validS2[:, :], (8, 128)))
        return (x, ctx_2048, mask_SxS2_bc0, mask_BxS2_bk0)
    x, ctx_2048, mask_SxS2_bc0, mask_BxS2_bk0 = _rec_inputs()

    def _L0_attn_setup():
        import jax, jax.numpy as jnp
        import numpy as np
        BATCH, SEQ, D_MODEL, N_HEADS, D_HEAD = (2, 256, 256, 16, 128)
        ATTN_SCALE = np.sqrt(D_HEAD).astype(np.float32)
        IGNORE = jnp.float32(-100000.0)
        key = jax.random.key(seed)
        ks = jax.random.split(key, 5)
        init = 1.0 / np.sqrt(D_MODEL)
        return {'x': jax.random.normal(ks[0], (BATCH, SEQ, D_MODEL), jnp.float32), 'W_Q': jax.random.normal(ks[1], (N_HEADS, D_MODEL, D_HEAD), jnp.float32) * init, 'W_K': jax.random.normal(ks[2], (N_HEADS, D_MODEL, D_HEAD), jnp.float32) * init, 'W_V': jax.random.normal(ks[3], (N_HEADS, D_MODEL, D_HEAD), jnp.float32) * init, 'W_O': jax.random.normal(ks[4], (N_HEADS, D_HEAD, D_MODEL), jnp.float32) * init, 'b_Q': jnp.zeros((N_HEADS, D_HEAD), jnp.float32), 'b_K': jnp.zeros((N_HEADS, D_HEAD), jnp.float32), 'b_V': jnp.zeros((N_HEADS, D_HEAD), jnp.float32), 'b_O': jnp.zeros((D_MODEL,), jnp.float32)}
    _L0_attn_all = _L0_attn_setup()
    _L0_attn_in = {k: v for k, v in _L0_attn_all.items() if k in ('W_Q', 'W_K', 'W_V', 'W_O', 'b_Q', 'b_K', 'b_V', 'b_O')}
    del _L0_attn_all

    def _L0_xattn_setup():
        import jax, jax.numpy as jnp
        import numpy as np
        B, LQ, LKV = (4, 128, 128)
        HID, H, G = (256, 32, 8)
        HD = HID // H
        HPG = H // G
        key = jax.random.key(seed)
        ks = jax.random.split(key, 10)
        s = 0.02
        inp = {'X': jax.random.normal(ks[0], (B, LQ, HID), jnp.float32), 'encoder_output': jax.random.normal(ks[1], (B, LKV, HID), jnp.float32), 'causal_mask': jnp.triu(jnp.ones((LQ, LKV), bool), 1), 'padding_mask': jnp.zeros((B, LKV), bool).at[B // 2:, LKV - LKV // 4:].set(True), 'Wq': jax.random.normal(ks[2], (HID, HID), jnp.float32) * s, 'bq': jnp.zeros((HID,), jnp.float32), 'Wk': jax.random.normal(ks[3], (G * HD, HID), jnp.float32) * s, 'bk': jnp.zeros((G * HD,), jnp.float32), 'Wv': jax.random.normal(ks[4], (G * HD, HID), jnp.float32) * s, 'bv': jnp.zeros((G * HD,), jnp.float32), 'Wo': jax.random.normal(ks[5], (HID, HID), jnp.float32) * s, 'bo': jnp.zeros((HID,), jnp.float32)}
        return inp
    _L0_xattn_all = _L0_xattn_setup()
    _L0_xattn_in = {k: v for k, v in _L0_xattn_all.items() if k in ('Wq', 'bq', 'Wk', 'bk', 'Wv', 'bv', 'Wo', 'bo')}
    del _L0_xattn_all

    def _L0_ffn_setup():
        import jax, jax.numpy as jnp
        import numpy as np
        TOP_K = 2
        key = jax.random.key(seed)
        ks = jax.random.split(key, 7)
        B, S, H = (2, 256, 256)
        E, A, NS = (8, 64, 2048)
        x = jax.random.normal(ks[0], (B, S, H), jnp.float32)
        gate_w = jax.random.normal(ks[1], (E, H), jnp.float32) * 0.01
        W = jax.random.normal(ks[2], (H, H), jnp.float32) * 0.02
        atoms = jax.random.normal(ks[3], (A, NS), jnp.float32) * 0.02
        expert_atom_weights = jax.random.normal(ks[4], (E, A), jnp.float32) * 0.1
        importance = jax.random.normal(ks[5], (E, NS), jnp.float32) * 0.1
        mask_idx = jax.random.randint(ks[6], (NS,), 0, H * H, jnp.int32)
        return dict(x=x, gate_w=gate_w, W=W, atoms=atoms, expert_atom_weights=expert_atom_weights, importance=importance, mask_idx=mask_idx)
    _L0_ffn_all = _L0_ffn_setup()
    _L0_ffn_in = {k: v for k, v in _L0_ffn_all.items() if k in ('gate_w', 'W', 'atoms', 'expert_atom_weights', 'importance', 'mask_idx')}
    del _L0_ffn_all

    def _L1_attn_setup():
        import jax, jax.numpy as jnp
        import numpy as np
        B, S, D = (2, 256, 256)
        H, G = (32, 8)
        GS = H // G
        HD = D // H
        key = jax.random.key(seed)
        ks = jax.random.split(key, 5)
        x = jax.random.normal(ks[0], (B, S, D), dtype=jnp.float32)
        Wq = jax.random.normal(ks[1], (D, D), dtype=jnp.float32) * 0.02
        Wk = jax.random.normal(ks[2], (G * HD, D), dtype=jnp.float32) * 0.02
        Wv = jax.random.normal(ks[3], (G * HD, D), dtype=jnp.float32) * 0.02
        Wo = jax.random.normal(ks[4], (D, D), dtype=jnp.float32) * 0.02
        return {'x': x, 'Wq': Wq, 'Wk': Wk, 'Wv': Wv, 'Wo': Wo}
    _L1_attn_all = _L1_attn_setup()
    _L1_attn_in = {k: v for k, v in _L1_attn_all.items() if k in ('Wq', 'Wk', 'Wv', 'Wo')}
    del _L1_attn_all

    def _L1_xattn_setup():
        import jax, jax.numpy as jnp
        import numpy as np
        key = jax.random.key(seed)
        k1, k2, k3 = jax.random.split(key, 3)
        B, S, D, M = (8, 256, 256, 128)
        hidden_states = jax.random.normal(k1, (B, S, D), dtype=jnp.float32)
        memory_tokens = jax.random.normal(k2, (B, M, D), dtype=jnp.float32)
        memory_mask = jax.random.randint(k3, (B, M), 0, 2).astype(jnp.bool_)
        return {'hidden_states': hidden_states, 'memory_tokens': memory_tokens, 'memory_mask': memory_mask}
    _L1_xattn_all = _L1_xattn_setup()
    _L1_xattn_in = {k: v for k, v in _L1_xattn_all.items() if k in ()}
    del _L1_xattn_all

    def _L1_ffn_setup():
        import jax, jax.numpy as jnp
        import numpy as np
        BLOCK_SIZE = 32
        HIDDEN_SIZE = 256
        MLP_DIM = 2048
        NVFP4_LUT = jnp.array([0.0, 0.5, 1.0, 1.5, 2.0, 3.0, 4.0, 6.0, 0.0, -0.5, -1.0, -1.5, -2.0, -3.0, -4.0, -6.0], dtype=jnp.float32)

        def dequant_nvfp4(W_packed, scales, block=BLOCK_SIZE):
            N = W_packed.shape[0]
            low = W_packed & 15
            high = W_packed >> 4 & 15
            idx = jnp.stack([low, high], axis=-1).reshape(N, -1)
            vals = NVFP4_LUT[idx]
            K = vals.shape[1]
            vals = vals.reshape(N, K // block, block) * scales[:, :, None]
            return vals.reshape(N, K)
        key = jax.random.key(seed)
        ks = jax.random.split(key, 7)
        x = jax.random.normal(ks[0], (4, 32, HIDDEN_SIZE), dtype=jnp.float32)
        gate_W_packed = jax.random.randint(ks[1], (MLP_DIM, HIDDEN_SIZE // 2), 0, 32, dtype=jnp.int32)
        gate_scales = jax.random.uniform(ks[2], (MLP_DIM, HIDDEN_SIZE // BLOCK_SIZE), dtype=jnp.float32) * 0.1 + 0.001
        up_W_packed = jax.random.randint(ks[3], (MLP_DIM, HIDDEN_SIZE // 2), 0, 32, dtype=jnp.int32)
        up_scales = jax.random.uniform(ks[4], (MLP_DIM, HIDDEN_SIZE // BLOCK_SIZE), dtype=jnp.float32) * 0.1 + 0.001
        down_W_packed = jax.random.randint(ks[5], (HIDDEN_SIZE, MLP_DIM // 2), 0, 32, dtype=jnp.int32)
        down_scales = jax.random.uniform(ks[6], (HIDDEN_SIZE, MLP_DIM // BLOCK_SIZE), dtype=jnp.float32) * 0.1 + 0.001
        return {'x': x, 'gate_W_packed': gate_W_packed, 'gate_scales': gate_scales, 'up_W_packed': up_W_packed, 'up_scales': up_scales, 'down_W_packed': down_W_packed, 'down_scales': down_scales}
    _L1_ffn_all = _L1_ffn_setup()
    _L1_ffn_in = {k: v for k, v in _L1_ffn_all.items() if k in ('gate_W_packed', 'gate_scales', 'up_W_packed', 'up_scales', 'down_W_packed', 'down_scales')}
    del _L1_ffn_all

    def _L2_attn_setup():
        import jax, jax.numpy as jnp
        import numpy as np
        B, S, HID = (1, 256, 256)
        NH, NKV, HD = (16, 4, 128)
        WIN = 128
        THETA = 10000.0

        def _rotate_half(x):
            h = x.shape[-1] // 2
            return jnp.concatenate((-x[..., h:], x[..., :h]), axis=-1)

        def _rope_cos_sin(seq_len, dtype):
            inv_freq = 1.0 / THETA ** (jnp.arange(0, HD, 2, dtype=jnp.float32) / HD)
            t = jnp.arange(seq_len, dtype=jnp.float32)
            freqs = jnp.outer(t, inv_freq)
            emb = jnp.concatenate((freqs, freqs), axis=-1)
            return (jnp.cos(emb).astype(dtype)[None, None], jnp.sin(emb).astype(dtype)[None, None])
        key = jax.random.key(seed)
        ks = jax.random.split(key, 5)
        return {'hidden_states': jax.random.normal(ks[0], (B, S, HID), dtype=jnp.float32), 'w_q': jax.random.normal(ks[1], (HID, NH * HD), dtype=jnp.float32) * 0.02, 'w_k': jax.random.normal(ks[2], (HID, NKV * HD), dtype=jnp.float32) * 0.02, 'w_v': jax.random.normal(ks[3], (HID, NKV * HD), dtype=jnp.float32) * 0.02, 'w_o': jax.random.normal(ks[4], (NH * HD, HID), dtype=jnp.float32) * 0.02}
    _L2_attn_all = _L2_attn_setup()
    _L2_attn_in = {k: v for k, v in _L2_attn_all.items() if k in ('w_q', 'w_k', 'w_v', 'w_o')}
    del _L2_attn_all

    def _L2_xattn_setup():
        import jax, jax.numpy as jnp
        import numpy as np
        B, S, D = (8, 128, 256)
        H, HD = (16, 128)
        key = jax.random.key(seed)
        ks = jax.random.split(key, 6)
        fan_in = 1.0 / np.sqrt(D)
        return {'inputs_q': jax.random.normal(ks[0], (B, S, D), jnp.float32), 'inputs_kv': jax.random.normal(ks[1], (B, S, D), jnp.float32), 'Wq': jax.random.normal(ks[2], (D, H * HD), jnp.float32) * fan_in, 'Wk': jax.random.normal(ks[3], (D, H * HD), jnp.float32) * fan_in, 'Wv': jax.random.normal(ks[4], (D, H * HD), jnp.float32) * fan_in, 'Wo': jax.random.normal(ks[5], (H * HD, D), jnp.float32) * (1.0 / np.sqrt(H * HD))}
    _L2_xattn_all = _L2_xattn_setup()
    _L2_xattn_in = {k: v for k, v in _L2_xattn_all.items() if k in ('Wq', 'Wk', 'Wv', 'Wo')}
    del _L2_xattn_all

    def _L2_ffn_setup():
        import jax, jax.numpy as jnp
        import numpy as np
        from functools import partial
        E = 8
        K = 2
        H = 256
        F = 1024

        def _moe_forward(x, gate_w, gate_b, fc1_w, fc1_b, fc2_w, fc2_b, alpha):
            B_, S_, H_ = x.shape
            xf = x.reshape(-1, H_)
            logits = xf @ gate_w + gate_b
            top_val, top_idx = jax.lax.top_k(logits, K)
            gate_score = jax.nn.softmax(top_val, axis=-1)
            onehot = jax.nn.one_hot(top_idx, E, dtype=xf.dtype)
            comb = jnp.einsum('tk,tke->et', gate_score, onehot) * alpha[:, None]

            def body(acc, p):
                w1, b1, w2, b2, w = p
                h = jax.nn.gelu(xf @ w1 + b1, approximate=False)
                y = h @ w2 + b2
                return (acc + y * w[:, None], None)
            out0 = jnp.zeros_like(xf)
            out, _ = jax.lax.scan(body, out0, (fc1_w, fc1_b, fc2_w, fc2_b, comb))
            return out.reshape(B_, S_, H_)
        key = jax.random.key(seed)
        ks = jax.random.split(key, 8)
        s = 0.02
        return {'hidden_states': jax.random.normal(ks[0], (2, 256, H), jnp.float32), 'gate_w': jax.random.normal(ks[1], (H, E), jnp.float32) * s, 'gate_b': jax.random.normal(ks[2], (E,), jnp.float32) * s, 'fc1_w': jax.random.normal(ks[3], (E, H, F), jnp.float32) * s, 'fc1_b': jax.random.normal(ks[4], (E, F), jnp.float32) * s, 'fc2_w': jax.random.normal(ks[5], (E, F, H), jnp.float32) * s, 'fc2_b': jax.random.normal(ks[6], (E, H), jnp.float32) * s, 'alpha': jax.random.normal(ks[7], (E,), jnp.float32)}
    _L2_ffn_all = _L2_ffn_setup()
    _L2_ffn_in = {k: v for k, v in _L2_ffn_all.items() if k in ('gate_w', 'gate_b', 'fc1_w', 'fc1_b', 'fc2_w', 'fc2_b', 'alpha')}
    del _L2_ffn_all

    def _L3_attn_setup():
        import jax, jax.numpy as jnp
        import numpy as np
        from jax import lax

        def _causal_depthwise_conv(x, conv_w, conv_b):
            K = conv_w.shape[-1]
            xc = jnp.transpose(x, (0, 2, 1))
            xc = jnp.pad(xc, ((0, 0), (0, 0), (K - 1, 0)))
            D = xc.shape[1]
            y = lax.conv_general_dilated(xc, conv_w, window_strides=(1,), padding='VALID', dimension_numbers=('NCH', 'OIH', 'NCH'), feature_group_count=D)
            y = y + conv_b[None, :, None]
            return jnp.transpose(y, (0, 2, 1))
        key = jax.random.key(seed)
        ks = jax.random.split(key, 7)
        B, L, Dm, S, K = (4, 512, 256, 64, 4)
        s = 0.02
        x = jax.random.normal(ks[0], (B, L, Dm), dtype=jnp.float32)
        Wxproj = jax.random.normal(ks[1], (2 * S + 1, Dm), dtype=jnp.float32) * s
        Winproj = jax.random.normal(ks[2], (S, Dm), dtype=jnp.float32) * s
        Woutproj = jax.random.normal(ks[3], (Dm, S), dtype=jnp.float32) * s
        conv_w = jax.random.normal(ks[4], (Dm, 1, K), dtype=jnp.float32) * 0.5
        conv_b = jax.random.normal(ks[5], (Dm,), dtype=jnp.float32) * 0.02
        A_log = jnp.log(jnp.arange(1, S + 1, dtype=jnp.float32))
        D = jnp.ones((Dm,), dtype=jnp.float32)
        return {'x': x, 'Wxproj': Wxproj, 'Winproj': Winproj, 'Woutproj': Woutproj, 'conv_w': conv_w, 'conv_b': conv_b, 'A_log': A_log, 'D': D}
    _L3_attn_all = _L3_attn_setup()
    _L3_attn_in = {k: v for k, v in _L3_attn_all.items() if k in ('Wxproj', 'Winproj', 'Woutproj', 'conv_w', 'conv_b', 'A_log', 'D')}
    del _L3_attn_all

    def _L3_xattn_setup():
        import jax, jax.numpy as jnp
        import numpy as np
        N_HEAD = 8
        key = jax.random.key(seed)
        k1, k2, k3 = jax.random.split(key, 3)
        b, d, m = (4, 128, 256)
        c, n = (128, 256)
        q = jax.random.normal(k1, (b, d, m), dtype=jnp.float32)
        k = jax.random.normal(k2, (d // d * b, d, n), dtype=jnp.float32).reshape(b, d, n)
        v = jax.random.normal(k3, (b, c, n), dtype=jnp.float32)
        return {'q': q, 'k': k, 'v': v}
    _L3_xattn_all = _L3_xattn_setup()
    _L3_xattn_in = {k: v for k, v in _L3_xattn_all.items() if k in ()}
    del _L3_xattn_all

    def _L3_ffn_setup():
        import jax, jax.numpy as jnp
        import numpy as np
        TOP_K = 4

        def _silu_and_mul(gu):
            g, u = jnp.split(gu, 2, axis=-1)
            return jax.nn.silu(g) * u
        key = jax.random.key(seed)
        ks = jax.random.split(key, 7)
        H, E, I, Is = (256, 16, 176, 704)
        s = 0.02
        return {'hidden_states': jax.random.normal(ks[0], (4, 128, H), dtype=jnp.float32), 'gate_w': jax.random.normal(ks[1], (E, H), dtype=jnp.float32) * s, 'sgate_w': jax.random.normal(ks[2], (1, H), dtype=jnp.float32) * s, 'w13': jax.random.normal(ks[3], (E, 2 * I, H), dtype=jnp.float32) * s, 'w2': jax.random.normal(ks[4], (E, H, I), dtype=jnp.float32) * s, 'shared_gate_up_w': jax.random.normal(ks[5], (2 * Is, H), dtype=jnp.float32) * s, 'shared_down_w': jax.random.normal(ks[6], (H, Is), dtype=jnp.float32) * s}
    _L3_ffn_all = _L3_ffn_setup()
    _L3_ffn_in = {k: v for k, v in _L3_ffn_all.items() if k in ('gate_w', 'sgate_w', 'w13', 'w2', 'shared_gate_up_w', 'shared_down_w')}
    del _L3_ffn_all
    return {'x': x, 'ctx_2048': ctx_2048, 'mask_SxS2_bc0': mask_SxS2_bc0, 'mask_BxS2_bk0': mask_BxS2_bk0, 'L0_attn_W_Q': _L0_attn_in['W_Q'], 'L0_attn_W_K': _L0_attn_in['W_K'], 'L0_attn_W_V': _L0_attn_in['W_V'], 'L0_attn_W_O': _L0_attn_in['W_O'], 'L0_attn_b_Q': _L0_attn_in['b_Q'], 'L0_attn_b_K': _L0_attn_in['b_K'], 'L0_attn_b_V': _L0_attn_in['b_V'], 'L0_attn_b_O': _L0_attn_in['b_O'], 'L0_xattn_Wq': _L0_xattn_in['Wq'], 'L0_xattn_bq': _L0_xattn_in['bq'], 'L0_xattn_Wk': _L0_xattn_in['Wk'], 'L0_xattn_bk': _L0_xattn_in['bk'], 'L0_xattn_Wv': _L0_xattn_in['Wv'], 'L0_xattn_bv': _L0_xattn_in['bv'], 'L0_xattn_Wo': _L0_xattn_in['Wo'], 'L0_xattn_bo': _L0_xattn_in['bo'], 'L0_ffn_gate_w': _L0_ffn_in['gate_w'], 'L0_ffn_W': _L0_ffn_in['W'], 'L0_ffn_atoms': _L0_ffn_in['atoms'], 'L0_ffn_expert_atom_weights': _L0_ffn_in['expert_atom_weights'], 'L0_ffn_importance': _L0_ffn_in['importance'], 'L0_ffn_mask_idx': _L0_ffn_in['mask_idx'], 'L1_attn_Wq': _L1_attn_in['Wq'], 'L1_attn_Wk': _L1_attn_in['Wk'], 'L1_attn_Wv': _L1_attn_in['Wv'], 'L1_attn_Wo': _L1_attn_in['Wo'], 'L1_ffn_gate_W_packed': _L1_ffn_in['gate_W_packed'], 'L1_ffn_gate_scales': _L1_ffn_in['gate_scales'], 'L1_ffn_up_W_packed': _L1_ffn_in['up_W_packed'], 'L1_ffn_up_scales': _L1_ffn_in['up_scales'], 'L1_ffn_down_W_packed': _L1_ffn_in['down_W_packed'], 'L1_ffn_down_scales': _L1_ffn_in['down_scales'], 'L2_attn_w_q': _L2_attn_in['w_q'], 'L2_attn_w_k': _L2_attn_in['w_k'], 'L2_attn_w_v': _L2_attn_in['w_v'], 'L2_attn_w_o': _L2_attn_in['w_o'], 'L2_xattn_Wq': _L2_xattn_in['Wq'], 'L2_xattn_Wk': _L2_xattn_in['Wk'], 'L2_xattn_Wv': _L2_xattn_in['Wv'], 'L2_xattn_Wo': _L2_xattn_in['Wo'], 'L2_ffn_gate_w': _L2_ffn_in['gate_w'], 'L2_ffn_gate_b': _L2_ffn_in['gate_b'], 'L2_ffn_fc1_w': _L2_ffn_in['fc1_w'], 'L2_ffn_fc1_b': _L2_ffn_in['fc1_b'], 'L2_ffn_fc2_w': _L2_ffn_in['fc2_w'], 'L2_ffn_fc2_b': _L2_ffn_in['fc2_b'], 'L2_ffn_alpha': _L2_ffn_in['alpha'], 'L3_attn_Wxproj': _L3_attn_in['Wxproj'], 'L3_attn_Winproj': _L3_attn_in['Winproj'], 'L3_attn_Woutproj': _L3_attn_in['Woutproj'], 'L3_attn_conv_w': _L3_attn_in['conv_w'], 'L3_attn_conv_b': _L3_attn_in['conv_b'], 'L3_attn_A_log': _L3_attn_in['A_log'], 'L3_attn_D': _L3_attn_in['D'], 'L3_ffn_gate_w': _L3_ffn_in['gate_w'], 'L3_ffn_sgate_w': _L3_ffn_in['sgate_w'], 'L3_ffn_w13': _L3_ffn_in['w13'], 'L3_ffn_w2': _L3_ffn_in['w2'], 'L3_ffn_shared_gate_up_w': _L3_ffn_in['shared_gate_up_w'], 'L3_ffn_shared_down_w': _L3_ffn_in['shared_down_w']}

def reference(x, ctx_2048, mask_SxS2_bc0, mask_BxS2_bk0, L0_attn_W_Q, L0_attn_W_K, L0_attn_W_V, L0_attn_W_O, L0_attn_b_Q, L0_attn_b_K, L0_attn_b_V, L0_attn_b_O, L0_xattn_Wq, L0_xattn_bq, L0_xattn_Wk, L0_xattn_bk, L0_xattn_Wv, L0_xattn_bv, L0_xattn_Wo, L0_xattn_bo, L0_ffn_gate_w, L0_ffn_W, L0_ffn_atoms, L0_ffn_expert_atom_weights, L0_ffn_importance, L0_ffn_mask_idx, L1_attn_Wq, L1_attn_Wk, L1_attn_Wv, L1_attn_Wo, L1_ffn_gate_W_packed, L1_ffn_gate_scales, L1_ffn_up_W_packed, L1_ffn_up_scales, L1_ffn_down_W_packed, L1_ffn_down_scales, L2_attn_w_q, L2_attn_w_k, L2_attn_w_v, L2_attn_w_o, L2_xattn_Wq, L2_xattn_Wk, L2_xattn_Wv, L2_xattn_Wo, L2_ffn_gate_w, L2_ffn_gate_b, L2_ffn_fc1_w, L2_ffn_fc1_b, L2_ffn_fc2_w, L2_ffn_fc2_b, L2_ffn_alpha, L3_attn_Wxproj, L3_attn_Winproj, L3_attn_Woutproj, L3_attn_conv_w, L3_attn_conv_b, L3_attn_A_log, L3_attn_D, L3_ffn_gate_w, L3_ffn_sgate_w, L3_ffn_w13, L3_ffn_w2, L3_ffn_shared_gate_up_w, L3_ffn_shared_down_w):
    import jax
    import jax.numpy as jnp

    def _L0_attn_ref(x, W_Q, W_K, W_V, W_O, b_Q, b_K, b_V, b_O):
        import jax, jax.numpy as jnp
        import numpy as np
        BATCH, SEQ, D_MODEL, N_HEADS, D_HEAD = (2, 256, 256, 16, 128)
        ATTN_SCALE = np.sqrt(D_HEAD).astype(np.float32)
        IGNORE = jnp.float32(-100000.0)
        q = jnp.einsum('bpd,hde->bphe', x, W_Q) + b_Q
        k = jnp.einsum('bpd,hde->bphe', x, W_K) + b_K
        v = jnp.einsum('bpd,hde->bphe', x, W_V) + b_V
        scores = jnp.einsum('bqhe,bkhe->bhqk', q, k) / ATTN_SCALE
        S = x.shape[1]
        causal = jnp.tril(jnp.ones((S, S), bool))
        scores = jnp.where(causal, scores, IGNORE)
        attn = jax.nn.softmax(scores, axis=-1)
        z = jnp.einsum('bkhe,bhqk->bqhe', v, attn)
        out = jnp.einsum('bqhe,hed->bqd', z, W_O) + b_O
        return out

    def _L0_xattn_ref(X, encoder_output, causal_mask, padding_mask, Wq, bq, Wk, bk, Wv, bv, Wo, bo):
        import jax, jax.numpy as jnp
        import numpy as np
        B, LQ, LKV = (4, 128, 128)
        HID, H, G = (256, 32, 8)
        HD = HID // H
        HPG = H // G
        b = X.shape[0]
        q = X @ Wq.T + bq
        k = encoder_output @ Wk.T + bk
        v = encoder_output @ Wv.T + bv
        q = q.reshape(b, LQ, G, HPG, HD).transpose(0, 2, 3, 1, 4)
        k = k.reshape(b, LKV, G, HD).transpose(0, 2, 1, 3)
        v = v.reshape(b, LKV, G, HD).transpose(0, 2, 1, 3)
        scores = jnp.einsum('bgrqd,bgkd->bgrqk', q, k) / jnp.sqrt(jnp.float32(HD))
        scores = jnp.where(causal_mask[None, None, None, :, :], -jnp.inf, scores)
        scores = jnp.where(padding_mask[:, None, None, None, :], -jnp.inf, scores)
        w = jax.nn.softmax(scores, axis=-1)
        out = jnp.einsum('bgrqk,bgkd->bgrqd', w, v)
        out = out.reshape(b, H, LQ, HD).transpose(0, 2, 1, 3).reshape(b, LQ, HID)
        return out @ Wo.T + bo

    def _L0_ffn_ref(x, gate_w, W, atoms, expert_atom_weights, importance, mask_idx):
        import jax, jax.numpy as jnp
        import numpy as np
        TOP_K = 2
        B, S, H = x.shape
        xt = x.reshape(-1, H)
        logits = jnp.clip(xt @ gate_w.T, -50.0, 50.0)
        top_w, top_idx = jax.lax.top_k(logits, TOP_K)
        rw = jax.nn.softmax(top_w, axis=-1)
        deltas = jax.nn.softmax(expert_atom_weights, axis=-1) @ atoms
        weighted = deltas * jax.nn.sigmoid(importance)
        rows = mask_idx // H
        cols = mask_idx % H
        vals = jnp.einsum('tk,tks->ts', rw, weighted[top_idx])
        xg = xt[:, cols]
        contrib = jax.ops.segment_sum((xg * vals).T, rows, num_segments=H)
        out = xt @ W.T + contrib.T
        return out.reshape(B, S, H)

    def _L1_attn_ref(x, Wq, Wk, Wv, Wo):
        import jax, jax.numpy as jnp
        import numpy as np
        B, S, D = (2, 256, 256)
        H, G = (32, 8)
        GS = H // G
        HD = D // H
        b, s, _ = x.shape
        q = (x @ Wq.T).reshape(b, s, G, GS, HD)
        k = (x @ Wk.T).reshape(b, s, G, HD)
        v = (x @ Wv.T).reshape(b, s, G, HD)
        scores = jnp.einsum('bqgjd,bkgd->bgjqk', q, k) / np.sqrt(HD).astype(np.float32)
        qpos = jnp.arange(s)
        mask = qpos[:, None] < qpos[None, :]
        scores = jnp.where(mask, -jnp.inf, scores)
        w = jax.nn.softmax(scores, axis=-1)
        ctx = jnp.einsum('bgjqk,bkgd->bqgjd', w, v).reshape(b, s, D)
        return ctx @ Wo.T

    def _L1_xattn_ref(hidden_states, memory_tokens, memory_mask):
        import jax, jax.numpy as jnp
        import numpy as np
        B, S, D = hidden_states.shape
        scale = 1.0 / jnp.sqrt(jnp.asarray(D, hidden_states.dtype))
        scores = jnp.einsum('bsd,bmd->bsm', hidden_states, memory_tokens) * scale
        neg_inf = jnp.asarray(-1e+30, scores.dtype)
        scores = jnp.where(memory_mask[:, None, :], scores, neg_inf)
        attn = jax.nn.softmax(scores, axis=-1)
        readout = jnp.einsum('bsm,bmd->bsd', attn, memory_tokens)
        valid_b = jnp.any(memory_mask, axis=-1)
        out = jnp.where(valid_b[:, None, None], readout, jnp.zeros_like(readout))
        return out

    def _L1_ffn_ref(x, gate_W_packed, gate_scales, up_W_packed, up_scales, down_W_packed, down_scales):
        import jax, jax.numpy as jnp
        import numpy as np
        BLOCK_SIZE = 32
        HIDDEN_SIZE = 256
        MLP_DIM = 2048
        NVFP4_LUT = jnp.array([0.0, 0.5, 1.0, 1.5, 2.0, 3.0, 4.0, 6.0, 0.0, -0.5, -1.0, -1.5, -2.0, -3.0, -4.0, -6.0], dtype=jnp.float32)

        def dequant_nvfp4(W_packed, scales, block=BLOCK_SIZE):
            N = W_packed.shape[0]
            low = W_packed & 15
            high = W_packed >> 4 & 15
            idx = jnp.stack([low, high], axis=-1).reshape(N, -1)
            vals = NVFP4_LUT[idx]
            K = vals.shape[1]
            vals = vals.reshape(N, K // block, block) * scales[:, :, None]
            return vals.reshape(N, K)
        B, S, H = x.shape
        xt = x.reshape(B * S, H)
        Wg = dequant_nvfp4(gate_W_packed, gate_scales)
        Wu = dequant_nvfp4(up_W_packed, up_scales)
        Wd = dequant_nvfp4(down_W_packed, down_scales)
        gate = jnp.einsum('th,nh->tn', xt, Wg)
        up = jnp.einsum('th,nh->tn', xt, Wu)
        gelu = jnp.tanh(0.7978845608028654 * (gate + 0.044715 * gate ** 3)) * gate * 0.5 + gate * 0.5
        inter = gelu * up
        out = jnp.einsum('tn,hn->th', inter, Wd)
        return out.reshape(B, S, H)

    def _L2_attn_ref(hidden_states, w_q, w_k, w_v, w_o):
        import jax, jax.numpy as jnp
        import numpy as np
        B, S, HID = (1, 256, 256)
        NH, NKV, HD = (16, 4, 128)
        WIN = 128
        THETA = 10000.0

        def _rotate_half(x):
            h = x.shape[-1] // 2
            return jnp.concatenate((-x[..., h:], x[..., :h]), axis=-1)

        def _rope_cos_sin(seq_len, dtype):
            inv_freq = 1.0 / THETA ** (jnp.arange(0, HD, 2, dtype=jnp.float32) / HD)
            t = jnp.arange(seq_len, dtype=jnp.float32)
            freqs = jnp.outer(t, inv_freq)
            emb = jnp.concatenate((freqs, freqs), axis=-1)
            return (jnp.cos(emb).astype(dtype)[None, None], jnp.sin(emb).astype(dtype)[None, None])
        b, s, _ = hidden_states.shape
        dt = hidden_states.dtype
        q = (hidden_states @ w_q).reshape(b, s, NH, HD).transpose(0, 2, 1, 3)
        k = (hidden_states @ w_k).reshape(b, s, NKV, HD).transpose(0, 2, 1, 3)
        v = (hidden_states @ w_v).reshape(b, s, NKV, HD).transpose(0, 2, 1, 3)
        cos, sin = _rope_cos_sin(s, dt)
        q = q * cos + _rotate_half(q) * sin
        k = k * cos + _rotate_half(k) * sin
        rep = NH // NKV
        k = jnp.repeat(k, rep, axis=1)
        v = jnp.repeat(v, rep, axis=1)
        qpos = jnp.arange(s) + (s - s)
        kpos = jnp.arange(s)
        dist = qpos[:, None] - kpos[None, :]
        bad = (dist < 0) | (dist > WIN)
        bias = jnp.where(bad, jnp.finfo(dt).min, jnp.zeros((), dt))[None, None]
        scores = jnp.einsum('bhqd,bhkd->bhqk', q, k) / jnp.sqrt(jnp.asarray(HD, dt))
        probs = jax.nn.softmax(scores + bias, axis=-1)
        out = jnp.einsum('bhqk,bhkd->bhqd', probs, v)
        out = out.transpose(0, 2, 1, 3).reshape(b, s, NH * HD)
        return out @ w_o

    def _L2_xattn_ref(inputs_q, inputs_kv, Wq, Wk, Wv, Wo):
        import jax, jax.numpy as jnp
        import numpy as np
        B, S, D = (8, 128, 256)
        H, HD = (16, 128)
        b, sq, _ = inputs_q.shape
        skv = inputs_kv.shape[1]
        q = (inputs_q @ Wq).reshape(b, sq, H, HD) * (1.0 / np.sqrt(HD))
        k = (inputs_kv @ Wk).reshape(b, skv, H, HD)
        v = (inputs_kv @ Wv).reshape(b, skv, H, HD)
        scores = jnp.einsum('bqhd,bkhd->bhqk', q, k)
        attn = jax.nn.softmax(scores, axis=-1)
        ctx = jnp.einsum('bhqk,bkhd->bqhd', attn, v).reshape(b, sq, H * HD)
        return ctx @ Wo

    def _L2_ffn_ref(hidden_states, gate_w, gate_b, fc1_w, fc1_b, fc2_w, fc2_b, alpha):
        import jax, jax.numpy as jnp
        import numpy as np
        from functools import partial
        E = 8
        K = 2
        H = 256
        F = 1024

        def _moe_forward(x, gate_w, gate_b, fc1_w, fc1_b, fc2_w, fc2_b, alpha):
            B_, S_, H_ = x.shape
            xf = x.reshape(-1, H_)
            logits = xf @ gate_w + gate_b
            top_val, top_idx = jax.lax.top_k(logits, K)
            gate_score = jax.nn.softmax(top_val, axis=-1)
            onehot = jax.nn.one_hot(top_idx, E, dtype=xf.dtype)
            comb = jnp.einsum('tk,tke->et', gate_score, onehot) * alpha[:, None]

            def body(acc, p):
                w1, b1, w2, b2, w = p
                h = jax.nn.gelu(xf @ w1 + b1, approximate=False)
                y = h @ w2 + b2
                return (acc + y * w[:, None], None)
            out0 = jnp.zeros_like(xf)
            out, _ = jax.lax.scan(body, out0, (fc1_w, fc1_b, fc2_w, fc2_b, comb))
            return out.reshape(B_, S_, H_)
        return _moe_forward(hidden_states, gate_w, gate_b, fc1_w, fc1_b, fc2_w, fc2_b, alpha)

    def _L3_attn_ref(x, Wxproj, Winproj, Woutproj, conv_w, conv_b, A_log, D):
        import jax, jax.numpy as jnp
        import numpy as np
        from jax import lax

        def _causal_depthwise_conv(x, conv_w, conv_b):
            K = conv_w.shape[-1]
            xc = jnp.transpose(x, (0, 2, 1))
            xc = jnp.pad(xc, ((0, 0), (0, 0), (K - 1, 0)))
            D = xc.shape[1]
            y = lax.conv_general_dilated(xc, conv_w, window_strides=(1,), padding='VALID', dimension_numbers=('NCH', 'OIH', 'NCH'), feature_group_count=D)
            y = y + conv_b[None, :, None]
            return jnp.transpose(y, (0, 2, 1))
        S = A_log.shape[0]
        x_conv = _causal_depthwise_conv(x, conv_w, conv_b)
        ssm_params = jnp.einsum('bld,pd->blp', x, Wxproj)
        Bmat = ssm_params[..., :S]
        Cmat = ssm_params[..., S:2 * S]
        delta = jax.nn.softplus(ssm_params[..., 2 * S:])
        A = -jnp.exp(A_log)
        deltaA = jnp.exp(A[None, None, :] * delta)
        x_state = jnp.einsum('bld,sd->bls', x_conv, Winproj)
        Bu = delta * Bmat * x_state

        def combine(c1, c2):
            a1, b1 = c1
            a2, b2 = c2
            return (a1 * a2, a2 * b1 + b2)
        _, h = lax.associative_scan(combine, (deltaA, Bu), axis=1)
        h_mod = Cmat * h
        out = jnp.einsum('bls,ds->bld', h_mod, Woutproj) + D[None, None, :] * x_conv
        return out

    def _L3_xattn_ref(q, k, v):
        import jax, jax.numpy as jnp
        import numpy as np
        N_HEAD = 8
        b, d, m = q.shape
        c = v.shape[1]
        h = N_HEAD
        qh = q.reshape(b * h, d // h, m)
        kh = k.reshape(b * h, d // h, -1)
        vh = v.reshape(b * h, c // h, -1)
        scale = 1.0 / jnp.sqrt(jnp.asarray(d // h, dtype=q.dtype))
        qk = jnp.einsum('bdm,bdn->bmn', qh, kh) * scale
        sm = jax.nn.softmax(qk, axis=-1)
        ret = jnp.einsum('bmn,bcn->bcm', sm, vh)
        return ret.reshape(b, c, m)

    def _L3_ffn_ref(hidden_states, gate_w, sgate_w, w13, w2, shared_gate_up_w, shared_down_w):
        import jax, jax.numpy as jnp
        import numpy as np
        TOP_K = 4

        def _silu_and_mul(gu):
            g, u = jnp.split(gu, 2, axis=-1)
            return jax.nn.silu(g) * u
        B, S, H = hidden_states.shape
        x = hidden_states.reshape(-1, H)
        E = gate_w.shape[0]
        shared = _silu_and_mul(x @ shared_gate_up_w.T) @ shared_down_w.T
        shared = shared * jax.nn.sigmoid(x @ sgate_w.T)
        router_logits = x @ gate_w.T
        routing_weights = jax.nn.softmax(router_logits.astype(jnp.float32), axis=-1)
        topk_w, topk_ids = jax.lax.top_k(routing_weights, TOP_K)

        def body(acc, ew):
            w13_e, w2_e, e = ew
            coef = jnp.sum(jnp.where(topk_ids == e, topk_w, 0.0), axis=-1)
            h = _silu_and_mul(x @ w13_e.T)
            acc = acc + (h @ w2_e.T).astype(jnp.float32) * coef[:, None]
            return (acc, None)
        init = jnp.zeros((x.shape[0], H), dtype=jnp.float32)
        sparse_out, _ = jax.lax.scan(body, init, (w13, w2, jnp.arange(E)))
        out = shared + sparse_out.astype(x.dtype)
        return out.reshape(B, S, H)
    x = x + _L0_attn_ref(_layernorm(x, axis=-1), L0_attn_W_Q, L0_attn_W_K, L0_attn_W_V, L0_attn_W_O, L0_attn_b_Q, L0_attn_b_K, L0_attn_b_V, L0_attn_b_O)
    x = x + _L0_xattn_ref(_layernorm(x, axis=-1), ctx_2048, mask_SxS2_bc0, mask_BxS2_bk0, L0_xattn_Wq, L0_xattn_bq, L0_xattn_Wk, L0_xattn_bk, L0_xattn_Wv, L0_xattn_bv, L0_xattn_Wo, L0_xattn_bo)
    x = x + _L0_ffn_ref(_layernorm(x, axis=-1), L0_ffn_gate_w, L0_ffn_W, L0_ffn_atoms, L0_ffn_expert_atom_weights, L0_ffn_importance, L0_ffn_mask_idx)
    x = x + _L1_attn_ref(_layernorm(x, axis=-1), L1_attn_Wq, L1_attn_Wk, L1_attn_Wv, L1_attn_Wo)
    x = x + _L1_xattn_ref(_layernorm(x, axis=-1), ctx_2048, mask_BxS2_bk0)
    x = x + _L1_ffn_ref(_layernorm(x, axis=-1), L1_ffn_gate_W_packed, L1_ffn_gate_scales, L1_ffn_up_W_packed, L1_ffn_up_scales, L1_ffn_down_W_packed, L1_ffn_down_scales)
    x = x + _L2_attn_ref(_layernorm(x, axis=-1), L2_attn_w_q, L2_attn_w_k, L2_attn_w_v, L2_attn_w_o)
    x = x + _L2_xattn_ref(_layernorm(x, axis=-1), ctx_2048, L2_xattn_Wq, L2_xattn_Wk, L2_xattn_Wv, L2_xattn_Wo)
    x = x + _L2_ffn_ref(_layernorm(x, axis=-1), L2_ffn_gate_w, L2_ffn_gate_b, L2_ffn_fc1_w, L2_ffn_fc1_b, L2_ffn_fc2_w, L2_ffn_fc2_b, L2_ffn_alpha)
    x = x + _L3_attn_ref(_layernorm(x, axis=-1), L3_attn_Wxproj, L3_attn_Winproj, L3_attn_Woutproj, L3_attn_conv_w, L3_attn_conv_b, L3_attn_A_log, L3_attn_D)
    x = x + _L3_xattn_ref(_layernorm(x, axis=-1), ctx_2048, ctx_2048)
    x = x + _L3_ffn_ref(_layernorm(x, axis=-1), L3_ffn_gate_w, L3_ffn_sgate_w, L3_ffn_w13, L3_ffn_w2, L3_ffn_shared_gate_up_w, L3_ffn_shared_down_w)
    return x

_drawn_inputs = setup_inputs


def setup_inputs(seed=0):
    import zlib

    import numpy as np

    out = dict(_drawn_inputs(seed))
    spreads = {'L0_attn_b_Q': (0.0, 0.1),
     'L0_attn_b_K': (0.0, 0.8),
     'L0_attn_b_V': (0.0, 0.1),
     'L0_attn_b_O': (0.0, 0.1),
     'L0_xattn_bq': (0.0, 0.8),
     'L0_xattn_bk': (0.0, 0.8),
     'L0_xattn_bv': (0.0, 0.1),
     'L0_xattn_bo': (0.0, 0.1),
     'L3_attn_D': (1.0, 0.6)}
    factors = {'L0_xattn_Wq': 8.0,
     'L0_xattn_Wk': 8.0,
     'L0_ffn_gate_w': 8.0,
     'L0_ffn_atoms': 8.0,
     'L0_ffn_expert_atom_weights': 8.0,
     'L0_ffn_importance': 8.0,
     'L1_attn_Wq': 8.0,
     'L1_attn_Wk': 8.0,
     'L2_attn_w_q': 8.0,
     'L2_attn_w_k': 8.0,
     'L2_attn_w_v': 6.899,
     'L2_attn_w_o': 6.739,
     'L2_xattn_Wq': 3.959,
     'L2_xattn_Wk': 3.945,
     'L2_ffn_gate_w': 8.0,
     'L2_ffn_gate_b': 8.0,
     'L2_ffn_fc1_w': 8.0,
     'L2_ffn_fc1_b': 8.0,
     'L2_ffn_fc2_w': 8.0,
     'L2_ffn_fc2_b': 8.0,
     'L2_ffn_alpha': 8.0,
     'L3_attn_Wxproj': 8.0,
     'L3_attn_Winproj': 8.0,
     'L3_attn_Woutproj': 8.0,
     'L3_attn_conv_b': 8.0,
     'L3_attn_A_log': 8.0,
     'L3_ffn_gate_w': 8.0,
     'L3_ffn_sgate_w': 8.0,
     'L3_ffn_w13': 8.0,
     'L3_ffn_w2': 8.0,
     'L3_ffn_shared_gate_up_w': 8.0,
     'L3_ffn_shared_down_w': 8.0}
    for name, (base, spread) in spreads.items():
        noise = np.random.default_rng([zlib.crc32(name.encode()), seed]).standard_normal(out[name].shape)
        drawn = base * np.exp(spread * noise) if base else spread * noise
        out[name] = jnp.asarray(drawn.astype(out[name].dtype))
    for name, factor in factors.items():
        out[name] = (out[name] * factor).astype(out[name].dtype)
    return out
```

```python
from contextlib import ExitStack, contextmanager

import numpy as np

import concourse.bass as bass
from concourse import mybir

F32 = mybir.dt.float32
BF16 = mybir.dt.bfloat16
I32 = mybir.dt.int32
U8 = mybir.dt.uint8
ALU = mybir.AluOpType
ACT = mybir.ActivationFunctionType
AX = mybir.AxisListType.X

P = 128
B = 8
DM = 256
DC = DM // P
EPS = 1e-5
NEG = -1e30
BIG = 3e38


class Tally:

    def __init__(self, sem, credit):
        self.sem, self.credit, self.base = sem, credit, 0

    def at(self, steps):
        return steps + (self.credit + self.base)


class Own:

    def __init__(self, eng, sem):
        self.eng, self.sem, self.start, self.k = eng, sem, 0, 0

    def up(self):
        self.k += 1
        return 1

    def now(self):
        return self.start + self.k

    @contextmanager
    def loop(self, count, per):
        base = self.start + self.k
        with self.eng.Fori(0, count) as i:
            self.start, self.k = (i * per + base if per else base), 0
            yield i
            assert self.k == per, (self.eng, self.k, per)
        self.start, self.k = base + count * per, 0


class Attention:

    def __init__(self, w, nw, wq, wk, wv, wo, scale, bq=None, bk=None, bv=None, bo=None, cos=None, sin=None,
                 causal=False, cross=False, gqa=False, rope=False):
        self.w, self.nw = w, nw
        self.wq, self.wk, self.wv, self.wo = wq, wk, wv, wo
        self.bq, self.bk, self.bv, self.bo = bq, bk, bv, bo
        self.cos, self.sin, self.scale = cos, sin, scale
        self.causal, self.cross, self.gqa, self.rope = causal, cross, gqa, rope


class FeedForward:

    def __init__(self, E, nf, M, gated, func, weighted, up, down, arrived, load=None, bias=None):
        self.E, self.nf, self.M, self.gated, self.func, self.weighted = E, nf, M, gated, func, weighted
        self.up, self.down, self.arrived, self.load, self.bias = up, down, arrived, load, bias


def build(nc, D, out, stages):
    ctx = ExitStack()
    with ctx:
        def sb(name, shape, dt=F32):
            return ctx.enter_context(nc.sbuf_tensor(name, shape, dt))

        def sem(name):
            return ctx.enter_context(nc.semaphore(name))

        x = sb("x", [P, B, DM])
        ctxn = sb("ctxn", [P, B, DM])
        ctxT = sb("ctxT", [P, DC, B * P])
        xnT = sb("xnT", [P, DC, B * P])
        arena_a = sb("arena_a", [P, 16384])
        arena_b = sb("arena_b", [P, 16384])
        work = sb("work", [P, 9216])
        xn2 = sb("xn2", [P, 2, DM])
        ident = sb("ident", [P, P])
        ident16 = sb("ident16", [P, P], BF16)
        causal16 = sb("causal16", [P, P], BF16)
        bn = sb("bn", [P, B, 6])
        stat = sb("stat", [P, 6, B])
        small = sb("small", [P, 1024])

        pair_mask = sb("pair_mask", [P, P], U8)
        row_mask = sb("row_mask", [P, B, P], U8)

        psum = [ctx.enter_context(nc.psum_tensor(f"bank{i}", [P, 512], F32)) for i in range(8)]

        tallies = []

        def tally(name, credit=1):
            tallies.append(Tally(sem(name), credit))
            return tallies[-1]

        var_ready = tally("var_ready")
        std_ready = tally("std_ready")
        xn_ready = tally("xn_ready")
        xnt_ready = tally("xnt_ready", 2)
        xnt_done = tally("xnt_done", 2)
        slice_ready = tally("slice_ready")
        proj_ready = tally("proj_ready")
        proj_done = tally("proj_done", 2)
        scores_ready = tally("scores_ready")
        max_ready = tally("max_ready")
        exp_done = tally("exp_done", 2)
        recip_ready = tally("recip_ready")
        probs_ready = tally("probs_ready")
        probsT_ready = tally("probsT_ready")
        probsT_done = tally("probsT_done")
        mix_ready = tally("mix_ready")
        mix_done = tally("mix_done")
        out_ready = tally("out_ready")
        out_done = tally("out_done")
        kpad_ready = tally("kpad_ready")
        aux_ready = tally("aux_ready")
        aux_done = tally("aux_done")
        aux2_ready = tally("aux2_ready")
        aux3_ready = tally("aux3_ready")
        aux4_ready = tally("aux4_ready")
        aux5_ready = tally("aux5_ready")
        aux6_ready = tally("aux6_ready")
        up_ready = tally("up_ready")
        gate_ready = tally("gate_ready")
        hidden_done = tally("hidden_done", 2)
        acc_ready = tally("acc_ready")
        acc_done = tally("acc_done", 2)
        codes_ready = tally("codes_ready")
        scale_ready = tally("scale_ready")
        weights_ready = tally("weights_ready")
        stage_done = tally("stage_done")
        loaded = {s: sem(f"loaded_{s}") for s in
                  ("x", "const", "ctx", "w0", "w1", "w2", "w3", "w5a", "w5b", "w6", "w7", "w8", "w8a", "w8b", "w9", "w11", "w11a", "w11b")}
        stored = sem("stored")
        passed = sem("passed")
        masks16_ready = sem("masks16_ready")
        credits_given = sem("credits_given")
        dve_own, act_own, pool_own = sem("dve_own"), sem("act_own"), sem("pool_own")
        pe, act, dve, pool, sp = nc.tensor, nc.scalar, nc.vector, nc.gpsimd, nc.sync
        V, A, G = Own(dve, dve_own), Own(act, act_own), Own(pool, pool_own)

        def stand_alone(eng):
            eng.sem_inc(passed, 1)

        def rows_(v, off, k, n):
            return v[:, off:off + k * n].rearrange("p (k n) -> p k n", k=k)

        def dve_norm(s, natural=None):
            with V.loop(B, 1) as b:
                dve.bn_stats(bn[:, b, :], x[:, b, :]).then_inc(dve_own, V.up())
            dve.wait_ge(dve_own, V.now())
            mean, var, rstd, diff, sq, std = (stat[:, k, :] for k in range(6))
            dve.tensor_tensor(diff, bn[:, :, 1], bn[:, :, 4], ALU.subtract).then_inc(dve_own, V.up())
            dve.tensor_tensor(mean, bn[:, :, 1], bn[:, :, 4], ALU.add).then_inc(dve_own, V.up())
            dve.tensor_tensor(var, bn[:, :, 2], bn[:, :, 5], ALU.add).then_inc(dve_own, V.up())
            dve.wait_ge(dve_own, V.now())
            dve.tensor_tensor(sq, diff, diff, ALU.mult).then_inc(dve_own, V.up())
            dve.tensor_scalar(mean, mean, 0.5, None, ALU.mult).then_inc(dve_own, V.up())
            dve.tensor_scalar(var, var, 1.0 / DM, EPS, ALU.mult, ALU.add).then_inc(dve_own, V.up())
            dve.wait_ge(dve_own, V.now())
            dve.scalar_tensor_tensor(var, sq, 0.25, var, ALU.mult, ALU.add).then_inc(var_ready.sem, 1)
            dve.wait_ge(std_ready.sem, std_ready.at(1))
            dve.reciprocal(rstd, std).then_inc(dve_own, V.up())
            dve.wait_ge(dve_own, V.now())
            with V.loop(B // 2, 0) as i:
                for par in range(2):
                    b = i * 2 + par
                    if natural is None:
                        dve.wait_ge(xnt_ready.sem, xnt_ready.at(b - 1))
                        dst = xn2[:, par, :]
                    else:
                        dst = natural[:, b, :]
                    dve.tensor_scalar(dst, x[:, b, :], stat[:, 0, bass.ds(b, 1)], stat[:, 2, bass.ds(b, 1)],
                                      ALU.subtract, ALU.mult).then_inc(xn_ready.sem, 1)

        def act_norm(s, natural=None):
            act.wait_ge(var_ready.sem, var_ready.at(1))
            act.activation(stat[:, 5, :], stat[:, 1, :], ACT.Sqrt).then_inc(std_ready.sem, 1)
            if natural is None:
                with A.loop(B // 2, 0) as i:
                    for par in range(2):
                        b = i * 2 + par
                        act.wait_ge(xnt_ready.sem, xnt_ready.at(b + 1))
                        stand_alone(act)
                        act.activation(xnT[:, :, bass.ds(b * P, P)],
                                       psum[3 + par][:, 0:DM].rearrange("p (c t) -> p c t", c=DC),
                                       ACT.Copy).then_inc(xnt_done.sem, 1)

        def pe_norm(s, step=1):
            with pe.Fori(0, B // 2) as i:
                for par in range(2):
                    b = i * 2 + par
                    pe.wait_ge(xn_ready.sem, xn_ready.at(b + 1))
                    pe.wait_ge(xnt_done.sem, xnt_done.at(b - 1))
                    for c in range(DC):
                        rows = xn2[:, par, c::2] if step == 2 else xn2[:, par, c * P:(c + 1) * P]
                        last = pe.transpose(psum[3 + par][:, c * P:(c + 1) * P], rows, ident[:, :])
                    last.then_inc(xnt_ready.sem, 1)

        SC, TP, ZP, OP, PJ = psum[0:2], psum[2], psum[3], psum[4], psum[5:7]
        QG = work[:, 0:512].rearrange("p (j t) -> p j t", j=4)
        KG = work[:, 512:1024].rearrange("p (j t) -> p j t", j=4)
        VG = work[:, 1024:2048].rearrange("p (r n) -> p r n", r=2)
        PR = work[:, 2048:3072].rearrange("p (r n) -> p r n", r=2)
        PT = work[:, 3072:3584].rearrange("p (j t) -> p j t", j=4)
        ZS = work[:, 3584:4096]
        xb = work[:, 4096:4352].rearrange("p (c t) -> p c t", c=DC)
        cb = work[:, 4352:4608].rearrange("p (c t) -> p c t", c=DC)
        RT = work[:, 4608:5120]
        KP = work[:, 5120:6144].rearrange("p (r n) -> p r n", r=2)
        nmax = small[:, 0:8].rearrange("p (r j) -> p r j", r=2)
        smax = small[:, 8:16].rearrange("p (r j) -> p r j", r=2)
        sums = small[:, 16:24].rearrange("p (r j) -> p r j", r=2)
        rsum = small[:, 24:32].rearrange("p (r j) -> p r j", r=2)

        def dve_max(u, r, nh, scale):
            dve.wait_ge(scores_ready.sem, scores_ready.at(u + 1))
            dve.tensor_reduce(nmax[:, r, 0:nh], SC[r][:, :].rearrange("p (j t) -> p j t", j=nh), AX, ALU.max,
                              negate=True).then_inc(dve_own, V.up())
            dve.wait_ge(dve_own, V.now())
            dve.tensor_scalar(smax[:, r, 0:nh], nmax[:, r, 0:nh], scale, None, ALU.mult).then_inc(max_ready.sem, 1)

        def act_exp(u, r, nh, scale):
            act.wait_ge(max_ready.sem, max_ready.at(u + 1))
            w = 512 // nh
            for j in range(nh):
                cols = slice(j * w, (j + 1) * w)
                last = act.activation(PR[:, r, cols], SC[r][:, cols], ACT.Exp, bias=smax[:, r, j:j + 1],
                                      scale=scale, accum_out=sums[:, r, j:j + 1])
            last.then_inc(exp_done.sem, 1)

        def dve_recip(u, r, nh):
            dve.wait_ge(exp_done.sem, exp_done.at(u + 1))
            dve.reciprocal(rsum[:, r, 0:nh], sums[:, r, 0:nh]).then_inc(recip_ready.sem, 1)

        def pool_normalise(u, r, nh):
            pool.wait_ge(recip_ready.sem, recip_ready.at(u + 1))
            w = 512 // nh
            probs = PR[:, r, :].rearrange("p (j t) -> p j t", j=nh)
            pool.tensor_tensor(probs, probs, rsum[:, r, 0:nh].unsqueeze(2).to_broadcast([P, nh, w]),
                               ALU.mult).then_inc(probs_ready.sem, 1)

        def pe_probsT(u, r):
            pe.wait_ge(probs_ready.sem, probs_ready.at(u + 1))
            pe.wait_ge(probsT_done.sem, probsT_done.at(u))
            for j in range(4):
                last = pe.transpose(TP[:, j * P:(j + 1) * P], PR[:, r, j * P:(j + 1) * P], ident[:, :])
            last.then_inc(probsT_ready.sem, 1)

        def dve_probsT(u):
            dve.wait_ge(probsT_ready.sem, probsT_ready.at(u + 1))
            dve.tensor_copy(work[:, 3072:3584], TP[:, :]).then_inc(probsT_done.sem, 1)

        def attn128_unit(b, g):
            return b * 4 + g

        def pe_attn128(s, c):
            def tail(b, g):
                u = attn128_unit(b, g)
                pe_probsT(u, g % 2)
                pe.wait_ge(proj_done.sem, proj_done.at(3 * u + 3))
                pe.wait_ge(probsT_done.sem, probsT_done.at(u + 1))
                pe.wait_ge(mix_done.sem, mix_done.at(u))
                for j in range(4):
                    vals = VG[:, g % 2, 0:P] if c.gqa else VG[:, g % 2, j * P:(j + 1) * P]
                    last = pe.matmul(ZP[:, j * P:(j + 1) * P], vals, PT[:, j, :], start=True, stop=True)
                last.then_inc(mix_ready.sem, 1)
                pe.wait_ge(mix_done.sem, mix_done.at(u + 1))
                pe.wait_ge(out_done.sem, out_done.at(u))
                for j in range(4):
                    last = pe.matmul(OP[:, 0:DM], ZS[:, j * P:(j + 1) * P], c.wo[:, 4 * g + j, :],
                                     start=(j == 0), stop=(j == 3))
                last.then_inc(out_ready.sem, 1)

            pe.wait_ge(loaded[c.w], 16 * c.nw)
            with pe.Fori(0, B) as b:
                pe.wait_ge(slice_ready.sem, slice_ready.at(b + 1))
                src = cb if c.cross else xb
                for g in range(4):
                    u = attn128_unit(b, g)
                    pe.wait_ge(proj_done.sem, proj_done.at(3 * u - 1))
                    for j in range(4):
                        for k in range(DC):
                            last = pe.matmul(PJ[(3 * g) % 2][:, j * P:(j + 1) * P],
                                             c.wq[:, k, (4 * g + j) * P:(4 * g + j + 1) * P], xb[:, k, :],
                                             start=(k == 0), stop=(k == DC - 1))
                    last.then_inc(proj_ready.sem, 1)
                    pe.wait_ge(proj_done.sem, proj_done.at(3 * u))
                    for j in range(1 if c.gqa else 4):
                        h = g if c.gqa else 4 * g + j
                        for k in range(DC):
                            last = pe.matmul(PJ[(3 * g + 1) % 2][:, j * P:(j + 1) * P],
                                             c.wk[:, k, h * P:(h + 1) * P], src[:, k, :],
                                             start=(k == 0), stop=(k == DC - 1))
                    last.then_inc(proj_ready.sem, 1)
                    pe.wait_ge(proj_done.sem, proj_done.at(3 * u + 1))
                    nv = P if c.gqa else 4 * P
                    for k in range(DC):
                        last = pe.matmul(PJ[(3 * g + 2) % 2][:, 0:nv], src[:, k, :],
                                         c.wv[:, k, g * nv:(g + 1) * nv], start=(k == 0), stop=(k == DC - 1))
                    last.then_inc(proj_ready.sem, 1)
                    pe.wait_ge(proj_done.sem, proj_done.at(3 * u + 2))
                    pe.wait_ge(exp_done.sem, exp_done.at(u - 1))
                    for j in range(4):
                        keys = KG[:, 0, :] if c.gqa else KG[:, j, :]
                        last = pe.matmul(SC[g % 2][:, j * P:(j + 1) * P], QG[:, j, :], keys,
                                         start=True, stop=not c.causal)
                        if c.causal:
                            last = pe.matmul(SC[g % 2][:, j * P:(j + 1) * P], ident16[:, :], causal16[:, :],
                                             start=False, stop=True)
                    last.then_inc(scores_ready.sem, 1)
                    if g:
                        tail(b, g - 1)
                tail(b, 3)

        def dve_attn128(s, c):
            if c.bo is not None:
                dve.wait_ge(xn_ready.sem, xn_ready.at(B))
                dve.tensor_tensor(x[:, :, :], x[:, :, :], c.bo.unsqueeze(1).to_broadcast([P, B, DM]),
                                  ALU.add).then_inc(dve_own, V.up())
                dve.wait_ge(dve_own, V.now())

            def evac_qk(b, g, u, n, dst, bias, nj):
                dve.wait_ge(proj_ready.sem, proj_ready.at(3 * u + n + 1))
                bank = PJ[(3 * g + n) % 2][:, 0:nj * P].rearrange("p (j t) -> p j t", j=nj)
                if c.rope:
                    dve.wait_ge(aux_ready.sem, aux_ready.at(2 * u + n + 1))
                    rot = RT.rearrange("p (j t) -> p j t", j=4)[:, 0:nj, :]
                    cos, sin = (t.unsqueeze(1).to_broadcast([P, nj, P]) for t in (c.cos, c.sin))
                    dve.tensor_tensor(rot, rot, sin, ALU.mult).then_inc(dve_own, V.up())
                    dve.tensor_tensor(dst[:, 0:nj, :], bank, cos, ALU.mult).then_inc(dve_own, V.up())
                    dve.wait_ge(dve_own, V.now())
                    dve.tensor_tensor(dst[:, 0:nj, :], dst[:, 0:nj, :], rot, ALU.add).then_inc(proj_done.sem, 1)
                elif bias is None:
                    dve.tensor_copy(dst[:, 0:nj, :], bank).then_inc(proj_done.sem, 1)
                else:
                    dve.tensor_tensor(dst[:, 0:nj, :], bank,
                                      bias[:, 4 * g:4 * g + 4].unsqueeze(2).to_broadcast([P, 4, P]),
                                      ALU.add).then_inc(proj_done.sem, 1)

            def tail(b, g):
                u = attn128_unit(b, g)
                dve_probsT(u)

            def add_out(b, g):
                dve.wait_ge(out_ready.sem, out_ready.at(attn128_unit(b, g) + 1))
                dve.tensor_tensor(x[:, b, :], x[:, b, :], OP[:, 0:DM], ALU.add).then_inc(out_done.sem, 1)

            with V.loop(B, 4 + (16 if c.rope else 0)) as b:
                for g in range(4):
                    u = attn128_unit(b, g)
                    evac_qk(b, g, u, 0, QG, c.bq, 4)
                    evac_qk(b, g, u, 1, KG, c.bk, 1 if c.gqa else 4)
                    dve.wait_ge(proj_ready.sem, proj_ready.at(3 * u + 3))
                    nv = P if c.gqa else 4 * P
                    bank = PJ[(3 * g + 2) % 2][:, 0:nv]
                    if c.bv is None:
                        dve.tensor_copy(VG[:, g % 2, 0:nv], bank).then_inc(proj_done.sem, 1)
                    else:
                        dve.tensor_tensor(VG[:, g % 2, :], bank, c.bv[:, g * nv:(g + 1) * nv],
                                          ALU.add).then_inc(proj_done.sem, 1)
                    dve_max(u, g % 2, 4, c.scale)
                    if g:
                        tail(b, g - 1)
                    dve_recip(u, g % 2, 4)
                    if g:
                        add_out(b, g - 1)
                tail(b, 3)
                add_out(b, 3)

        def act_attn128(s, c):
            def mix(b, g):
                act.wait_ge(mix_ready.sem, mix_ready.at(attn128_unit(b, g) + 1))
                act.activation(ZS, ZP[:, :], ACT.Copy).then_inc(mix_done.sem, 1)

            with A.loop(B, 0) as b:
                for g in range(4):
                    u = attn128_unit(b, g)
                    if c.rope:
                        for n, nj in ((0, 4), (1, 1)):
                            act.wait_ge(proj_ready.sem, proj_ready.at(3 * u + n + 1))
                            act.wait_ge(proj_done.sem, proj_done.at(3 * u + n))
                            bank = PJ[(3 * g + n) % 2]
                            act.activation(RT[0:64, 0:nj * P], bank[64:128, 0:nj * P], ACT.Copy)
                            act.activation(RT[64:128, 0:nj * P], bank[0:64, 0:nj * P],
                                           ACT.Copy).then_inc(aux_ready.sem, 1)
                    act_exp(u, g % 2, 4, c.scale)
                    if g:
                        mix(b, g - 1)
                mix(b, 3)

        def pool_attn128(s, c):
            pool.wait_ge(xnt_done.sem, xnt_done.at(B))
            with G.loop(B, 1 if c.cross else 0) as b:
                pool.wait_ge(proj_ready.sem, proj_ready.at(12 * b))
                if c.cross:
                    pool.tensor_copy(cb, ctxT[:, :, bass.ds(b * P, P)]).then_inc(pool_own, G.up())
                    pool.wait_ge(pool_own, G.now())
                pool.tensor_copy(xb, xnT[:, :, bass.ds(b * P, P)]).then_inc(slice_ready.sem, 1)
                for g in range(4):
                    pool_normalise(attn128_unit(b, g), g % 2, 4)

        QB = work[:, 6144:6400].rearrange("p (c t) -> p c t", c=2)
        KB = work[:, 6400:6656].rearrange("p (c t) -> p c t", c=2)
        VB = work[:, 6656:6720]
        ZB = work[:, 6720:6976]
        ZT = work[:, 6976:7232].rearrange("p (c t) -> p c t", c=2)
        heads8 = sb("heads8", [P, 16])
        mask16 = sb("mask16", [P, B, P], BF16)

        def pe_attn8(s, c):
            def tail(b, g):
                u = b * 8 + g
                pe_probsT(u, g % 2)
                pe.wait_ge(probsT_done.sem, probsT_done.at(u + 1))
                if g == 0:
                    pe.wait_ge(mix_done.sem, mix_done.at(b))
                for j in range(4):
                    h = 4 * g + j
                    last = pe.matmul(ZP[:, h * 8:h * 8 + 8], PT[:, j, :], VB[:, g * 8:g * 8 + 8],
                                     start=True, stop=True)
                last.then_inc(mix_ready.sem, 1)

            pe.wait_ge(loaded[c.w], 16 * c.nw)
            with pe.Fori(0, B) as b:
                pe.wait_ge(slice_ready.sem, slice_ready.at(b + 1))
                pe.wait_ge(proj_done.sem, proj_done.at(3 * b - 1))
                src = cb if c.cross else xb
                for n, (w, v) in enumerate(((c.wq, xb), (c.wk, src))):
                    for m in range(2):
                        for k in range(DC):
                            last = pe.matmul(PJ[0][:, (2 * n + m) * P:(2 * n + m + 1) * P],
                                             w[:, k, m * P:(m + 1) * P], v[:, k, :],
                                             start=(k == 0), stop=(k == DC - 1))
                last.then_inc(proj_ready.sem, 1)
                pe.wait_ge(proj_done.sem, proj_done.at(3 * b))
                pe.wait_ge(out_done.sem, out_done.at(b))
                for k in range(DC):
                    last = pe.matmul(PJ[1][:, 0:64], src[:, k, :], c.wv[:, k, :], start=(k == 0), stop=(k == DC - 1))
                last.then_inc(proj_ready.sem, 1)
                pe.wait_ge(proj_done.sem, proj_done.at(3 * b + 3))
                for g in range(8):
                    u = b * 8 + g
                    pe.wait_ge(kpad_ready.sem, kpad_ready.at(u + 1))
                    pe.wait_ge(exp_done.sem, exp_done.at(u - 1))
                    mask = causal16[:, :].unsqueeze(1) if c.causal else mask16[:, bass.ds(b, 1), :]
                    pe.matmul(SC[g % 2][:, :].rearrange("p (j t) -> p j t", j=4), ident16[:, :],
                              mask.to_broadcast([P, 4, P]), start=True, stop=False)
                    pe.matmul(SC[g % 2][:, :], QB[:, g // 4, :], KP[:, g % 2, :],
                              start=False, stop=True).then_inc(scores_ready.sem, 1)
                    if g:
                        tail(b, g - 1)
                tail(b, 7)
                pe.wait_ge(mix_done.sem, mix_done.at(b + 1))
                pe.wait_ge(aux_done.sem, aux_done.at(b))
                for k in range(2):
                    last = pe.transpose(OP[:, k * P:(k + 1) * P], ZB[:, k * P:(k + 1) * P], ident[:, :])
                last.then_inc(aux_ready.sem, 1)
                pe.wait_ge(aux_done.sem, aux_done.at(b + 1))
                for k in range(2):
                    last = pe.matmul(PJ[1][:, 0:DM], ZT[:, k, :], c.wo[:, k, :], start=(k == 0), stop=(k == 1))
                last.then_inc(out_ready.sem, 1)

        def dve_attn8(s, c):
            dve.wait_ge(xn_ready.sem, xn_ready.at(B))
            if c.bo is not None:
                dve.tensor_tensor(x[:, :, :], x[:, :, :], c.bo.unsqueeze(1).to_broadcast([P, B, DM]),
                                  ALU.add).then_inc(dve_own, V.up())
                dve.wait_ge(dve_own, V.now())
            with V.loop(B, 8) as b:
                dve.wait_ge(proj_ready.sem, proj_ready.at(2 * b + 1))
                for n, (dst, bias) in enumerate(((QB, c.bq), (KB, c.bk))):
                    bank = PJ[0][:, 2 * n * P:2 * (n + 1) * P].rearrange("p (c t) -> p c t", c=2)
                    if bias is None:
                        dve.tensor_copy(dst, bank).then_inc(proj_done.sem, 1)
                    else:
                        dve.tensor_tensor(dst, bank, bias.unsqueeze(2).to_broadcast([P, 2, P]),
                                          ALU.add).then_inc(proj_done.sem, 1)
                dve.wait_ge(proj_ready.sem, proj_ready.at(2 * b + 2))
                if c.bv is None:
                    dve.tensor_copy(VB, PJ[1][:, 0:64]).then_inc(proj_done.sem, 1)
                else:
                    dve.tensor_tensor(VB, PJ[1][:, 0:64], c.bv, ALU.add).then_inc(proj_done.sem, 1)
                for g in range(8):
                    u = b * 8 + g
                    dve_max(u, g % 2, 4, c.scale)
                    if g:
                        dve_probsT(u - 1)
                    dve_recip(u, g % 2, 4)
                dve_probsT(b * 8 + 7)
                dve.wait_ge(aux_ready.sem, aux_ready.at(b + 1))
                dve.tensor_copy(ZT, OP[:, 0:DM].rearrange("p (c t) -> p c t", c=2)).then_inc(aux_done.sem, 1)
                dve.wait_ge(out_ready.sem, out_ready.at(b + 1))
                dve.tensor_tensor(x[:, b, :], x[:, b, :], PJ[1][:, 0:DM], ALU.add).then_inc(out_done.sem, 1)

        def act_attn8(s, c):
            with A.loop(B, 0) as b:
                for g in range(8):
                    act_exp(b * 8 + g, g % 2, 4, c.scale)
                act.wait_ge(mix_ready.sem, mix_ready.at(b * 8 + 8))
                act.activation(ZB, ZP[:, 0:DM], ACT.Copy).then_inc(mix_done.sem, 1)

        def pool_attn8(s, c):
            def kpad(g):
                pool.tensor_tensor(KP[:, g % 2, :].rearrange("p (j t) -> p j t", j=4),
                                   KB[:, g // 4, :].unsqueeze(1).to_broadcast([P, 4, P]),
                                   heads8[:, 4 * (g % 4):4 * (g % 4) + 4].unsqueeze(2).to_broadcast([P, 4, P]),
                                   ALU.mult).then_inc(kpad_ready.sem, 1)

            pool.wait_ge(xnt_done.sem, xnt_done.at(B))
            with G.loop(B, 1 if c.cross else 0) as b:
                pool.wait_ge(proj_ready.sem, proj_ready.at(2 * b))
                if c.cross:
                    pool.tensor_copy(cb, ctxT[:, :, bass.ds(b * P, P)]).then_inc(pool_own, G.up())
                    pool.wait_ge(pool_own, G.now())
                pool.tensor_copy(xb, xnT[:, :, bass.ds(b * P, P)]).then_inc(slice_ready.sem, 1)
                pool.wait_ge(proj_done.sem, proj_done.at(3 * b + 2))
                kpad(0)
                for g in range(8):
                    if g < 7:
                        if g:
                            pool.wait_ge(scores_ready.sem, scores_ready.at(b * 8 + g))
                        kpad(g + 1)
                    pool_normalise(b * 8 + g, g % 2, 4)

        valid = small[:, 64:72]

        def pe_memory(s):
            pe.wait_ge(aux2_ready.sem, aux2_ready.at(1))
            for u in range(2):
                for j in range(4):
                    b = 4 * u + j
                    for k in range(DC):
                        pe.matmul(SC[u][:, j * P:(j + 1) * P], xnT[:, k, b * P:(b + 1) * P],
                                  ctxT[:, k, b * P:(b + 1) * P], start=(k == 0), stop=False)
                    last = pe.matmul(SC[u][:, j * P:(j + 1) * P], ident16[:, :], mask16[:, b, :],
                                     start=False, stop=True)
                last.then_inc(scores_ready.sem, 1)
            for u in range(2):
                pe_probsT(u, u)
                pe.wait_ge(probsT_done.sem, probsT_done.at(u + 1))
                for half in range(2):
                    bank = (ZP, OP, PJ[0], PJ[1])[2 * u + half]
                    for j in range(2):
                        b = 4 * u + 2 * half + j
                        last = pe.matmul(bank[:, j * DM:(j + 1) * DM], PT[:, 2 * half + j, :], ctxn[:, b, :],
                                         start=True, stop=True)
                last.then_inc(out_ready.sem, 1)

        def dve_memory(s):
            for u in range(2):
                dve_max(u, u, 4, DM ** -0.5)
            for u in range(2):
                dve_recip(u, u, 4)
            for u in range(2):
                dve_probsT(u)
            for u in range(2):
                dve.wait_ge(out_ready.sem, out_ready.at(u + 1))
                for half in range(2):
                    bank = (ZP, OP, PJ[0], PJ[1])[2 * u + half]
                    for j in range(2):
                        b = 4 * u + 2 * half + j
                        dve.scalar_tensor_tensor(x[:, b, :], bank[:, j * DM:(j + 1) * DM], valid[:, b:b + 1],
                                                 x[:, b, :], ALU.mult, ALU.add).then_inc(out_done.sem, 1)

        def act_memory(s):
            for u in range(2):
                act_exp(u, u, 4, DM ** -0.5)

        def pool_memory(s):
            for u in range(2):
                pool_normalise(u, u, 4)

        heads16 = sb("heads16", [P, 8])
        natural = xnT[:, :, :].rearrange("p c n -> p (c n)").rearrange("p (b d) -> p b d", b=B)
        xs = work[:, 6144:6400]

        def pe_feature_attn(s):
            def tail(b, h):
                u = b * 8 + h
                pe_probsT(u, h % 2)
                pe.wait_ge(probsT_done.sem, probsT_done.at(u + 1))
                if h == 0:
                    pe.wait_ge(mix_done.sem, mix_done.at(b))
                for m in range(2):
                    for n in range(2):
                        last = pe.matmul(ZP[:, m * P + 16 * h:m * P + 16 * h + 16], PT[:, 2 * m + n, :],
                                         ctxT[:, n, bass.ds(b * P + 16 * h, 16)], start=(n == 0), stop=(n == 1))
                last.then_inc(mix_ready.sem, 1)

            with pe.Fori(0, B) as b:
                pe.wait_ge(slice_ready.sem, slice_ready.at(b + 1))
                for h in range(8):
                    u = b * 8 + h
                    pe.wait_ge(kpad_ready.sem, kpad_ready.at(u + 1))
                    pe.wait_ge(exp_done.sem, exp_done.at(u - 1))
                    for m in range(2):
                        last = pe.matmul(SC[h % 2][:, m * DM:(m + 1) * DM], xs[:, m * P:(m + 1) * P],
                                         KP[:, h % 2, 0:DM], start=True, stop=True)
                    last.then_inc(scores_ready.sem, 1)
                    if h:
                        tail(b, h - 1)
                tail(b, 7)
                pe.wait_ge(mix_done.sem, mix_done.at(b + 1))
                pe.wait_ge(out_done.sem, out_done.at(b))
                for m in range(2):
                    last = pe.transpose(OP[:, m * P:(m + 1) * P], ZB[:, m * P:(m + 1) * P], ident[:, :])
                last.then_inc(out_ready.sem, 1)

        def dve_feature_attn(s):
            with V.loop(B, 8) as b:
                for h in range(8):
                    u = b * 8 + h
                    dve_max(u, h % 2, 2, 0.25)
                    if h:
                        dve_probsT(u - 1)
                    dve_recip(u, h % 2, 2)
                dve_probsT(b * 8 + 7)
                dve.wait_ge(out_ready.sem, out_ready.at(b + 1))
                dve.tensor_tensor(x[:, b, :], x[:, b, :], OP[:, 0:DM], ALU.add).then_inc(out_done.sem, 1)

        def act_feature_attn(s):
            with A.loop(B, 0) as b:
                for h in range(8):
                    act_exp(b * 8 + h, h % 2, 2, 0.25)
                act.wait_ge(mix_ready.sem, mix_ready.at(b * 8 + 8))
                act.activation(ZB, ZP[:, 0:DM], ACT.Copy).then_inc(mix_done.sem, 1)

        def pool_feature_attn(s):
            def kpad(b, h):
                stand_alone(pool)
                pool.tensor_tensor(KP[:, h % 2, 0:DM], ctxn[:, b, :], heads16[:, h:h + 1].to_broadcast([P, DM]),
                                   ALU.mult).then_inc(kpad_ready.sem, 1)

            pool.wait_ge(xn_ready.sem, xn_ready.at(B))
            with G.loop(B, 0) as b:
                pool.wait_ge(scores_ready.sem, scores_ready.at(b * 8))
                pool.tensor_copy(xs, natural[:, b, :]).then_inc(slice_ready.sem, 1)
                kpad(b, 0)
                for h in range(8):
                    if h < 7:
                        if h:
                            pool.wait_ge(scores_ready.sem, scores_ready.at(b * 8 + h))
                        kpad(b, h + 1)
                    pool_normalise(b * 8 + h, h % 2, 2)

        lg = work[:, 7296:7424].rearrange("p (b e) -> p b e", b=B)
        coef = small[:, 96:256].rearrange("p (b e) -> p b e", b=B)
        tri = rows_(arena_b, 15360, 16, 16)
        pair = work[:, 0:2048]
        tied = work[:, 2048:4096]
        rank = work[:, 7424:7552].rearrange("p (b e) -> p b e", b=B)
        peak = small[:, 72:80]
        denom = small[:, 80:88]

        def pe_route(E, w, sgate=None):
            for b in range(B):
                for k in range(DC):
                    last = pe.matmul(PJ[0][:, b * E:(b + 1) * E], xnT[:, k, b * P:(b + 1) * P], w[:, k, :],
                                     start=(k == 0), stop=(k == DC - 1))
            if sgate is not None:
                for b in range(B):
                    for k in range(DC):
                        last = pe.matmul(PJ[1][:, b:b + 1], xnT[:, k, b * P:(b + 1) * P], sgate[:, k, :],
                                         start=(k == 0), stop=(k == DC - 1))
            last.then_inc(aux2_ready.sem, 1)

        def dve_route(E, k, clip=None, bias=None, alpha=None, over_all=False):
            dve.wait_ge(aux2_ready.sem, aux2_ready.at(1))
            L = lg[:, :, 0:E]
            bank = PJ[0][:, 0:B * E].rearrange("p (b e) -> p b e", b=B)
            if clip is not None:
                dve.tensor_scalar(L, bank, clip, -clip, ALU.min, ALU.max).then_inc(dve_own, V.up())
            elif bias is not None:
                dve.tensor_tensor(L, bank, bias.unsqueeze(1).to_broadcast([P, B, E]), ALU.add).then_inc(dve_own, V.up())
            else:
                dve.tensor_copy(L, bank).then_inc(dve_own, V.up())
            dve.wait_ge(dve_own, V.now())
            four = [P, B, E, E]
            pairs, ties = (t[:, 0:B * E * E].rearrange("p (b e j) -> p b e j", b=B, e=E) for t in (pair, tied))
            other, own = L.unsqueeze(2).to_broadcast(four), L.unsqueeze(3).to_broadcast(four)
            flat = [t[:, 0:B * E * E] for t in (pair, tied)]
            dve.tensor_tensor(pairs, other, own, ALU.is_gt).then_inc(dve_own, V.up())
            dve.tensor_tensor(ties, other, own, ALU.is_equal).then_inc(dve_own, V.up())
            dve.tensor_reduce(peak, L, AX, ALU.max).then_inc(dve_own, V.up())
            dve.wait_ge(dve_own, V.now())
            dve.tensor_tensor(ties, ties, tri[:, 0:E, 0:E].unsqueeze(1).to_broadcast(four),
                              ALU.mult).then_inc(dve_own, V.up())
            dve.tensor_tensor(L, L, peak.unsqueeze(2).to_broadcast([P, B, E]), ALU.subtract).then_inc(aux3_ready.sem, 1)
            dve.wait_ge(dve_own, V.now())
            dve.tensor_tensor(flat[0], flat[0], flat[1], ALU.add).then_inc(dve_own, V.up())
            dve.wait_ge(dve_own, V.now())
            R = rank[:, :, 0:E]
            dve.tensor_reduce(R, pairs, AX, ALU.add).then_inc(dve_own, V.up())
            dve.wait_ge(dve_own, V.now())
            dve.tensor_scalar(R, R, float(k), None, ALU.is_lt).then_inc(dve_own, V.up())
            dve.wait_ge(aux4_ready.sem, aux4_ready.at(1))
            if over_all:
                dve.tensor_reduce(denom, L, AX, ALU.add).then_inc(dve_own, V.up())
            dve.wait_ge(dve_own, V.now())
            C = coef[:, :, 0:E]
            dve.tensor_tensor(C, L, R, ALU.mult).then_inc(dve_own, V.up())
            dve.wait_ge(dve_own, V.now())
            if not over_all:
                dve.tensor_reduce(denom, C, AX, ALU.add).then_inc(dve_own, V.up())
                dve.wait_ge(dve_own, V.now())
            dve.reciprocal(denom, denom).then_inc(dve_own, V.up())
            dve.wait_ge(dve_own, V.now())
            dve.tensor_tensor(C, C, denom.unsqueeze(2).to_broadcast([P, B, E]), ALU.mult).then_inc(dve_own, V.up())
            dve.wait_ge(dve_own, V.now())
            if alpha is not None:
                dve.tensor_tensor(C, C, alpha.unsqueeze(1).to_broadcast([P, B, E]), ALU.mult).then_inc(dve_own, V.up())
                dve.wait_ge(dve_own, V.now())

        def act_route(E):
            act.wait_ge(aux3_ready.sem, aux3_ready.at(1))
            act.activation(lg[:, :, 0:E], lg[:, :, 0:E], ACT.Exp).then_inc(aux4_ready.sem, 1)

        coefT = work[0:B, 8192:9216]

        def pe_coefT(E):
            pe.wait_ge(aux5_ready.sem, aux5_ready.at(1))
            for b in range(B):
                last = pe.transpose(SC[b // 4][0:E, (b % 4) * P:(b % 4 + 1) * P], coef[:, b, 0:E], ident[:, :])
            last.then_inc(aux6_ready.sem, 1)

        NS = 2048
        gatewT = rows_(arena_b, 14848, 2, 8)
        WT = rows_(arena_b, 2048, 2, DM)
        atoms = arena_b[0:64, 2560:4608]
        slots = arena_b[0:8, 4608:6656]
        gather = rows_(arena_b, 6656, 2, NS)
        scatter = rows_(arena_b, 10752, 16, DM)
        eaw = arena_b[0:8, 14864:14928]
        eawT = arena_b[0:64, 14928:14936]
        colsi = work[:, 0:2048].bitcast(I32)
        colsf = work[:, 2048:4096]
        rowsi = small[:, 512:528].bitcast(I32)
        rowsf = small[:, 528:544]
        iotaf = arena_b[:, 15104:15360]
        iotap = sb("iotap", [P, 2])
        em = small[0:8, 88:92]
        xv = work[:, 4096:5120].rearrange("p (r n) -> p r n", r=2)
        xg = work[:, 5120:6144].rearrange("p (r n) -> p r n", r=2)

        def dve_slots_prepare():
            dve.wait_ge(loaded["w2"], 16 * 7)
            dve.tensor_reduce(em[:, 0:1], eaw, AX, ALU.max, negate=True).then_inc(aux_ready.sem, 1)
            dve.tensor_scalar(rowsi, rowsi, 8, None, ALU.arith_shift_right).then_inc(dve_own, V.up())
            dve.tensor_scalar(colsi, colsi, DM - 1, None, ALU.bitwise_and).then_inc(dve_own, V.up())
            dve.wait_ge(dve_own, V.now())
            dve.tensor_copy(rowsf, rowsi).then_inc(dve_own, V.up())
            dve.tensor_copy(colsf, colsi).then_inc(dve_own, V.up())
            dve.wait_ge(dve_own, V.now())
            for k in range(DC):
                dve.tensor_scalar(gather[:, k, :], colsf, iotap[:, k:k + 1], None,
                                  ALU.is_equal).then_inc(dve_own, V.up())
            with V.loop(NS // P, 1) as i:
                dve.tensor_scalar(scatter[:, i, :], iotaf[:, :], rowsf[:, bass.ds(i, 1)], None,
                                  ALU.is_equal).then_inc(dve_own, V.up())
            dve.wait_ge(aux_done.sem, aux_done.at(1))
            dve.reciprocal(em[:, 2:3], em[:, 1:2]).then_inc(dve_own, V.up())
            dve.wait_ge(dve_own, V.now())
            dve.tensor_scalar(eaw, eaw, em[:, 2:3], None, ALU.mult).then_inc(slice_ready.sem, 1)
            dve.wait_ge(proj_ready.sem, proj_ready.at(1))
            dve.tensor_copy(eawT, TP[0:64, 0:8]).then_inc(slice_ready.sem, 1)
            dve.wait_ge(aux_done.sem, aux_done.at(2))
            for i in range(4):
                dve.wait_ge(proj_ready.sem, proj_ready.at(i + 2))
                dve.tensor_tensor(slots[:, i * 512:(i + 1) * 512], (SC[0], SC[1], TP, ZP)[i][0:8, :],
                                  slots[:, i * 512:(i + 1) * 512], ALU.mult).then_inc(proj_done.sem, 1)

        def act_slots_prepare():
            act.wait_ge(aux_ready.sem, aux_ready.at(1))
            act.activation(eaw, eaw, ACT.Exp, bias=em[:, 0:1], accum_out=em[:, 1:2]).then_inc(aux_done.sem, 1)
            act.activation(slots, slots, ACT.Sigmoid).then_inc(aux_done.sem, 1)

        def pe_slots_prepare():
            pe.wait_ge(slice_ready.sem, slice_ready.at(1))
            pe.transpose(TP[0:64, 0:8], eaw, ident[0:8, 0:8]).then_inc(proj_ready.sem, 1)
            pe.wait_ge(slice_ready.sem, slice_ready.at(2))
            for i in range(4):
                pe.matmul((SC[0], SC[1], TP, ZP)[i][0:8, :], eawT, atoms[:, i * 512:(i + 1) * 512],
                          start=True, stop=True).then_inc(proj_ready.sem, 1)
            pe.wait_ge(proj_done.sem, proj_done.at(4))

        def pe_slots():
            pe_coefT(8)
            for b in range(B):
                bank = (ZP, OP, PJ[0], PJ[1])[b // 2]
                for k in range(DC):
                    last = pe.matmul(bank[:, (b % 2) * DM:(b % 2 + 1) * DM], xnT[:, k, b * P:(b + 1) * P],
                                     WT[:, k, :], start=(k == 0), stop=(k == DC - 1))
            last.then_inc(out_ready.sem, 1)
            pe.wait_ge(out_done.sem, out_done.at(B))
            pe.wait_ge(slice_ready.sem, slice_ready.at(3))
            GX, VL, ACC = (psum[0], psum[1]), (psum[2], psum[3]), psum[4:6]

            def scatter_out(h, i):
                u = h * 16 + i
                pe.wait_ge(probs_ready.sem, probs_ready.at(u + 1))
                for t in range(4):
                    last = pe.matmul(ACC[t // 2][:, (t % 2) * DM:(t % 2 + 1) * DM], xg[:, i % 2, t * P:(t + 1) * P],
                                     scatter[:, i, :], start=(i == 0 and t % 2 == 0), stop=(i == 15),
                                     skip_group_check=True)
                last.then_inc(mix_ready.sem, 1)

            with pe.Fori(0, 2) as h:
                pe.wait_ge(out_done.sem, out_done.at(B + h * 4))
                for i in range(16):
                    u = h * 16 + i
                    if i >= 2:
                        pe.wait_ge(probs_ready.sem, probs_ready.at(u - 1))
                    for k in range(DC):
                        pe.matmul(GX[i % 2][:, :], gather[:, k, i * P:(i + 1) * P],
                                  xnT[:, k, bass.ds(h * 512, 512)], start=(k == 0), stop=(k == DC - 1))
                    pe.matmul(VL[i % 2][:, :], slots[:, i * P:(i + 1) * P],
                              coefT[:, bass.ds(h * 512, 512)], start=True, stop=True).then_inc(scores_ready.sem, 1)
                    if i:
                        scatter_out(h, i - 1)
                scatter_out(h, 15)

        def act_slots():
            with A.loop(16, 0) as v:
                for r in range(2):
                    u = v * 2 + r
                    act.wait_ge(scores_ready.sem, scores_ready.at(u + 1))
                    act.activation(xv[:, r, :], psum[2 + r][:, :], ACT.Copy).then_inc(mix_done.sem, 1)

        def dve_slots():
            dve.sem_inc(aux5_ready.sem, 1)
            dve.wait_ge(aux6_ready.sem, aux6_ready.at(1))
            for i in range(2):
                dve.tensor_copy(coefT[:, i * 512:(i + 1) * 512], SC[i][0:8, :]).then_inc(dve_own, V.up())
            dve.wait_ge(dve_own, V.now())
            dve.sem_inc(slice_ready.sem, 1)
            dve.wait_ge(out_ready.sem, out_ready.at(1))
            for b in range(B):
                bank = (ZP, OP, PJ[0], PJ[1])[b // 2]
                dve.tensor_tensor(x[:, b, :], x[:, b, :], bank[:, (b % 2) * DM:(b % 2 + 1) * DM],
                                  ALU.add).then_inc(out_done.sem, 1)
            with V.loop(2, 0) as h:
                with V.loop(8, 0) as v:
                    for r in range(2):
                        u = h * 16 + v * 2 + r
                        dve.wait_ge(mix_done.sem, mix_done.at(u + 1))
                        dve.tensor_tensor(xg[:, r, :], psum[r][:, :], xv[:, r, :], ALU.mult).then_inc(probs_ready.sem, 1)
                dve.wait_ge(mix_ready.sem, mix_ready.at((h + 1) * 16))
                for t in range(4):
                    dve.tensor_tensor(x[:, bass.ds(h * 4 + t, 1), :], x[:, bass.ds(h * 4 + t, 1), :],
                                      psum[4 + t // 2][:, (t % 2) * DM:(t % 2 + 1) * DM].unsqueeze(1),
                                      ALU.add).then_inc(out_done.sem, 1)

        hid = work[:, 4096:5120].rearrange("p (r n) -> p r n", r=2)
        gat = work[:, 5120:6144].rearrange("p (r n) -> p r n", r=2)

        def pe_ffn(c):
            def down(par, e, h, f):
                v = (e * 2 + h) * c.nf + f
                if f == 0:
                    pe.wait_ge(acc_done.sem, acc_done.at(e * 2 + h - 1))
                pe.wait_ge(hidden_done.sem, hidden_done.at(v + 1))
                for t in range(4):
                    bank = psum[4 + 2 * h + t // 2]
                    last = pe.matmul(bank[:, (t % 2) * DM:(t % 2 + 1) * DM], hid[0:c.M, f % 2, t * P:(t + 1) * P],
                                     c.down[par][:, f, :], start=(f == 0 and t % 2 == 0), stop=(f == c.nf - 1),
                                     skip_group_check=True)
                if f == c.nf - 1:
                    last.then_inc(acc_ready.sem, 1)

            with pe.Fori(0, c.E // 2) as i:
                for par in range(2):
                    e = i * 2 + par
                    c.arrived(pe, i, par)
                    for h in range(2):
                        for f in range(c.nf):
                            v = (e * 2 + h) * c.nf + f
                            pe.wait_ge(hidden_done.sem, hidden_done.at(v - 1))
                            for g in range(2 if c.gated else 1):
                                for k in range(DC):
                                    last = pe.matmul(psum[2 * g + f % 2][0:c.M, :], c.up[par](g, f, k),
                                                     xnT[:, k, h * 512:(h + 1) * 512],
                                                     start=(k == 0), stop=(k == DC - 1))
                            last.then_inc(up_ready.sem, 1)
                            if (h, f) != (0, 0):
                                down(par, e, *((h, f - 1) if f else (h - 1, c.nf - 1)))
                    down(par, e, 1, c.nf - 1)

        def act_ffn(c):
            with A.loop(c.E // 2, 0) as i:
                for par in range(2):
                    e = i * 2 + par
                    for h in range(2):
                        for f in range(c.nf):
                            v = (e * 2 + h) * c.nf + f
                            act.wait_ge(up_ready.sem, up_ready.at(v + 1))
                            if c.gated:
                                act.activation(gat[0:c.M, f % 2, :], psum[f % 2][0:c.M, :],
                                               c.func).then_inc(gate_ready.sem, 1)
                            else:
                                stand_alone(act)
                                act.activation(hid[0:c.M, f % 2, :], psum[f % 2][0:c.M, :], c.func,
                                               bias=c.bias[:, bass.ds(e * c.nf + f, 1)]).then_inc(hidden_done.sem, 1)

        def dve_ffn_half(c, e, h, between=None):
            if c.gated:
                for f in range(c.nf):
                    v = (e * 2 + h) * c.nf + f
                    dve.wait_ge(gate_ready.sem, gate_ready.at(v + 1))
                    dve.tensor_tensor(hid[0:c.M, f % 2, :], gat[0:c.M, f % 2, :], psum[2 + f % 2][0:c.M, :],
                                      ALU.mult).then_inc(hidden_done.sem, 1)
                    if between is not None:
                        between(h * c.nf + f)
            dve.wait_ge(acc_ready.sem, acc_ready.at(e * 2 + h + 1))
            for t in range(4):
                bank = psum[4 + 2 * h + t // 2][:, (t % 2) * DM:(t % 2 + 1) * DM]
                b = 4 * h + t
                if c.weighted:
                    last = dve.scalar_tensor_tensor(x[:, b, :], bank, coef[:, b, bass.ds(e, 1)], x[:, b, :],
                                                    ALU.mult, ALU.add)
                else:
                    last = dve.tensor_tensor(x[:, b, :], x[:, b, :], bank, ALU.add)
            last.then_inc(acc_done.sem, 1)

        def dve_ffn(c):
            with V.loop(c.E // 2, 0) as i:
                for par in range(2):
                    for h in range(2):
                        dve_ffn_half(c, i * 2 + par, h)

        def sp_ring(c):
            with sp.Fori(1, c.E // 2) as i:
                for par in range(2):
                    e = i * 2 + par
                    sp.wait_ge(acc_ready.sem, acc_ready.at(2 * e - 2))
                    c.load(par, e)

        W4 = 3 * DM
        codes = [arena_a[:, 2048 + r * W4:2048 + (r + 1) * W4].bitcast(I32) for r in range(2)]
        scales = [arena_a[:, 3584 + r * W4:3584 + (r + 1) * W4] for r in range(2)]
        mags = arena_a[:, 5120:6656]
        sgns = arena_a[:, 6656:8192]
        tops = arena_a[:, 8192:9728]
        sfac = arena_a[:, 9728:11264]
        wq4 = [arena_a[:, 11264 + r * 1536:11264 + (r + 1) * 1536] for r in range(2)]
        lows = arena_a[:, 14336:15872]

        def dve_dequant(i, r, piece, first=False):
            m, g, j = mags.bitcast(I32), sgns.bitcast(I32), i * 2 + r
            if piece == 0:
                dve.wait_ge(loaded["w5" + "ab"[r]], (i + 1) * 32)
                dve.wait_ge(scale_ready.sem, scale_ready.at(j))
                dve.tensor_scalar(m[:, 0:W4], codes[r], 7, None, ALU.bitwise_and)
                dve.tensor_scalar(m[:, W4:2 * W4], codes[r], 4, 7, ALU.logical_shift_right,
                                  ALU.bitwise_and).then_inc(dve_own, V.up())
            elif piece == 1:
                dve.tensor_scalar(g[:, 0:W4], codes[r], 8, None, ALU.bitwise_and)
                dve.tensor_scalar(g[:, W4:2 * W4], codes[r], 4, 8, ALU.logical_shift_right,
                                  ALU.bitwise_and).then_inc(codes_ready.sem, 1)
                dve.wait_ge(dve_own, V.now())
                dve.scalar_tensor_tensor(lows, m, 4.0, m, ALU.max, ALU.add).then_inc(dve_own, V.up())
            elif piece == 2:
                dve.wait_ge(scale_ready.sem, scale_ready.at(j + 1))
                dve.wait_ge(dve_own, V.now())
                dve.scalar_tensor_tensor(lows, lows, 0.5, tops, ALU.mult, ALU.add).then_inc(dve_own, V.up())
            else:
                dve.wait_ge(dve_own, V.now())
                if not first:
                    dve.wait_ge(acc_ready.sem, acc_ready.at(j * 2 - 2))
                dve.tensor_tensor(wq4[r], lows, sfac, ALU.mult).then_inc(weights_ready.sem, 1)

        def pool_dequant():
            with G.loop(4, 2) as i:
                for r in range(2):
                    j = i * 2 + r
                    pool.wait_ge(codes_ready.sem, codes_ready.at(j + 1))
                    pool.wait_ge(weights_ready.sem, weights_ready.at(j))
                    stand_alone(pool)
                    pool.tensor_scalar(tops, mags.bitcast(I32), 6.0, -8.0, ALU.max, ALU.add)
                    pool.tensor_scalar(sfac, sgns.bitcast(I32), -0.25, 1.0, ALU.mult, ALU.add).then_inc(pool_own, G.up())
                    pool.wait_ge(pool_own, G.now())
                    pool.tensor_tensor(sfac.rearrange("p (l n) -> p l n", l=2), sfac.rearrange("p (l n) -> p l n", l=2),
                                       scales[r].unsqueeze(1).to_broadcast([P, 2, W4]),
                                       ALU.mult).then_inc(scale_ready.sem, 1)

        xc = [work[:, k * 1024:(k + 1) * 1024].rearrange("p (b t) -> p b t", b=B) for k in range(DC)]
        dx = rows_(arena_b, 12288, 2, 1024)
        NT = B * P
        sp_, sn_, dl_, da_, bu_, hh_ = (work[0:64, 2048 + k * NT:2048 + (k + 1) * NT] for k in range(6))
        wB = rows_(arena_b, 8192, 2, 64)
        wC = rows_(arena_b, 8320, 2, 64)
        wD = rows_(arena_b, 8448, 2, 64)
        wIn = rows_(arena_b, 8576, 2, 64)
        wOut = arena_b[0:64, 8704:8960]
        cw = small[:, 544:552].rearrange("p (c k) -> p c k", c=DC)
        cbias = small[:, 552:554]
        dskip = small[:, 554:556]
        alog = small[0:64, 556:557]
        nega = small[0:64, 557:558]

        def dve_scan():
            dve.wait_ge(loaded["w9"], 16 * 9)
            dve.wait_ge(xnt_done.sem, xnt_done.at(B))
            xk = [xnT[:, k, :].rearrange("p (b t) -> p b t", b=B) for k in range(DC)]
            for k in range(DC):
                dve.tensor_scalar(xc[k], xk[k], cw[:, k, 3:4], cbias[:, k:k + 1], ALU.mult,
                                  ALU.add).then_inc(dve_own, V.up())
            for d in range(1, 4):
                dve.wait_ge(dve_own, V.now())
                for k in range(DC):
                    dve.scalar_tensor_tensor(xc[k][:, :, d:P], xk[k][:, :, 0:P - d], cw[:, k, 3 - d:4 - d],
                                             xc[k][:, :, d:P], ALU.mult, ALU.add).then_inc(dve_own, V.up())
            dve.wait_ge(dve_own, V.now())
            dve.sem_inc(aux3_ready.sem, 1)
            for k in range(DC):
                dve.tensor_scalar(dx[:, k, :], xc[k].rearrange("p b t -> p (b t)"), dskip[:, k:k + 1], None,
                                  ALU.mult).then_inc(dve_own, V.up())
            dve.wait_ge(aux_ready.sem, aux_ready.at(3))
            for i in range(2):
                half = slice(i * 512, (i + 1) * 512)
                dve.tensor_scalar(sp_[:, half], psum[4 + i][0:64, :], 0.0, None, ALU.max).then_inc(dve_own, V.up())
                dve.tensor_scalar(sn_[:, half], psum[4 + i][0:64, :], 0.0, None, ALU.min).then_inc(dve_own, V.up())
            dve.wait_ge(dve_own, V.now())
            dve.tensor_tensor(sn_, sn_, sp_, ALU.subtract).then_inc(aux4_ready.sem, 1)
            dve.wait_ge(aux5_ready.sem, aux5_ready.at(1))
            dve.tensor_tensor(dl_, dl_, sp_, ALU.add).then_inc(dve_own, V.up())
            dve.wait_ge(dve_own, V.now())
            dve.sem_inc(aux6_ready.sem, 1)
            for i in range(2):
                half = slice(i * 512, (i + 1) * 512)
                dve.tensor_tensor(bu_[:, half], dl_[:, half], psum[i][0:64, :], ALU.mult).then_inc(dve_own, V.up())
            dve.wait_ge(dve_own, V.now())
            dve.wait_ge(aux2_ready.sem, aux2_ready.at(1))
            for i in range(2):
                half = slice(i * 512, (i + 1) * 512)
                dve.tensor_tensor(bu_[:, half], bu_[:, half], psum[6 + i][0:64, :], ALU.mult).then_inc(dve_own, V.up())
            dve.wait_ge(aux5_ready.sem, aux5_ready.at(2))
            dve.memset(da_.rearrange("p (b t) -> p b t", b=B)[:, :, 0:1], 0.0).then_inc(dve_own, V.up())
            dve.wait_ge(dve_own, V.now())
            dve.tensor_tensor_scan(hh_, da_, bu_, 0.0, ALU.mult, ALU.add).then_inc(dve_own, V.up())
            dve.wait_ge(dve_own, V.now())
            for i in range(2):
                half = slice(i * 512, (i + 1) * 512)
                last = dve.tensor_tensor(hh_[:, half], hh_[:, half], psum[2 + i][0:64, :], ALU.mult)
                last.then_inc(slice_ready.sem, 1)
            for b in range(B):
                dve.wait_ge(out_ready.sem, out_ready.at(b + 1))
                dve.tensor_tensor(x[:, b, :], x[:, b, :], psum[b % 4][:, 0:DM], ALU.add).then_inc(out_done.sem, 1)

        def act_scan():
            act.wait_ge(loaded["w9"], 16 * 9)
            act.activation(nega, alog, ACT.Exp).then_inc(act_own, A.up())
            act.wait_ge(act_own, A.now())
            act.activation(nega, nega, ACT.Copy, scale=-1.0).then_inc(act_own, A.up())
            act.wait_ge(act_own, A.now())
            act.wait_ge(aux4_ready.sem, aux4_ready.at(1))
            act.activation(sn_, sn_, ACT.Exp).then_inc(act_own, A.up())
            act.wait_ge(act_own, A.now())
            act.activation(dl_, sn_, ACT.Ln, bias=1.0).then_inc(aux5_ready.sem, 1)
            act.wait_ge(aux6_ready.sem, aux6_ready.at(1))
            act.activation(da_, dl_, ACT.Exp, scale=nega).then_inc(aux5_ready.sem, 1)

        def pe_scan():
            pe.wait_ge(loaded["w9"], 16 * 9)
            for n, w in enumerate((wB, wC, wD)):
                for i in range(2):
                    for k in range(DC):
                        last = pe.matmul(psum[2 * n + i][0:64, :], w[:, k, :], xnT[:, k, i * 512:(i + 1) * 512],
                                         start=(k == 0), stop=(k == DC - 1))
                last.then_inc(aux_ready.sem, 1)
            pe.wait_ge(aux3_ready.sem, aux3_ready.at(1))
            for i in range(2):
                for k in range(DC):
                    last = pe.matmul(psum[6 + i][0:64, :], wIn[:, k, :],
                                     work[:, k * 1024 + i * 512:k * 1024 + (i + 1) * 512],
                                     start=(k == 0), stop=(k == DC - 1))
            last.then_inc(aux2_ready.sem, 1)
            pe.wait_ge(slice_ready.sem, slice_ready.at(2))
            for b in range(B):
                if b >= 4:
                    pe.wait_ge(out_done.sem, out_done.at(b - 3))
                toks = slice(b * P, (b + 1) * P)
                pe.matmul(psum[b % 4][:, 0:DM], hh_[:, toks], wOut, start=True, stop=False, skip_group_check=True)
                for k in range(DC):
                    last = pe.matmul(psum[b % 4][:, k * P:(k + 1) * P], dx[:, k, toks], ident[:, :],
                                     start=False, stop=(k == DC - 1), skip_group_check=True)
                last.then_inc(out_ready.sem, 1)

        bqT, bkT = small[:, 32:48], small[:, 48:64]
        bo0, bv0 = small[:, 256:512], work[:, 7168:9216]
        s0 = Attention(wq=rows_(arena_a, 0, 2, 2048), wk=rows_(arena_a, 4096, 2, 2048), wv=rows_(arena_a, 8192, 2, 2048),
                 wo=rows_(arena_a, 12288, 16, DM), bq=bqT, bk=bkT, bv=bv0, bo=bo0, causal=True,
                 scale=128 ** -0.5, w="w0", nw=8)

        wts1 = [(rows_(ar, 0, 2, DM), rows_(ar, 512, 2, DM), rows_(ar, 1024, 2, 64), rows_(ar, 1152, 2, DM))
                for ar in (arena_b, arena_a)]
        s1 = Attention(wq=wts1[0][0], wk=wts1[0][1], wv=wts1[0][2], wo=wts1[0][3], bq=small[:, 560:562],
                 bk=small[:, 562:564], bv=small[:, 564:628], bo=small[:, 640:896], cross=True, scale=8 ** -0.5,
                 w="w1", nw=10)
        s3 = Attention(wq=wts1[1][0], wk=wts1[1][1], wv=wts1[1][2], wo=wts1[1][3], causal=True, scale=8 ** -0.5,
                 w="w3", nw=4)
        wts5 = [w.rearrange("p (l m n) -> p l m n", l=2, m=3) for w in wq4]
        s5 = FeedForward(E=8, nf=2, M=P, gated=True, func=ACT.Gelu_apprx_tanh, weighted=False,
                 up=[lambda g, f, k, w=w: w[:, k, g, f::2] for w in wts5], down=[w[:, :, 2, :] for w in wts5],
                 arrived=lambda eng, i, par: eng.wait_ge(weights_ready.sem, weights_ready.at(i * 2 + par + 1)))
        s6 = Attention(wq=rows_(arena_b, 0, 2, 2048), wk=rows_(arena_b, 4096, 2, 512), wv=rows_(arena_b, 5120, 2, 512),
                 wo=rows_(arena_b, 6144, 16, DM), cos=arena_b[:, 10240:10368], sin=arena_b[:, 10368:10496],
                 gqa=True, causal=True, rope=True, scale=128 ** -0.5, w="w6", nw=6)
        s7 = Attention(wq=s0.wq, wk=s0.wk, wv=s0.wv, wo=s0.wo, cross=True, scale=128 ** -0.5, w="w7", nw=4)
        fc1 = [rows_(arena_b, 4096 * r, 2, 1024) for r in range(2)]
        fc2 = [rows_(arena_b, 4096 * r + 2048, 8, DM) for r in range(2)]
        b2e, gatew8 = arena_b[0:8, 9216:9472], rows_(arena_b, 9472, 2, 8)
        gateb8, alpha8 = small[:, 960:968], small[:, 968:976]
        s8 = FeedForward(E=8, nf=8, M=P, gated=False, func=ACT.Gelu, weighted=True, bias=small[:, 896:960],
                 up=[lambda g, f, k, w=w: w[:, k, f * P:(f + 1) * P] for w in fc1], down=fc2,
                 arrived=lambda eng, i, par: eng.wait_ge(loaded["w8" + "ab"[par]], (i + 1) * 32),
                 load=lambda r, e: load_expert(fc1, "fc1", fc2, "fc2", "w8", r, e))
        MI = 88
        w13 = [rows_(arena_a, 2048 * r, 2, 4 * MI) for r in range(2)]
        w2 = [rows_(arena_a, 2048 * r + 704, 2, DM)[0:MI] for r in range(2)]
        gatew11, sgate11 = rows_(arena_a, 4096, 2, 16), rows_(arena_a, 4128, 2, 1)
        s11 = FeedForward(E=20, nf=2, M=MI, gated=True, func=ACT.Silu, weighted=True,
                  up=[lambda g, f, k, w=w: w[:, k, (2 * g + f) * MI:(2 * g + f + 1) * MI] for w in w13], down=w2,
                  arrived=lambda eng, i, par: eng.wait_ge(loaded["w11" + "ab"[par]], (i + 1) * 32),
                  load=lambda r, e: load_expert(w13, "w13", w2, "w2", "w11", r, e))

        def load_expert(ups, up_name, downs, down_name, landed, r, e):
            for dst, name in ((ups[r], up_name), (downs[r], down_name)):
                src = D[name][e] if isinstance(e, int) else D[name][bass.ds(e, 1)].rearrange("e p k n -> (e p) k n")
                sp.dma_start(dst, src).then_inc(loaded[landed + "ab"[r]], 16)

        def n(k, *which):
            return {w: k for w in which}

        softmax = ("scores_ready", "max_ready", "exp_done", "recip_ready", "probs_ready", "probsT_ready",
                   "probsT_done")
        norm = n(1, "var_ready", "std_ready") | n(B, "xn_ready", "xnt_ready", "xnt_done")
        attn128 = norm | n(4 * B, *softmax, "mix_ready", "mix_done", "out_ready", "out_done") \
            | n(12 * B, "proj_ready", "proj_done") | n(B, "slice_ready")
        attn8 = norm | n(8 * B, *softmax, "mix_ready", "kpad_ready") \
            | n(B, "slice_ready", "mix_done", "aux_ready", "aux_done", "out_ready", "out_done") \
            | n(2 * B, "proj_ready") | n(3 * B, "proj_done")
        route = n(1, "aux2_ready", "aux3_ready", "aux4_ready")

        def ffn(c):
            return n(2 * c.E * c.nf, "up_ready", "hidden_done", *(["gate_ready"] if c.gated else [])) \
                | n(2 * c.E, "acc_ready", "acc_done")

        steps = {
            0: attn128,
            1: attn8 | n(1, "aux2_ready"),
            2: norm | route | n(1, "aux_ready", "aux5_ready", "aux6_ready") | n(2, "aux_done") | n(3, "slice_ready")
            | n(5, "proj_ready") | n(4, "proj_done") | n(1, "out_ready") | n(16, "out_done")
            | n(32, "scores_ready", "mix_done", "probs_ready", "mix_ready"),
            3: attn8,
            4: norm | n(2, *softmax, "out_ready") | n(1, "aux2_ready") | n(B, "out_done"),
            5: norm | ffn(s5) | n(8, "codes_ready", "scale_ready", "weights_ready"),
            6: attn128 | n(8 * B, "aux_ready"),
            7: attn128,
            8: norm | route | n(1, "aux5_ready", "aux6_ready", "slice_ready", "out_ready") | n(B, "out_done") | ffn(s8),
            9: norm | n(3, "aux_ready") | n(1, "aux2_ready", "aux3_ready", "aux4_ready", "aux6_ready")
            | n(2, "aux5_ready", "slice_ready") | n(B, "out_ready", "out_done"),
            10: n(1, "var_ready", "std_ready") | n(B, "xn_ready", "slice_ready", "mix_done", "out_ready", "out_done")
            | n(8 * B, *softmax, "mix_ready", "kpad_ready"),
            11: norm | route | n(1, "aux6_ready") | ffn(s11),
        }
        bases, total = {}, {t.sem.name: 0 for t in tallies}
        for s in stages:
            bases[s] = dict(total)
            for n, k in steps[s].items():
                total[n] += k
        done_before = {s: k for k, s in enumerate(stages)}

        def enter(eng, s):
            for t in tallies:
                t.base = bases[s][t.sem.name]
            if done_before[s]:
                eng.wait_ge(stage_done.sem, done_before[s] + 1)

        block = ctx.enter_context(nc.Block())

        @block.sync
        def _(sp_eng):
            def load(landed, *pairs):
                if landed[0] == "w" and int(landed.strip("wab")) not in stages and pairs[0][1] != "mask_pair":
                    return
                for dst, name in pairs:
                    sp.dma_start(dst, name if not isinstance(name, str) else D[name]).then_inc(loaded[landed], 16)

            def after(s):
                if s in done_before:
                    sp.wait_ge(stage_done.sem, done_before[s] + 2)

            def every(name):
                return D[name].partition_broadcast(P)

            load("x", (x[:, :, :], D["x"].rearrange("b t d -> t b d")))
            load("const", (ident[:, :], "ident"), (xn2[:, 0, 0:P], "causal"),
                 (heads8[:, :], "heads8"), (heads16[:, :], "heads16"), (tri[:, :, :], every("tri")),
                 (iotaf[:, :], every("iotaf")), (iotap[:, :], "iotap"))
            if 0 in stages:
                load("w0", (s0.bq, "bqT"), (s0.bk, "bkT"), (s0.bv, every("bv0")), (s0.bo, every("bo0")),
                     (s0.wq, "wq0"), (s0.wk, "wk0"), (s0.wv, "wv0"), (s0.wo, "wo0"))
            load("ctx", (ctxn[:, :, :], D["ctx"].rearrange("b t d -> t b d")), (ctxT[:, :, :], "ctxT"))
            if 1 in stages:
                load("w1", (s1.wq, "wq1"), (s1.wk, "wk1"), (s1.wv, "wv1"), (s1.wo, "wo1"), (s1.bq, "bq1"),
                     (s1.bk, "bk1"), (s1.bv, every("bv1")), (s1.bo, every("bo1")))
            load("w1", (pair_mask[:, :], "mask_pair"), (row_mask[:, :, :], every("mask_row")))
            if 2 in stages:
                load("w2", (WT, "WT"), (atoms, "atoms"), (slots, "importance"), (eaw, "eaw"), (gatewT, "gatew2"),
                     (rowsi, "slot_rows"))
            after(0)
            load("w3", (s3.wq, "wq3"), (s3.wk, "wk3"), (s3.wv, "wv3"), (s3.wo, "wo3"))
            if 5 in stages:
                for r in range(2):
                    load("w5" + "ab"[r], (codes[r], D["codes"][r]), (scales[r], D["scales"][r]))
            after(1)
            if 2 in stages:
                load("w2", (colsi, every("slot_cols")))
            after(2)
            if 6 in stages:
                load("w6", (s6.wq, "wq6"), (s6.wk, "wk6"), (s6.wv, "wv6"), (s6.wo, "wo6"), (s6.cos, "cosT"),
                     (s6.sin, "sinT"))
            if 5 in stages:
                enter(sp, 5)
                with sp.Fori(1, 4) as i:
                    for r in range(2):
                        j = i * 2 + r
                        sp.wait_ge(scale_ready.sem, scale_ready.at(j - 1))
                        for dst, name in ((codes[r], "codes"), (scales[r], "scales")):
                            sp.dma_start(dst, D[name][bass.ds(j, 1)].rearrange("e p n -> (e p) n")
                                         ).then_inc(loaded["w5" + "ab"[r]], 16)
            after(5)
            if 7 in stages:
                load("w7", (s7.wq, "wq7"), (s7.wk, "wk7"), (s7.wv, "wv7"), (s7.wo, "wo7"))
            after(6)
            load("w8", (b2e, "b2e"), (gatew8, "gatew8"), (gateb8, every("gateb8")), (alpha8, every("alpha8")),
                 (s8.bias, "b1T"))
            if 8 in stages:
                for r in range(2):
                    s8.load(r, r)
            load("w9", (wB, "wB9"), (wC, "wC9"), (wD, "wD9"), (wIn, "wIn9"), (wOut, "wOut9"), (cw, "cw9"),
                 (cbias, "cb9"), (dskip, "dskip9"), (alog, "alog9"))
            after(7)
            load("w11", (gatew11, "gatew11"), (sgate11, "sgate11"))
            if 11 in stages:
                for r in range(2):
                    s11.load(r, r)
            for s, c in ((8, s8), (11, s11)):
                if s in stages:
                    enter(sp, s)
                    sp_ring(c)
            sp.wait_ge(stage_done.sem, len(stages) + 1)
            sp.dma_start(out.rearrange("b t d -> t b d"), x[:, :, :]).then_inc(stored, 16)
            sp.wait_ge(stored, 16)

        @block.gpsimd
        def _(pool_eng):
            for t in tallies:
                pool.sem_inc(t.sem, t.credit)
            pool.sem_inc(credits_given, 1)
            pool.wait_ge(loaded["const"], 16 * 7)
            pool.wait_ge(loaded["ctx"], 32)
            for s in stages:
                enter(pool, s)
                if s in (0, 6, 7):
                    pool_attn128(s, {0: s0, 6: s6, 7: s7}[s])
                elif s in (1, 3):
                    pool_attn8(s, {1: s1, 3: s3}[s])
                elif s == 4:
                    pool_memory(s)
                elif s == 5:
                    pool_dequant()
                elif s == 10:
                    pool_feature_attn(s)

        @block.scalar
        def _(act_eng):
            act.wait_ge(credits_given, 1)
            for s in stages:
                enter(act, s)
                if s == 2:
                    act_slots_prepare()
                act_norm(s, natural if s == 10 else None)
                if s in (0, 6, 7):
                    act_attn128(s, {0: s0, 6: s6, 7: s7}[s])
                elif s in (1, 3):
                    act_attn8(s, {1: s1, 3: s3}[s])
                elif s == 2:
                    act_route(8)
                    act_slots()
                elif s == 4:
                    act_memory(s)
                elif s == 5:
                    act_ffn(s5)
                elif s == 8:
                    act.wait_ge(loaded["w8"], 16 * 5)
                    act_route(8)
                    act_ffn(s8)
                elif s == 9:
                    act_scan()
                elif s == 10:
                    act_feature_attn(s)
                elif s == 11:
                    act.wait_ge(aux2_ready.sem, aux2_ready.at(1))
                    act.activation(coef[:, :, 16:20], PJ[1][:, 0:B].unsqueeze(2).to_broadcast([P, B, 4]),
                                   ACT.Sigmoid).then_inc(aux6_ready.sem, 1)
                    act_route(16)
                    act_ffn(s11)

        @block.vector
        def _(dve_eng):
            dve.wait_ge(credits_given, 1)
            dve.wait_ge(loaded["const"], 16 * 7)
            dve.tensor_copy(ident16[:, :], ident[:, :]).then_inc(masks16_ready, 1)
            dve.tensor_copy(causal16[:, :], xn2[:, 0, 0:P]).then_inc(masks16_ready, 1)
            dve.wait_ge(loaded["x"], 16)
            for s in stages:
                enter(dve, s)
                if s == 1:
                    dve.wait_ge(loaded["w1"], 16 * 10)
                    dve.tensor_tensor(mask16[:, :, :], row_mask[:, :, :],
                                      pair_mask[:, :].unsqueeze(1).to_broadcast([P, B, P]),
                                      ALU.max).then_inc(dve_own, V.up())
                    dve.wait_ge(dve_own, V.now())
                    dve.tensor_scalar(mask16[:, :, :], mask16[:, :, :], NEG, None, ALU.mult).then_inc(aux2_ready.sem, 1)
                elif s == 2:
                    dve_slots_prepare()
                elif s == 4:
                    dve.wait_ge(loaded["w1"], 16 * (10 if 1 in stages else 2))
                    dve.tensor_scalar(mask16[:, :, :], row_mask[:, :, :], -NEG, NEG, ALU.mult,
                                      ALU.add).then_inc(aux2_ready.sem, 1)
                    dve.tensor_reduce(valid, row_mask[:, :, :], AX, ALU.max).then_inc(dve_own, V.up())
                elif s == 5:
                    for piece in range(4):
                        dve_dequant(0, 0, piece, first=True)
                elif s == 0:
                    dve.wait_ge(loaded["w0"], 16 * 8)
                elif s == 6:
                    dve.wait_ge(loaded["w6"], 16 * 6)
                dve_norm(s, natural if s == 10 else None)
                if s in (0, 6, 7):
                    dve_attn128(s, {0: s0, 6: s6, 7: s7}[s])
                    dve.wait_ge(out_done.sem, out_done.at(4 * B))
                elif s in (1, 3):
                    dve_attn8(s, {1: s1, 3: s3}[s])
                    dve.wait_ge(out_done.sem, out_done.at(B))
                elif s == 2:
                    dve_route(8, 2, clip=50.0)
                    dve_slots()
                    dve.wait_ge(out_done.sem, out_done.at(2 * B))
                elif s == 4:
                    dve_memory(s)
                    dve.wait_ge(out_done.sem, out_done.at(B))
                elif s == 5:
                    for h in range(2):
                        dve_ffn_half(s5, 0, h, lambda k: dve_dequant(0, 1, k, first=True))
                    with V.loop(3, 6) as i:
                        for h in range(2):
                            dve_ffn_half(s5, i * 2 + 1, h, lambda k: dve_dequant(i + 1, 0, k))
                        for h in range(2):
                            dve_ffn_half(s5, i * 2 + 2, h, lambda k: dve_dequant(i + 1, 1, k))
                    for h in range(2):
                        dve_ffn_half(s5, 7, h)
                    dve.wait_ge(acc_done.sem, acc_done.at(2 * s5.E))
                elif s == 8:
                    dve.wait_ge(loaded["w8"], 16 * 5)
                    dve_route(8, 2, bias=gateb8, alpha=alpha8)
                    dve.sem_inc(aux5_ready.sem, 1)
                    dve.wait_ge(aux6_ready.sem, aux6_ready.at(1))
                    for i in range(2):
                        dve.tensor_copy(coefT[:, i * 512:(i + 1) * 512], SC[i][0:8, :]).then_inc(dve_own, V.up())
                    dve.wait_ge(dve_own, V.now())
                    dve.sem_inc(slice_ready.sem, 1)
                    dve.wait_ge(out_ready.sem, out_ready.at(1))
                    for b in range(B):
                        bank = (ZP, OP, PJ[0], PJ[1])[b // 2]
                        dve.tensor_tensor(x[:, b, :], x[:, b, :], bank[:, (b % 2) * DM:(b % 2 + 1) * DM],
                                          ALU.add).then_inc(out_done.sem, 1)
                    dve.wait_ge(out_done.sem, out_done.at(B))
                    dve_ffn(s8)
                    dve.wait_ge(acc_done.sem, acc_done.at(2 * s8.E))
                elif s == 9:
                    dve_scan()
                    dve.wait_ge(out_done.sem, out_done.at(B))
                elif s == 10:
                    dve_feature_attn(s)
                    dve.wait_ge(out_done.sem, out_done.at(B))
                elif s == 11:
                    dve_route(16, 4, over_all=True)
                    dve.wait_ge(aux6_ready.sem, aux6_ready.at(1))
                    dve_ffn(s11)
                    dve.wait_ge(acc_done.sem, acc_done.at(2 * s11.E))
                dve.sem_inc(stage_done.sem, 1)

        @block.tensor
        def _(pe_eng):
            pe.wait_ge(credits_given, 1)
            pe.wait_ge(masks16_ready, 2)
            pe.wait_ge(loaded["const"], 16 * 7)
            pe.wait_ge(loaded["ctx"], 32)
            for s in stages:
                enter(pe, s)
                if s == 2:
                    pe.wait_ge(loaded["w2"], 16 * 7)
                    pe_slots_prepare()
                if s != 10:
                    pe_norm(s, 2 if s == 5 else 1)
                    pe.wait_ge(xnt_done.sem, xnt_done.at(B))
                if s in (0, 6, 7):
                    pe_attn128(s, {0: s0, 6: s6, 7: s7}[s])
                elif s in (1, 3):
                    if s == 1:
                        pe.wait_ge(aux2_ready.sem, aux2_ready.at(1))
                    pe_attn8(s, {1: s1, 3: s3}[s])
                elif s == 2:
                    pe_route(8, gatewT)
                    pe_slots()
                elif s == 4:
                    pe_memory(s)
                elif s == 5:
                    pe_ffn(s5)
                elif s == 8:
                    pe.wait_ge(loaded["w8"], 16 * 5)
                    pe_route(8, gatew8)
                    pe_coefT(8)
                    pe.wait_ge(slice_ready.sem, slice_ready.at(1))
                    for b in range(B):
                        bank = (ZP, OP, PJ[0], PJ[1])[b // 2]
                        last = pe.matmul(bank[:, (b % 2) * DM:(b % 2 + 1) * DM], coefT[:, b * P:(b + 1) * P], b2e,
                                         start=True, stop=True)
                    last.then_inc(out_ready.sem, 1)
                    pe.wait_ge(out_done.sem, out_done.at(B))
                    pe_ffn(s8)
                elif s == 9:
                    pe_scan()
                elif s == 10:
                    pe_feature_attn(s)
                elif s == 11:
                    pe.wait_ge(loaded["w11"], 32)
                    pe_route(16, gatew11, sgate11)
                    pe.wait_ge(aux3_ready.sem, aux3_ready.at(1))
                    pe.wait_ge(aux6_ready.sem, aux6_ready.at(1))
                    pe_ffn(s11)


def layouts(I):
    c = np.ascontiguousarray

    def kxn(w):
        return c(w.reshape(-1, P, w.shape[-1]).transpose(1, 0, 2))

    def col(v, n):
        return c(v.reshape(n, P).T)

    d = {"x": I["x"], "ctx": I["ctx_2048"], "ctxT": kxn(I["ctx_2048"].reshape(B * P, DM).T)}
    d["mask_pair"], d["mask_row"] = I["mask_SxS2_bc0"], I["mask_BxS2_bk0"]
    d["bqT"], d["bkT"] = c(I["L0_attn_b_Q"].T), c(I["L0_attn_b_K"].T)
    d["bv0"], d["bo0"] = I["L0_attn_b_V"].reshape(-1), I["L0_attn_b_O"]
    for n, k in (("wq0", "W_Q"), ("wk0", "W_K"), ("wv0", "W_V")):
        d[n] = kxn(I["L0_attn_" + k].transpose(1, 0, 2).reshape(DM, -1))
    d["wo0"] = c(I["L0_attn_W_O"].transpose(1, 0, 2))
    rep = np.arange(DM) // 32 * 8 + np.arange(DM) % 8
    for s, p in (("1", "L0_xattn_"), ("3", "L1_attn_")):
        d["wq" + s], d["wk" + s] = kxn(I[p + "Wq"].T), kxn(I[p + "Wk"][rep].T)
        d["wv" + s], d["wo" + s] = kxn(I[p + "Wv"].T), kxn(I[p + "Wo"].T)
    d["bq1"], d["bk1"] = col(I["L0_xattn_bq"], 2), col(I["L0_xattn_bk"][rep], 2)
    d["bv1"], d["bo1"] = I["L0_xattn_bv"], I["L0_xattn_bo"]
    d["WT"], d["atoms"], d["importance"] = kxn(I["L0_ffn_W"].T), I["L0_ffn_atoms"], I["L0_ffn_importance"]
    d["eaw"], d["gatew2"] = I["L0_ffn_expert_atom_weights"], kxn(I["L0_ffn_gate_w"].T)
    d["slot_cols"], d["slot_rows"] = I["L0_ffn_mask_idx"], col(I["L0_ffn_mask_idx"], 16)
    def tiles(gate, up, down):
        g, u = (w.reshape(8, DM, P).transpose(0, 2, 1) for w in (gate, up))
        return c(np.stack([g, u, down.reshape(DM, 8, P).transpose(1, 2, 0)], axis=2).reshape(8, P, 3 * DM))

    d["codes"] = tiles(*(I[f"L1_ffn_{k}_W_packed"] for k in ("gate", "up", "down")))
    d["scales"] = tiles(*(np.repeat(I[f"L1_ffn_{k}_scales"], 16, axis=1) for k in ("gate", "up", "down")))
    for n in "qkv":
        d[f"w{n}6"], d[f"w{n}7"] = kxn(I["L2_attn_w_" + n]), kxn(I["L2_xattn_W" + n])
    d["wo6"], d["wo7"] = kxn(I["L2_attn_w_o"]), kxn(I["L2_xattn_Wo"])
    d["fc1"] = c(I["L2_ffn_fc1_w"].reshape(8, DC, P, 1024).transpose(0, 2, 1, 3))
    d["fc2"] = c(I["L2_ffn_fc2_w"].reshape(8, 8, P, DM).transpose(0, 2, 1, 3))
    d["b1T"], d["b2e"] = col(I["L2_ffn_fc1_b"].reshape(-1), 64), I["L2_ffn_fc2_b"]
    d["gatew8"], d["gateb8"], d["alpha8"] = kxn(I["L2_ffn_gate_w"]), I["L2_ffn_gate_b"], I["L2_ffn_alpha"]
    wx = I["L3_attn_Wxproj"]
    d["wB9"], d["wC9"] = kxn(wx[0:64].T), kxn(wx[64:128].T)
    d["wD9"] = kxn(np.repeat(wx[128:129], 64, axis=0).T)
    d["wIn9"], d["wOut9"] = kxn(I["L3_attn_Winproj"].T), c(I["L3_attn_Woutproj"].T)
    d["cw9"] = c(I["L3_attn_conv_w"].reshape(DC, P, 4).transpose(1, 0, 2))
    d["cb9"], d["dskip9"] = col(I["L3_attn_conv_b"], 2), col(I["L3_attn_D"], 2)
    d["alog9"] = I["L3_attn_A_log"].reshape(64, 1)
    w13, w2 = I["L3_ffn_w13"], I["L3_ffn_w2"]
    sgu, sd = I["L3_ffn_shared_gate_up_w"], I["L3_ffn_shared_down_w"]
    sh13 = sgu.reshape(2, 4, 176, DM).transpose(1, 0, 2, 3).reshape(4, 352, DM)
    sh2 = sd.reshape(DM, 4, 176).transpose(1, 0, 2)
    w13, w2 = np.concatenate([w13, sh13]), np.concatenate([w2, sh2])
    d["w13"] = c(w13.reshape(20, 352, DC, P).transpose(0, 3, 2, 1))
    d["w2"] = c(w2.reshape(20, DM, 2, 88).transpose(0, 3, 2, 1))
    d["gatew11"], d["sgate11"] = kxn(I["L3_ffn_gate_w"].T), kxn(I["L3_ffn_sgate_w"].T)
    t = np.arange(P)
    d["ident"] = np.eye(P, dtype=np.float32)
    d["causal"] = np.where(t[None, :] <= t[:, None], 0.0, NEG).astype(np.float32)
    d["heads8"] = (t[:, None] // 8 == np.arange(16)).astype(np.float32)
    d["heads16"] = (t[:, None] // 16 == np.arange(8)).astype(np.float32)
    d["tri"] = np.tril(np.ones((16, 16), np.float32), -1)
    d["iotaf"] = np.arange(DM, dtype=np.float32)
    d["iotap"] = np.stack([t, t + P], 1).astype(np.float32)
    inv = 1.0 / np.float32(10000.0) ** (np.arange(0, P, 2, dtype=np.float32) / np.float32(P))
    ang = np.outer(np.arange(P, dtype=np.float32), inv).astype(np.float32)
    d["cosT"] = c(np.concatenate([np.cos(ang), np.cos(ang)], 1).T.astype(np.float32))
    d["sinT"] = c(np.concatenate([-np.sin(ang), np.sin(ang)], 1).T.astype(np.float32))
    return d


STAGES = tuple(range(12))


def kernel(**inputs):
    import concourse.bacc as bacc
    from concourse.bass_utils import run_bass_kernel_spmd

    nc = bacc.Bacc("TRN2", target_bir_lowering=False, num_devices=1)
    arrays = layouts({k: np.asarray(v) for k, v in inputs.items()})
    D = {n: nc.dram_tensor("in_" + n, a.shape, mybir.dt.from_np(a.dtype), kind="ExternalInput").ap()
         for n, a in arrays.items()}
    out = nc.dram_tensor("out", (B, P, DM), F32, kind="ExternalOutput").ap()
    build(nc, D, out, STAGES)
    got = run_bass_kernel_spmd(nc, [{"in_" + n: a for n, a in arrays.items()}], core_ids=[0])
    return got.results[0]["out"]
```

```python
from contextlib import ExitStack, contextmanager

import numpy as np

import concourse.bass as bass
from concourse import mybir

F32 = mybir.dt.float32
BF16 = mybir.dt.bfloat16
I32 = mybir.dt.int32
U8 = mybir.dt.uint8
ALU = mybir.AluOpType
ACT = mybir.ActivationFunctionType
AX = mybir.AxisListType.X

P = 128
B = 8
DM = 256
DC = DM // P
EPS = 1e-5
NEG = -1e30
BIG = 3e38


class Tally:

    def __init__(self, sem, credit):
        self.sem, self.credit, self.base = sem, credit, 0

    def at(self, steps):
        return steps + (self.credit + self.base)


class Own:

    def __init__(self, eng, sem):
        self.eng, self.sem, self.start, self.k = eng, sem, 0, 0

    def up(self):
        self.k += 1
        return 1

    def now(self):
        return self.start + self.k

    @contextmanager
    def loop(self, count, per):
        base = self.start + self.k
        with self.eng.Fori(0, count) as i:
            self.start, self.k = (i * per + base if per else base), 0
            yield i
            assert self.k == per, (self.eng, self.k, per)
        self.start, self.k = base + count * per, 0


class Attention:

    def __init__(self, w, nw, wq, wk, wv, wo, scale, bq=None, bk=None, bv=None, bo=None, cos=None, sin=None,
                 causal=False, cross=False, gqa=False, rope=False):
        self.w, self.nw = w, nw
        self.wq, self.wk, self.wv, self.wo = wq, wk, wv, wo
        self.bq, self.bk, self.bv, self.bo = bq, bk, bv, bo
        self.cos, self.sin, self.scale = cos, sin, scale
        self.causal, self.cross, self.gqa, self.rope = causal, cross, gqa, rope


class FeedForward:

    def __init__(self, E, nf, gated, func, up, down, arrived, load=None, bias=None, keep=False, coef_rows=None):
        self.E, self.nf, self.gated, self.func, self.keep, self.coef_rows = E, nf, gated, func, keep, coef_rows
        self.up, self.down, self.arrived, self.load, self.bias = up, down, arrived, load, bias


def build(nc, D, out, stages):
    ctx = ExitStack()
    with ctx:
        def sb(name, shape, dt=F32):
            return ctx.enter_context(nc.sbuf_tensor(name, shape, dt))

        def sem(name):
            return ctx.enter_context(nc.semaphore(name))

        x = sb("x", [P, B, DM])
        ctxn = sb("ctxn", [P, B, DM])
        ctxT = sb("ctxT", [P, DC, B * P])
        xnT = sb("xnT", [P, DC, B * P])
        arena_a = sb("arena_a", [P, 16384])
        arena_b = sb("arena_b", [P, 16384])
        work = sb("work", [P, 9216])
        xn2 = sb("xn2", [P, 2, DM])
        ident = sb("ident", [P, P])
        ident16 = sb("ident16", [P, P], BF16)
        causal16 = sb("causal16", [P, P], BF16)
        bn = sb("bn", [P, B, 6])
        stat = sb("stat", [P, 6, B])
        small = sb("small", [P, 1024])

        pair_mask = sb("pair_mask", [P, P], U8)
        row_mask = sb("row_mask", [P, B, P], U8)

        psum = [ctx.enter_context(nc.psum_tensor(f"bank{i}", [P, 512], F32)) for i in range(8)]

        tallies = []

        def tally(name, credit=1):
            tallies.append(Tally(sem(name), credit))
            return tallies[-1]

        var_ready = tally("var_ready")
        std_ready = tally("std_ready")
        xn_ready = tally("xn_ready")
        xnt_ready = tally("xnt_ready", 2)
        xnt_done = tally("xnt_done", 2)
        slice_ready = tally("slice_ready")
        proj_ready = tally("proj_ready")
        proj_done = tally("proj_done", 3)
        scores_ready = tally("scores_ready", 2)
        max_ready = tally("max_ready")
        exp_done = tally("exp_done", 2)
        recip_ready = tally("recip_ready")
        probs_ready = tally("probs_ready")
        probsT_ready = tally("probsT_ready")
        probsT_done = tally("probsT_done")
        mix_ready = tally("mix_ready")
        mix_done = tally("mix_done")
        out_ready = tally("out_ready")
        out_done = tally("out_done")
        kpad_ready = tally("kpad_ready")
        aux_ready = tally("aux_ready")
        aux_done = tally("aux_done")
        aux2_ready = tally("aux2_ready")
        aux3_ready = tally("aux3_ready")
        aux4_ready = tally("aux4_ready")
        aux5_ready = tally("aux5_ready")
        aux6_ready = tally("aux6_ready")
        up_ready = tally("up_ready")
        gate_ready = tally("gate_ready")
        hidden_done = tally("hidden_done", 2)
        acc_ready = tally("acc_ready")
        acc_done = tally("acc_done", 2)
        codes_ready = tally("codes_ready")
        scale_ready = tally("scale_ready")
        top_ready = tally("top_ready")
        sign_ready = tally("sign_ready")
        weights_ready = tally("weights_ready")
        stage_done = tally("stage_done")
        loaded = {s: sem(f"loaded_{s}") for s in
                  ("x", "const", "ctx", "w0", "w1", "w2", "w3", "w5a", "w5b", "w6", "w7", "w8", "w8a", "w8b", "w9", "w11", "w11a", "w11b")}
        stored = sem("stored")
        passed = sem("passed")
        masks16_ready = sem("masks16_ready")
        credits_given = sem("credits_given")
        dve_own, act_own, pool_own = sem("dve_own"), sem("act_own"), sem("pool_own")
        pe, act, dve, pool, sp = nc.tensor, nc.scalar, nc.vector, nc.gpsimd, nc.sync
        V, A, G = Own(dve, dve_own), Own(act, act_own), Own(pool, pool_own)

        def stand_alone(eng):
            eng.sem_inc(passed, 1)

        def rows_(v, off, k, n):
            return v[:, off:off + k * n].rearrange("p (k n) -> p k n", k=k)

        def dve_norm(s, natural=None):
            with V.loop(B, 1) as b:
                dve.bn_stats(bn[:, b, :], x[:, b, :]).then_inc(dve_own, V.up())
            dve.wait_ge(dve_own, V.now())
            mean, var, rstd, diff, sq, std = (stat[:, k, :] for k in range(6))
            dve.tensor_tensor(diff, bn[:, :, 1], bn[:, :, 4], ALU.subtract).then_inc(dve_own, V.up())
            dve.tensor_tensor(mean, bn[:, :, 1], bn[:, :, 4], ALU.add).then_inc(dve_own, V.up())
            dve.tensor_tensor(var, bn[:, :, 2], bn[:, :, 5], ALU.add).then_inc(dve_own, V.up())
            dve.wait_ge(dve_own, V.now())
            dve.tensor_tensor(sq, diff, diff, ALU.mult).then_inc(dve_own, V.up())
            dve.tensor_scalar(mean, mean, 0.5, None, ALU.mult).then_inc(dve_own, V.up())
            dve.tensor_scalar(var, var, 1.0 / DM, EPS, ALU.mult, ALU.add).then_inc(dve_own, V.up())
            dve.wait_ge(dve_own, V.now())
            dve.scalar_tensor_tensor(var, sq, 0.25, var, ALU.mult, ALU.add).then_inc(var_ready.sem, 1)
            dve.wait_ge(std_ready.sem, std_ready.at(1))
            dve.reciprocal(rstd, std).then_inc(dve_own, V.up())
            dve.wait_ge(dve_own, V.now())
            with V.loop(B // 2, 0) as i:
                for par in range(2):
                    b = i * 2 + par
                    if natural is None:
                        dve.wait_ge(xnt_ready.sem, xnt_ready.at(b - 1))
                        dst = xn2[:, par, :]
                    else:
                        dst = natural[:, b, :]
                    dve.tensor_scalar(dst, x[:, b, :], stat[:, 0, bass.ds(b, 1)], stat[:, 2, bass.ds(b, 1)],
                                      ALU.subtract, ALU.mult).then_inc(xn_ready.sem, 1)

        def act_norm(s, natural=None):
            act.wait_ge(var_ready.sem, var_ready.at(1))
            act.activation(stat[:, 5, :], stat[:, 1, :], ACT.Sqrt).then_inc(std_ready.sem, 1)
            if natural is None:
                with A.loop(B // 2, 0) as i:
                    for par in range(2):
                        b = i * 2 + par
                        act.wait_ge(xnt_ready.sem, xnt_ready.at(b + 1))
                        stand_alone(act)
                        act.activation(xnT[:, :, bass.ds(b * P, P)],
                                       psum[3 + par][:, 0:DM].rearrange("p (c t) -> p c t", c=DC),
                                       ACT.Copy).then_inc(xnt_done.sem, 1)

        def pe_norm(s, step=1):
            with pe.Fori(0, B // 2) as i:
                for par in range(2):
                    b = i * 2 + par
                    pe.wait_ge(xn_ready.sem, xn_ready.at(b + 1))
                    pe.wait_ge(xnt_done.sem, xnt_done.at(b - 1))
                    for c in range(DC):
                        rows = xn2[:, par, c::2] if step == 2 else xn2[:, par, c * P:(c + 1) * P]
                        last = pe.transpose(psum[3 + par][:, c * P:(c + 1) * P], rows, ident[:, :])
                    last.then_inc(xnt_ready.sem, 1)

        SC, TP, ZP, OP, PJ = psum[0:2], psum[2], psum[3], psum[4], psum[5:8]
        QG = work[:, 0:512].rearrange("p (j t) -> p j t", j=4)
        KG = work[:, 512:1024].rearrange("p (j t) -> p j t", j=4)
        VG = work[:, 1024:2048].rearrange("p (r n) -> p r n", r=2)
        PR = work[:, 2048:3072].rearrange("p (r n) -> p r n", r=2)
        PT = work[:, 3072:3584].rearrange("p (j t) -> p j t", j=4)
        ZS = work[:, 3584:4096]
        xb = work[:, 4096:4352].rearrange("p (c t) -> p c t", c=DC)
        cb = work[:, 4352:4608].rearrange("p (c t) -> p c t", c=DC)
        RT = [work[:, o:o + 512].rearrange("p (j t) -> p j t", j=4) for o in (4608, 6144)]
        KP = work[:, 5120:6144].rearrange("p (r n) -> p r n", r=2)
        nmax = small[:, 0:8].rearrange("p (r j) -> p r j", r=2)
        smax = small[:, 8:16].rearrange("p (r j) -> p r j", r=2)
        sums = small[:, 16:24].rearrange("p (r j) -> p r j", r=2)
        rsum = small[:, 24:32].rearrange("p (r j) -> p r j", r=2)

        def dve_max(u, r, nh, scale):
            dve.wait_ge(scores_ready.sem, scores_ready.at(u + 1))
            dve.tensor_reduce(nmax[:, r, 0:nh], SC[r][:, :].rearrange("p (j t) -> p j t", j=nh), AX, ALU.max,
                              negate=True).then_inc(dve_own, V.up())
            dve.wait_ge(dve_own, V.now())
            dve.tensor_scalar(smax[:, r, 0:nh], nmax[:, r, 0:nh], scale, None, ALU.mult).then_inc(max_ready.sem, 1)

        def act_exp(u, r, nh, scale, into=None):
            act.wait_ge(max_ready.sem, max_ready.at(u + 1))
            w = 512 // nh
            for j in range(nh):
                cols = slice(j * w, (j + 1) * w)
                last = act.activation(PR[:, r, cols], SC[r][:, cols], ACT.Exp, bias=smax[:, r, j:j + 1],
                                      scale=scale, accum_out=(sums[:, r, j:j + 1] if into is None else into[:, j:j + 1]))
            last.then_inc(exp_done.sem, 1)

        def dve_recip(u, r, nh):
            dve.wait_ge(exp_done.sem, exp_done.at(u + 1))
            dve.reciprocal(rsum[:, r, 0:nh], sums[:, r, 0:nh]).then_inc(recip_ready.sem, 1)

        def pool_normalise(u, r, nh):
            pool.wait_ge(recip_ready.sem, recip_ready.at(u + 1))
            w = 512 // nh
            probs = PR[:, r, :].rearrange("p (j t) -> p j t", j=nh)
            pool.tensor_tensor(probs, probs, rsum[:, r, 0:nh].unsqueeze(2).to_broadcast([P, nh, w]),
                               ALU.mult).then_inc(probs_ready.sem, 1)

        def pe_probsT(u, r):
            pe.wait_ge(probs_ready.sem, probs_ready.at(u + 1))
            pe.wait_ge(probsT_done.sem, probsT_done.at(u))
            for j in range(4):
                last = pe.transpose(TP[:, j * P:(j + 1) * P], PR[:, r, j * P:(j + 1) * P], ident[:, :])
            last.then_inc(probsT_ready.sem, 1)

        def dve_probsT(u):
            dve.wait_ge(probsT_ready.sem, probsT_ready.at(u + 1))
            dve.tensor_copy(work[:, 3072:3584], TP[:, :]).then_inc(probsT_done.sem, 1)

        def pe_attn128(s, c):
            src = cb if c.cross else xb

            def project(b, u, g, n):
                if n == 0 and g == 0:
                    pe.wait_ge(slice_ready.sem, slice_ready.at(b + 1))
                pe.wait_ge(proj_done.sem, proj_done.at(u * 3 + n - 2))
                w, v = (c.wk, src) if n else (c.wq, xb)
                for j in range(1 if n and c.gqa else 4):
                    h = g if n and c.gqa else 4 * g + j
                    for k in range(DC):
                        last = pe.matmul(PJ[n][:, j * P:(j + 1) * P], w[:, k, h * P:(h + 1) * P],
                                         v[:, k, :], start=(k == 0), stop=(k == DC - 1))
                last.then_inc(proj_ready.sem, 1)

            def values(u, g):
                pe.wait_ge(proj_done.sem, proj_done.at(u * 3))
                nv = P if c.gqa else 4 * P
                for k in range(DC):
                    last = pe.matmul(PJ[2][:, 0:nv], src[:, k, :], c.wv[:, k, g * nv:(g + 1) * nv],
                                     start=(k == 0), stop=(k == DC - 1))
                last.then_inc(proj_ready.sem, 1)

            def scores(u, g):
                pe.wait_ge(proj_done.sem, proj_done.at(u * 3 + 2))
                pe.wait_ge(exp_done.sem, exp_done.at(u - 1))
                if c.causal:
                    pe.matmul(SC[g % 2][:, :].rearrange("p (j t) -> p j t", j=4), ident16[:, :],
                              causal16[:, :].unsqueeze(1).to_broadcast([P, 4, P]), start=True, stop=False,
                              skip_group_check=True)
                for j in range(4):
                    last = pe.matmul(SC[g % 2][:, j * P:(j + 1) * P], QG[:, j, :], KG[:, 0 if c.gqa else j, :],
                                     start=not c.causal, stop=True, skip_group_check=True)
                last.then_inc(scores_ready.sem, 1)

            def step(b, g, last_unit=False):
                u, nxt = b * 4 + g, (g + 1) % 4
                if not last_unit:
                    project(b + 1, u + 1, nxt, 0)
                    project(b + 1, u + 1, nxt, 1)
                pe_probsT(u, g % 2)
                if not last_unit:
                    values(u + 1, nxt)
                pe.wait_ge(proj_done.sem, proj_done.at(u * 3 + 3))
                pe.wait_ge(probsT_done.sem, probsT_done.at(u + 1))
                pe.wait_ge(mix_done.sem, mix_done.at(u))
                for j in range(4):
                    vals = VG[:, g % 2, 0:P] if c.gqa else VG[:, g % 2, j * P:(j + 1) * P]
                    last = pe.matmul(ZP[:, j * P:(j + 1) * P], vals, PT[:, j, :], start=True, stop=True)
                last.then_inc(mix_ready.sem, 1)
                if not last_unit:
                    scores(u + 1, nxt)
                pe.wait_ge(mix_done.sem, mix_done.at(u + 1))
                pe.wait_ge(out_done.sem, out_done.at(u))
                for j in range(4):
                    last = pe.matmul(OP[:, 0:DM], ZS[:, j * P:(j + 1) * P], c.wo[:, 4 * g + j, :],
                                     start=(j == 0), stop=(j == 3))
                last.then_inc(out_ready.sem, 1)

            pe.wait_ge(loaded[c.w], 16 * c.nw)
            project(0, 0, 0, 0)
            project(0, 0, 0, 1)
            values(0, 0)
            scores(0, 0)
            with pe.Fori(0, B - 1) as b:
                for g in range(4):
                    step(b, g)
            for g in range(4):
                step(B - 1, g, last_unit=(g == 3))

        def dve_attn128(s, c):
            if c.bo is not None:
                dve.wait_ge(xn_ready.sem, xn_ready.at(B))
                dve.tensor_tensor(x[:, :, :], x[:, :, :], c.bo.unsqueeze(1).to_broadcast([P, B, DM]),
                                  ALU.add).then_inc(dve_own, V.up())
                dve.wait_ge(dve_own, V.now())

            def qk(n):
                return (QG, c.bq, 4) if n == 0 else (KG, c.bk, 1 if c.gqa else 4)

            def copy_qk(u, g, n):
                dst, bias, nj = qk(n)
                dve.wait_ge(proj_ready.sem, proj_ready.at(u * 3 + n + 1))
                bank = PJ[n][:, 0:nj * P].rearrange("p (j t) -> p j t", j=nj)
                if c.rope:
                    dve.wait_ge(scores_ready.sem, scores_ready.at(u))
                    dve.wait_ge(aux2_ready.sem, aux2_ready.at(u * 2 + n + 1))
                    dve.tensor_tensor(dst[:, 0:nj, :], bank, c.cos.unsqueeze(1).to_broadcast([P, nj, P]),
                                      ALU.mult).then_inc(dve_own, V.up())
                elif bias is None:
                    dve.tensor_copy(dst[:, 0:nj, :], bank).then_inc(proj_done.sem, 1)
                else:
                    dve.tensor_tensor(dst[:, 0:nj, :], bank,
                                      bias[:, 4 * g:4 * g + 4].unsqueeze(2).to_broadcast([P, 4, P]),
                                      ALU.add).then_inc(proj_done.sem, 1)

            def add_rotated(u):
                dve.wait_ge(dve_own, V.now())
                for n in range(2):
                    dst, _, nj = qk(n)
                    dve.wait_ge(aux_ready.sem, aux_ready.at(u * 2 + n + 1))
                    dve.tensor_tensor(dst[:, 0:nj, :], dst[:, 0:nj, :], RT[n][:, 0:nj, :],
                                      ALU.add).then_inc(proj_done.sem, 1)

            def copy_values(u, g):
                dve.wait_ge(proj_ready.sem, proj_ready.at(u * 3 + 3))
                nv = P if c.gqa else 4 * P
                bank = PJ[2][:, 0:nv]
                if c.bv is None:
                    dve.tensor_copy(VG[:, g % 2, 0:nv], bank).then_inc(proj_done.sem, 1)
                else:
                    dve.tensor_tensor(VG[:, g % 2, :], bank, c.bv[:, g * nv:(g + 1) * nv],
                                      ALU.add).then_inc(proj_done.sem, 1)

            def step(b, g, last_unit=False):
                u, nxt = b * 4 + g, (g + 1) % 4
                if not last_unit:
                    copy_qk(u + 1, nxt, 0)
                    copy_qk(u + 1, nxt, 1)
                dve_probsT(u)
                if not last_unit:
                    if c.rope:
                        add_rotated(u + 1)
                    copy_values(u + 1, nxt)
                    dve_max(u + 1, nxt % 2, 4, c.scale)
                    dve_recip(u + 1, nxt % 2, 4)
                dve.wait_ge(out_ready.sem, out_ready.at(u + 1))
                dve.tensor_tensor(x[:, b, :], x[:, b, :], OP[:, 0:DM], ALU.add).then_inc(out_done.sem, 1)

            copy_qk(0, 0, 0)
            copy_qk(0, 0, 1)
            if c.rope:
                add_rotated(0)
            copy_values(0, 0)
            dve_max(0, 0, 4, c.scale)
            dve_recip(0, 0, 4)
            with V.loop(B - 1, 4 + (8 if c.rope else 0)) as b:
                for g in range(4):
                    step(b, g)
            for g in range(4):
                step(B - 1, g, last_unit=(g == 3))

        def act_attn128(s, c):
            def rotate(u, g):
                for n, nj in ((0, 4), (1, 1)):
                    act.wait_ge(proj_ready.sem, proj_ready.at(u * 3 + n + 1))
                    act.wait_ge(proj_done.sem, proj_done.at(u * 3 + n - 2))
                    act.activation(RT[n][0:64, 0:nj, :], PJ[n][64:128, 0:nj * P].rearrange("p (j t) -> p j t", j=nj),
                                   ACT.Copy)
                    act.activation(RT[n][64:128, 0:nj, :], PJ[n][0:64, 0:nj * P].rearrange("p (j t) -> p j t", j=nj),
                                   ACT.Copy).then_inc(aux2_ready.sem, 1)

            def step(b, g, last_unit=False):
                u, nxt = b * 4 + g, (g + 1) % 4
                if c.rope and not last_unit:
                    rotate(u + 1, nxt)
                act.wait_ge(mix_ready.sem, mix_ready.at(u + 1))
                act.activation(ZS, ZP[:, :], ACT.Copy).then_inc(mix_done.sem, 1)
                if not last_unit:
                    act_exp(u + 1, nxt % 2, 4, c.scale)

            if c.rope:
                rotate(0, 0)
            act_exp(0, 0, 4, c.scale)
            with A.loop(B - 1, 0) as b:
                for g in range(4):
                    step(b, g)
            for g in range(4):
                step(B - 1, g, last_unit=(g == 3))

        def pool_attn128(s, c):
            def slices(b):
                if c.cross:
                    pool.tensor_copy(cb, ctxT[:, :, bass.ds(b * P, P)]).then_inc(pool_own, G.up())
                    pool.wait_ge(pool_own, G.now())
                pool.tensor_copy(xb, xnT[:, :, bass.ds(b * P, P)]).then_inc(slice_ready.sem, 1)

            def times_sines(u):
                for n, nj in ((0, 4), (1, 1)):
                    pool.wait_ge(aux2_ready.sem, aux2_ready.at(u * 2 + n + 1))
                    pool.tensor_tensor(RT[n][:, 0:nj, :], RT[n][:, 0:nj, :], c.sin.unsqueeze(1).to_broadcast([P, nj, P]),
                                       ALU.mult).then_inc(aux_ready.sem, 1)

            pool.wait_ge(xnt_done.sem, xnt_done.at(B))
            slices(0)
            if c.rope:
                times_sines(0)
            pool_normalise(0, 0, 4)
            with G.loop(B - 1, 1 if c.cross else 0) as b:
                for g in range(4):
                    if c.rope:
                        times_sines(b * 4 + g + 1)
                    if g == 2:
                        pool.wait_ge(proj_ready.sem, proj_ready.at(b * 12 + 12))
                        slices(b + 1)
                    pool_normalise(b * 4 + g + 1, (g + 1) % 2, 4)
            for g in range(1, 4):
                if c.rope:
                    times_sines((B - 1) * 4 + g)
                pool_normalise((B - 1) * 4 + g, g % 2, 4)

        QB = work[:, 6656:6912].rearrange("p (c t) -> p c t", c=2)
        KB = work[:, 6912:7168].rearrange("p (c t) -> p c t", c=2)
        VB = work[:, 7168:7232]
        ZB = work[:, 7232:7488]
        ZT = work[:, 7488:7744].rearrange("p (c t) -> p c t", c=2)
        PT2 = [work[:, o:o + 512].rearrange("p (j t) -> p j t", j=4) for o in (3072, 7744)]
        heads8 = sb("heads8", [P, 16])
        heads16 = sb("heads16", [P, 8])
        mask16 = sb("mask16", [P, B, P], BF16)
        sums32 = work[:, 8256:8288]
        rsum32 = work[:, 8288:8320]
        natural = xnT[:, :, :].rearrange("p c n -> p (c n)").rearrange("p (b d) -> p b d", b=B)
        xs = QB.rearrange("p c t -> p (c t)")

        def pe_small(s, c):
            def project(b):
                pe.wait_ge(slice_ready.sem, slice_ready.at(b + 1))
                if c is None:
                    return
                src = cb if c.cross else xb
                pe.wait_ge(proj_done.sem, proj_done.at(b * 3 - 1))
                for n, (w, v) in enumerate(((c.wq, xb), (c.wk, src))):
                    for m in range(2):
                        for k in range(DC):
                            last = pe.matmul(PJ[0][:, (2 * n + m) * P:(2 * n + m + 1) * P],
                                             w[:, k, m * P:(m + 1) * P], v[:, k, :],
                                             start=(k == 0), stop=(k == DC - 1))
                last.then_inc(proj_ready.sem, 1)
                pe.wait_ge(proj_done.sem, proj_done.at(b * 3))
                for k in range(DC):
                    last = pe.matmul(PJ[1][:, 0:64], src[:, k, :], c.wv[:, k, :], start=(k == 0), stop=(k == DC - 1))
                last.then_inc(proj_ready.sem, 1)

            def scores(b, g):
                u = b * 8 + g
                if c is not None:
                    pe.wait_ge(proj_done.sem, proj_done.at(b * 3 + 2))
                pe.wait_ge(kpad_ready.sem, kpad_ready.at(u + 1))
                pe.wait_ge(exp_done.sem, exp_done.at(u - 1))
                if c is None:
                    for m in range(2):
                        last = pe.matmul(SC[g % 2][:, m * DM:(m + 1) * DM], xs[:, m * P:(m + 1) * P],
                                         KP[:, g % 2, 0:DM], start=True, stop=True)
                    last.then_inc(scores_ready.sem, 1)
                    return
                mask = causal16[:, :].unsqueeze(1) if c.causal else mask16[:, bass.ds(b, 1), :]
                pe.matmul(SC[g % 2][:, :].rearrange("p (j t) -> p j t", j=4), ident16[:, :],
                          mask.to_broadcast([P, 4, P]), start=True, stop=False)
                pe.matmul(SC[g % 2][:, :], QB[:, g // 4, :], KP[:, g % 2, :],
                          start=False, stop=True).then_inc(scores_ready.sem, 1)

            def transposed(u, g):
                pe.wait_ge(exp_done.sem, exp_done.at(u + 1))
                pe.wait_ge(probsT_done.sem, probsT_done.at(u))
                for j in range(4):
                    last = pe.transpose(TP[:, j * P:(j + 1) * P], PR[:, g % 2, j * P:(j + 1) * P], ident[:, :])
                last.then_inc(probsT_ready.sem, 1)

            def mix(b, g):
                u = b * 8 + g
                pe.wait_ge(probsT_done.sem, probsT_done.at(u + 1))
                if g == 0:
                    pe.wait_ge(mix_done.sem, mix_done.at(b))
                    if c is not None:
                        pe.wait_ge(proj_done.sem, proj_done.at(b * 3 + 3))
                for j in range(4):
                    if c is None:
                        m, k = j // 2, j % 2
                        last = pe.matmul(ZP[:, m * P + 16 * g:m * P + 16 * g + 16], PT2[g % 2][:, j, :],
                                         ctxT[:, k, bass.ds(b * P + 16 * g, 16)], start=(k == 0), stop=(k == 1))
                    else:
                        h = 4 * g + j
                        last = pe.matmul(ZP[:, h * 8:h * 8 + 8], PT2[g % 2][:, j, :], VB[:, g * 8:g * 8 + 8],
                                         start=True, stop=True)
                last.then_inc(mix_ready.sem, 1)

            def result_transposed(b):
                pe.wait_ge(mix_done.sem, mix_done.at(b + 1))
                if c is None:
                    pe.wait_ge(out_done.sem, out_done.at(b))
                else:
                    pe.wait_ge(aux_done.sem, aux_done.at(b))
                for k in range(2):
                    last = pe.transpose(OP[:, k * P:(k + 1) * P], ZB[:, k * P:(k + 1) * P], ident[:, :])
                last.then_inc(out_ready.sem if c is None else aux_ready.sem, 1)

            def output(b):
                if c is None:
                    return
                pe.wait_ge(aux_done.sem, aux_done.at(b + 1))
                pe.wait_ge(out_done.sem, out_done.at(b))
                for k in range(2):
                    last = pe.matmul(PJ[2][:, 0:DM], ZT[:, k, :], c.wo[:, k, :], start=(k == 0), stop=(k == 1))
                last.then_inc(out_ready.sem, 1)

            def earlier(b, g, n):
                return (b, g - n) if g >= n else (b - 1, g + 8 - n)

            def body(b, first=False):
                project(b)
                for g in range(8):
                    if not first or g >= 2:
                        transposed(b * 8 + g - 2, g)
                    if not first or g >= 3:
                        mix(*earlier(b, g, 3))
                    if not first and g == 3:
                        result_transposed(b - 1)
                    if not first and g == 4:
                        output(b - 1)
                    scores(b, g)

            if c is not None:
                pe.wait_ge(loaded[c.w], 16 * c.nw)
            body(0, first=True)
            with pe.Fori(0, B - 1) as i:
                body(i + 1)
            last_seq = B - 1
            transposed(last_seq * 8 + 6, 6)
            mix(last_seq, 5)
            transposed(last_seq * 8 + 7, 7)
            mix(last_seq, 6)
            mix(last_seq, 7)
            result_transposed(last_seq)
            output(last_seq)

        def dve_small(s, c):
            nh = 2 if c is None else 4
            scale = 0.25 if c is None else c.scale
            dve.wait_ge(xn_ready.sem, xn_ready.at(B))
            if c is not None and c.bo is not None:
                dve.tensor_tensor(x[:, :, :], x[:, :, :], c.bo.unsqueeze(1).to_broadcast([P, B, DM]),
                                  ALU.add).then_inc(dve_own, V.up())
                dve.wait_ge(dve_own, V.now())

            def copy_qk(b):
                dve.wait_ge(proj_ready.sem, proj_ready.at(b * 2 + 1))
                for n, (dst, bias) in enumerate(((QB, c.bq), (KB, c.bk))):
                    bank = PJ[0][:, 2 * n * P:2 * (n + 1) * P].rearrange("p (c t) -> p c t", c=2)
                    if bias is None:
                        dve.tensor_copy(dst, bank).then_inc(proj_done.sem, 1)
                    else:
                        dve.tensor_tensor(dst, bank, bias.unsqueeze(2).to_broadcast([P, 2, P]),
                                          ALU.add).then_inc(proj_done.sem, 1)

            def copy_values(b):
                dve.wait_ge(proj_ready.sem, proj_ready.at(b * 2 + 2))
                if c.bv is None:
                    dve.tensor_copy(VB, PJ[1][:, 0:64]).then_inc(proj_done.sem, 1)
                else:
                    dve.tensor_tensor(VB, PJ[1][:, 0:64], c.bv, ALU.add).then_inc(proj_done.sem, 1)

            def copy_transposed(u, g):
                dve.wait_ge(probsT_ready.sem, probsT_ready.at(u + 1))
                dve.tensor_copy(PT2[g % 2].rearrange("p j t -> p (j t)"), TP[:, :]).then_inc(probsT_done.sem, 1)

            def invert_sums(b):
                dve.wait_ge(exp_done.sem, exp_done.at(b * 8 + 8))
                dve.reciprocal(rsum32[:, 0:8 * nh], sums32[:, 0:8 * nh]).then_inc(dve_own, V.up())

            def divide(b):
                dve.wait_ge(mix_ready.sem, mix_ready.at(b * 8 + 8))
                dve.wait_ge(dve_own, V.now())
                if c is None:
                    view = "p (m h n) -> p m h n"
                    dve.tensor_tensor(ZB.rearrange(view, m=2, h=8), ZP[:, 0:DM].rearrange(view, m=2, h=8),
                                      rsum32[:, 0:16].rearrange("p (h m) -> p m h", m=2).unsqueeze(3)
                                      .to_broadcast([P, 2, 8, 16]), ALU.mult).then_inc(mix_done.sem, 1)
                else:
                    view = "p (h n) -> p h n"
                    dve.tensor_tensor(ZB.rearrange(view, h=32), ZP[:, 0:DM].rearrange(view, h=32),
                                      rsum32.unsqueeze(2).to_broadcast([P, 32, 8]), ALU.mult).then_inc(mix_done.sem, 1)

            def copy_result(b):
                if c is not None:
                    dve.wait_ge(aux_ready.sem, aux_ready.at(b + 1))
                    dve.tensor_copy(ZT, OP[:, 0:DM].rearrange("p (c t) -> p c t", c=2)).then_inc(aux_done.sem, 1)

            def add_out(b):
                dve.wait_ge(out_ready.sem, out_ready.at(b + 1))
                dve.tensor_tensor(x[:, b, :], x[:, b, :], (OP if c is None else PJ[2])[:, 0:DM],
                                  ALU.add).then_inc(out_done.sem, 1)

            def body(b, first=False):
                if c is not None:
                    copy_qk(b)
                if not first:
                    invert_sums(b - 1)
                for g in range(8):
                    if not first or g >= 2:
                        copy_transposed(b * 8 + g - 2, g)
                    if not first and g == 2:
                        divide(b - 1)
                    if c is not None and g == 2:
                        copy_values(b)
                    if not first and g == 3:
                        copy_result(b - 1)
                    if not first and g == 4:
                        add_out(b - 1)
                    dve_max(b * 8 + g, g % 2, nh, scale)

            body(0, first=True)
            with V.loop(B - 1, 9) as i:
                body(i + 1)
            last_seq = B - 1
            copy_transposed(last_seq * 8 + 6, 6)
            copy_transposed(last_seq * 8 + 7, 7)
            invert_sums(last_seq)
            divide(last_seq)
            copy_result(last_seq)
            add_out(last_seq)

        def act_small(s, c):
            nh = 2 if c is None else 4
            with A.loop(B, 0) as b:
                for g in range(8):
                    act_exp(b * 8 + g, g % 2, nh, 0.25 if c is None else c.scale, sums32[:, g * nh:(g + 1) * nh])

        def pool_small(s, c):
            def slices(b):
                if c is None:
                    pool.tensor_copy(xs, natural[:, b, :]).then_inc(slice_ready.sem, 1)
                    return
                if c.cross:
                    pool.tensor_copy(cb, ctxT[:, :, bass.ds(b * P, P)]).then_inc(pool_own, G.up())
                    pool.wait_ge(pool_own, G.now())
                pool.tensor_copy(xb, xnT[:, :, bass.ds(b * P, P)]).then_inc(slice_ready.sem, 1)

            def kpad(b, g):
                if c is not None and g == 0:
                    pool.wait_ge(proj_done.sem, proj_done.at(b * 3 + 2))
                pool.wait_ge(scores_ready.sem, scores_ready.at(b * 8 + g - 1))
                if c is None:
                    stand_alone(pool)
                    pool.tensor_tensor(KP[:, g % 2, 0:DM], ctxn[:, b, :], heads16[:, g:g + 1].to_broadcast([P, DM]),
                                       ALU.mult).then_inc(kpad_ready.sem, 1)
                else:
                    pool.tensor_tensor(KP[:, g % 2, :].rearrange("p (j t) -> p j t", j=4),
                                       KB[:, g // 4, :].unsqueeze(1).to_broadcast([P, 4, P]),
                                       heads8[:, 4 * (g % 4):4 * (g % 4) + 4].unsqueeze(2).to_broadcast([P, 4, P]),
                                       ALU.mult).then_inc(kpad_ready.sem, 1)

            if c is None:
                pool.wait_ge(xn_ready.sem, xn_ready.at(B))
            else:
                pool.wait_ge(xnt_done.sem, xnt_done.at(B))
            slices(0)
            with G.loop(B - 1, 1 if c is not None and c.cross else 0) as b:
                for g in range(8):
                    kpad(b, g)
                    if g == 5 and c is not None:
                        pool.wait_ge(proj_ready.sem, proj_ready.at(b * 2 + 2))
                        slices(b + 1)
                if c is None:
                    pool.wait_ge(scores_ready.sem, scores_ready.at(b * 8 + 8))
                    slices(b + 1)
            for g in range(8):
                kpad(B - 1, g)

        valid = small[:, 64:72]

        def pe_memory(s):
            pe.wait_ge(aux2_ready.sem, aux2_ready.at(1))
            for u in range(2):
                for j in range(4):
                    b = 4 * u + j
                    for k in range(DC):
                        pe.matmul(SC[u][:, j * P:(j + 1) * P], xnT[:, k, b * P:(b + 1) * P],
                                  ctxT[:, k, b * P:(b + 1) * P], start=(k == 0), stop=False)
                    last = pe.matmul(SC[u][:, j * P:(j + 1) * P], ident16[:, :], mask16[:, b, :],
                                     start=False, stop=True)
                last.then_inc(scores_ready.sem, 1)
            for u in range(2):
                pe_probsT(u, u)
                pe.wait_ge(probsT_done.sem, probsT_done.at(u + 1))
                for half in range(2):
                    bank = (ZP, OP, PJ[0], PJ[1])[2 * u + half]
                    for j in range(2):
                        b = 4 * u + 2 * half + j
                        last = pe.matmul(bank[:, j * DM:(j + 1) * DM], PT[:, 2 * half + j, :], ctxn[:, b, :],
                                         start=True, stop=True)
                last.then_inc(out_ready.sem, 1)

        def dve_memory(s):
            for u in range(2):
                dve_max(u, u, 4, DM ** -0.5)
            for u in range(2):
                dve_recip(u, u, 4)
            for u in range(2):
                dve_probsT(u)
            for u in range(2):
                dve.wait_ge(out_ready.sem, out_ready.at(u + 1))
                for half in range(2):
                    bank = (ZP, OP, PJ[0], PJ[1])[2 * u + half]
                    for j in range(2):
                        b = 4 * u + 2 * half + j
                        dve.scalar_tensor_tensor(x[:, b, :], bank[:, j * DM:(j + 1) * DM], valid[:, b:b + 1],
                                                 x[:, b, :], ALU.mult, ALU.add).then_inc(out_done.sem, 1)

        def act_memory(s):
            for u in range(2):
                act_exp(u, u, 4, DM ** -0.5)

        def pool_memory(s):
            for u in range(2):
                pool_normalise(u, u, 4)

        lg = work[:, 7296:7424].rearrange("p (b e) -> p b e", b=B)
        coef = small[:, 96:256].rearrange("p (b e) -> p b e", b=B)
        tri = rows_(arena_b, 15360, 16, 16)
        pair = work[:, 0:2048]
        tied = work[:, 2048:4096]
        rank = work[:, 7424:7552].rearrange("p (b e) -> p b e", b=B)
        peak = small[:, 72:80]
        denom = small[:, 80:88]

        def pe_route(E, w, sgate=None):
            for b in range(B):
                for k in range(DC):
                    last = pe.matmul(PJ[0][:, b * E:(b + 1) * E], xnT[:, k, b * P:(b + 1) * P], w[:, k, :],
                                     start=(k == 0), stop=(k == DC - 1))
            if sgate is not None:
                for b in range(B):
                    for k in range(DC):
                        last = pe.matmul(PJ[1][:, b:b + 1], xnT[:, k, b * P:(b + 1) * P], sgate[:, k, :],
                                         start=(k == 0), stop=(k == DC - 1))
            last.then_inc(aux2_ready.sem, 1)

        def dve_route(E, k, clip=None, bias=None, alpha=None, over_all=False):
            dve.wait_ge(aux2_ready.sem, aux2_ready.at(1))
            L = lg[:, :, 0:E]
            bank = PJ[0][:, 0:B * E].rearrange("p (b e) -> p b e", b=B)
            if clip is not None:
                dve.tensor_scalar(L, bank, clip, -clip, ALU.min, ALU.max).then_inc(dve_own, V.up())
            elif bias is not None:
                dve.tensor_tensor(L, bank, bias.unsqueeze(1).to_broadcast([P, B, E]), ALU.add).then_inc(dve_own, V.up())
            else:
                dve.tensor_copy(L, bank).then_inc(dve_own, V.up())
            dve.wait_ge(dve_own, V.now())
            four = [P, B, E, E]
            pairs, ties = (t[:, 0:B * E * E].rearrange("p (b e j) -> p b e j", b=B, e=E) for t in (pair, tied))
            other, own = L.unsqueeze(2).to_broadcast(four), L.unsqueeze(3).to_broadcast(four)
            flat = [t[:, 0:B * E * E] for t in (pair, tied)]
            dve.tensor_tensor(pairs, other, own, ALU.is_gt).then_inc(dve_own, V.up())
            dve.tensor_tensor(ties, other, own, ALU.is_equal).then_inc(dve_own, V.up())
            dve.tensor_reduce(peak, L, AX, ALU.max).then_inc(dve_own, V.up())
            dve.wait_ge(dve_own, V.now())
            dve.tensor_tensor(ties, ties, tri[:, 0:E, 0:E].unsqueeze(1).to_broadcast(four),
                              ALU.mult).then_inc(dve_own, V.up())
            dve.tensor_tensor(L, L, peak.unsqueeze(2).to_broadcast([P, B, E]), ALU.subtract).then_inc(aux3_ready.sem, 1)
            dve.wait_ge(dve_own, V.now())
            dve.tensor_tensor(flat[0], flat[0], flat[1], ALU.add).then_inc(dve_own, V.up())
            dve.wait_ge(dve_own, V.now())
            R = rank[:, :, 0:E]
            dve.tensor_reduce(R, pairs, AX, ALU.add).then_inc(dve_own, V.up())
            dve.wait_ge(dve_own, V.now())
            dve.tensor_scalar(R, R, float(k), None, ALU.is_lt).then_inc(dve_own, V.up())
            dve.wait_ge(aux4_ready.sem, aux4_ready.at(1))
            if over_all:
                dve.tensor_reduce(denom, L, AX, ALU.add).then_inc(dve_own, V.up())
            dve.wait_ge(dve_own, V.now())
            C = coef[:, :, 0:E]
            dve.tensor_tensor(C, L, R, ALU.mult).then_inc(dve_own, V.up())
            dve.wait_ge(dve_own, V.now())
            if not over_all:
                dve.tensor_reduce(denom, C, AX, ALU.add).then_inc(dve_own, V.up())
                dve.wait_ge(dve_own, V.now())
            dve.reciprocal(denom, denom).then_inc(dve_own, V.up())
            dve.wait_ge(dve_own, V.now())
            dve.tensor_tensor(C, C, denom.unsqueeze(2).to_broadcast([P, B, E]), ALU.mult).then_inc(dve_own, V.up())
            dve.wait_ge(dve_own, V.now())
            if alpha is not None:
                dve.tensor_tensor(C, C, alpha.unsqueeze(1).to_broadcast([P, B, E]), ALU.mult).then_inc(dve_own, V.up())
                dve.wait_ge(dve_own, V.now())

        def act_route(E):
            act.wait_ge(aux3_ready.sem, aux3_ready.at(1))
            act.activation(lg[:, :, 0:E], lg[:, :, 0:E], ACT.Exp).then_inc(aux4_ready.sem, 1)

        coefT = work[0:B, 8192:9216]

        def pe_coefT(E):
            pe.wait_ge(aux5_ready.sem, aux5_ready.at(1))
            for b in range(B):
                last = pe.transpose(SC[b // 4][0:E, (b % 4) * P:(b % 4 + 1) * P], coef[:, b, 0:E], ident[:, :])
            last.then_inc(aux6_ready.sem, 1)

        NS = 2048
        gatewT = rows_(arena_b, 14848, 2, 8)
        WT = rows_(arena_b, 2048, 2, DM)
        atoms = arena_b[0:64, 2560:4608]
        slots = arena_b[0:8, 4608:6656]
        gather = rows_(arena_b, 6656, 2, NS)
        scatter = rows_(arena_b, 10752, 16, DM)
        eaw = arena_b[0:8, 14864:14928]
        eawT = arena_b[0:64, 14928:14936]
        colsi = work[:, 0:2048].bitcast(I32)
        colsf = work[:, 2048:4096]
        rowsi = small[:, 512:528].bitcast(I32)
        rowsf = small[:, 528:544]
        iotaf = arena_b[:, 15104:15360]
        iotap = sb("iotap", [P, 2])
        em = small[0:8, 88:92]
        xv = work[:, 4096:5120].rearrange("p (r n) -> p r n", r=2)
        xg = work[:, 5120:6144].rearrange("p (r n) -> p r n", r=2)

        def dve_slots_prepare():
            dve.wait_ge(loaded["w2"], 16 * 7)
            dve.tensor_reduce(em[:, 0:1], eaw, AX, ALU.max, negate=True).then_inc(aux_ready.sem, 1)
            dve.tensor_scalar(rowsi, rowsi, 8, None, ALU.arith_shift_right).then_inc(dve_own, V.up())
            dve.tensor_scalar(colsi, colsi, DM - 1, None, ALU.bitwise_and).then_inc(dve_own, V.up())
            dve.wait_ge(dve_own, V.now())
            dve.tensor_copy(rowsf, rowsi).then_inc(dve_own, V.up())
            dve.tensor_copy(colsf, colsi).then_inc(dve_own, V.up())
            dve.wait_ge(dve_own, V.now())
            for k in range(DC):
                dve.tensor_scalar(gather[:, k, :], colsf, iotap[:, k:k + 1], None,
                                  ALU.is_equal).then_inc(dve_own, V.up())
            with V.loop(NS // P, 1) as i:
                dve.tensor_scalar(scatter[:, i, :], iotaf[:, :], rowsf[:, bass.ds(i, 1)], None,
                                  ALU.is_equal).then_inc(dve_own, V.up())
            dve.wait_ge(aux_done.sem, aux_done.at(1))
            dve.reciprocal(em[:, 2:3], em[:, 1:2]).then_inc(dve_own, V.up())
            dve.wait_ge(dve_own, V.now())
            dve.tensor_scalar(eaw, eaw, em[:, 2:3], None, ALU.mult).then_inc(slice_ready.sem, 1)
            dve.wait_ge(proj_ready.sem, proj_ready.at(1))
            dve.tensor_copy(eawT, TP[0:64, 0:8]).then_inc(slice_ready.sem, 1)
            dve.wait_ge(aux_done.sem, aux_done.at(2))
            for i in range(4):
                dve.wait_ge(proj_ready.sem, proj_ready.at(i + 2))
                dve.tensor_tensor(slots[:, i * 512:(i + 1) * 512], (SC[0], SC[1], TP, ZP)[i][0:8, :],
                                  slots[:, i * 512:(i + 1) * 512], ALU.mult).then_inc(proj_done.sem, 1)

        def act_slots_prepare():
            act.wait_ge(aux_ready.sem, aux_ready.at(1))
            act.activation(eaw, eaw, ACT.Exp, bias=em[:, 0:1], accum_out=em[:, 1:2]).then_inc(aux_done.sem, 1)
            act.activation(slots, slots, ACT.Sigmoid).then_inc(aux_done.sem, 1)

        def pe_slots_prepare():
            pe.wait_ge(slice_ready.sem, slice_ready.at(1))
            pe.transpose(TP[0:64, 0:8], eaw, ident[0:8, 0:8]).then_inc(proj_ready.sem, 1)
            pe.wait_ge(slice_ready.sem, slice_ready.at(2))
            for i in range(4):
                pe.matmul((SC[0], SC[1], TP, ZP)[i][0:8, :], eawT, atoms[:, i * 512:(i + 1) * 512],
                          start=True, stop=True).then_inc(proj_ready.sem, 1)
            pe.wait_ge(proj_done.sem, proj_done.at(4))

        def pe_slots():
            pe_coefT(8)
            for b in range(B):
                bank = (ZP, OP, PJ[0], PJ[1])[b // 2]
                for k in range(DC):
                    last = pe.matmul(bank[:, (b % 2) * DM:(b % 2 + 1) * DM], xnT[:, k, b * P:(b + 1) * P],
                                     WT[:, k, :], start=(k == 0), stop=(k == DC - 1))
            last.then_inc(out_ready.sem, 1)
            pe.wait_ge(out_done.sem, out_done.at(B))
            pe.wait_ge(slice_ready.sem, slice_ready.at(3))
            GX, VL, ACC = (psum[0], psum[1]), (psum[2], psum[3]), psum[4:6]

            def scatter_out(h, i):
                u = h * 16 + i
                pe.wait_ge(probs_ready.sem, probs_ready.at(u + 1))
                for t in range(4):
                    last = pe.matmul(ACC[t // 2][:, (t % 2) * DM:(t % 2 + 1) * DM], xg[:, i % 2, t * P:(t + 1) * P],
                                     scatter[:, i, :], start=(i == 0 and t % 2 == 0), stop=(i == 15),
                                     skip_group_check=True)
                last.then_inc(mix_ready.sem, 1)

            with pe.Fori(0, 2) as h:
                pe.wait_ge(out_done.sem, out_done.at(B + h * 4))
                for i in range(16):
                    u = h * 16 + i
                    if i >= 2:
                        pe.wait_ge(probs_ready.sem, probs_ready.at(u - 1))
                    for k in range(DC):
                        pe.matmul(GX[i % 2][:, :], gather[:, k, i * P:(i + 1) * P],
                                  xnT[:, k, bass.ds(h * 512, 512)], start=(k == 0), stop=(k == DC - 1))
                    pe.matmul(VL[i % 2][:, :], slots[:, i * P:(i + 1) * P],
                              coefT[:, bass.ds(h * 512, 512)], start=True, stop=True).then_inc(scores_ready.sem, 1)
                    if i:
                        scatter_out(h, i - 1)
                scatter_out(h, 15)

        def act_slots():
            with A.loop(16, 0) as v:
                for r in range(2):
                    u = v * 2 + r
                    act.wait_ge(scores_ready.sem, scores_ready.at(u + 1))
                    act.activation(xv[:, r, :], psum[2 + r][:, :], ACT.Copy).then_inc(mix_done.sem, 1)

        def dve_slots():
            dve.sem_inc(aux5_ready.sem, 1)
            dve.wait_ge(aux6_ready.sem, aux6_ready.at(1))
            for i in range(2):
                dve.tensor_copy(coefT[:, i * 512:(i + 1) * 512], SC[i][0:8, :]).then_inc(dve_own, V.up())
            dve.wait_ge(dve_own, V.now())
            dve.sem_inc(slice_ready.sem, 1)
            dve.wait_ge(out_ready.sem, out_ready.at(1))
            for b in range(B):
                bank = (ZP, OP, PJ[0], PJ[1])[b // 2]
                dve.tensor_tensor(x[:, b, :], x[:, b, :], bank[:, (b % 2) * DM:(b % 2 + 1) * DM],
                                  ALU.add).then_inc(out_done.sem, 1)
            with V.loop(2, 0) as h:
                with V.loop(8, 0) as v:
                    for r in range(2):
                        u = h * 16 + v * 2 + r
                        dve.wait_ge(mix_done.sem, mix_done.at(u + 1))
                        dve.tensor_tensor(xg[:, r, :], psum[r][:, :], xv[:, r, :], ALU.mult).then_inc(probs_ready.sem, 1)
                dve.wait_ge(mix_ready.sem, mix_ready.at((h + 1) * 16))
                for t in range(4):
                    dve.tensor_tensor(x[:, bass.ds(h * 4 + t, 1), :], x[:, bass.ds(h * 4 + t, 1), :],
                                      psum[4 + t // 2][:, (t % 2) * DM:(t % 2 + 1) * DM].unsqueeze(1),
                                      ALU.add).then_inc(out_done.sem, 1)

        hid = work[:, 4096:5120].rearrange("p (r n) -> p r n", r=2)
        gat = work[:, 5120:6144].rearrange("p (r n) -> p r n", r=2)

        def pe_ffn(c):
            def down(r, e, h, f, first):
                v = (e * 2 + h) * c.nf + f
                if f == 0 and not c.keep:
                    pe.wait_ge(acc_done.sem, acc_done.at(e * 2 + h - 1))
                pe.wait_ge(hidden_done.sem, hidden_done.at(v + 1))
                opens = f == 0 and (not c.keep or first)
                for t in range(4):
                    bank = psum[4 + 2 * h + t // 2]
                    last = pe.matmul(bank[:, (t % 2) * DM:(t % 2 + 1) * DM], hid[:, f % 2, t * P:(t + 1) * P],
                                     c.down[r][:, f, :], start=(opens and t % 2 == 0), stop=(f == c.nf - 1),
                                     skip_group_check=True)
                if f == c.nf - 1:
                    last.then_inc(acc_ready.sem, 1)

            def tile(e, i, r, first):
                c.arrived(pe, i, r)
                for h in range(2):
                    for f in range(c.nf):
                        v = (e * 2 + h) * c.nf + f
                        pe.wait_ge(hidden_done.sem, hidden_done.at(v - 1))
                        if c.coef_rows is not None:
                            chunk, toks = c.coef_rows(e, f), slice(h * 512, (h + 1) * 512)
                        for g in range(2 if c.gated else 1):
                            bank = psum[2 * g + f % 2]
                            if g == 1 and c.coef_rows is not None:
                                pe.wait_ge(hidden_done.sem, hidden_done.at(v))
                                bank = psum[2]
                            for k in range(DC):
                                last = pe.matmul(bank[:, :], c.up[r](g, f, k), xnT[:, k, h * 512:(h + 1) * 512],
                                                 start=(k == 0), stop=(k == DC - 1))
                        if c.coef_rows is not None:
                            last = pe.matmul(psum[3][:, :], chunk, coef_parts[0:96, toks], start=True, stop=True)
                        last.then_inc(up_ready.sem, 1)
                        if (h, f) != (0, 0):
                            down(r, e, *((h, f - 1) if f else (h - 1, c.nf - 1)), first)
                down(r, e, 1, c.nf - 1, first)

            peeled = 1 if c.keep else 0
            for e in range(2 * peeled):
                tile(e, 0, e, e == 0)
            with pe.Fori(peeled, c.E // 2) as i:
                for r in range(2):
                    tile(i * 2 + r, i, r, False)

        def act_step(c, e, h, f):
            v = (e * 2 + h) * c.nf + f
            act.wait_ge(up_ready.sem, up_ready.at(v + 1))
            if c.gated:
                act.activation(gat[:, f % 2, :], psum[f % 2][:, :], c.func).then_inc(gate_ready.sem, 1)
            else:
                stand_alone(act)
                act.activation(hid[:, f % 2, :], psum[f % 2][:, :], c.func,
                               bias=c.bias[:, bass.ds(e * c.nf + f, 1)]).then_inc(hidden_done.sem, 1)

        def act_ffn(c):
            with A.loop(c.E // 2, 0) as i:
                for r in range(2):
                    for h in range(2):
                        for f in range(c.nf):
                            act_step(c, i * 2 + r, h, f)

        def dve_step(c, e, h, f):
            v = (e * 2 + h) * c.nf + f
            dve.wait_ge(gate_ready.sem, gate_ready.at(v + 1))
            if c.coef_rows is None:
                dve.tensor_tensor(hid[:, f % 2, :], gat[:, f % 2, :], psum[2 + f % 2][:, :],
                                  ALU.mult).then_inc(hidden_done.sem, 1)
            else:
                dve.tensor_tensor(hid[:, f % 2, :], gat[:, f % 2, :], psum[2][:, :], ALU.mult).then_inc(dve_own, V.up())
                dve.wait_ge(dve_own, V.now())
                dve.tensor_tensor(hid[:, f % 2, :], hid[:, f % 2, :], psum[3][:, :],
                                  ALU.mult).then_inc(hidden_done.sem, 1)

        def dve_add_kept(c):
            for h in range(2):
                dve.wait_ge(acc_ready.sem, acc_ready.at(2 * c.E - 1 + h))
                for t in range(4):
                    last = dve.tensor_tensor(x[:, 4 * h + t, :], x[:, 4 * h + t, :],
                                             psum[4 + 2 * h + t // 2][:, (t % 2) * DM:(t % 2 + 1) * DM], ALU.add)
                last.then_inc(acc_done.sem, 1)
            dve.wait_ge(acc_done.sem, acc_done.at(2))

        def dve_ffn_kept(c):
            with V.loop(c.E // 2, 4 * c.nf) as i:
                for r in range(2):
                    for h in range(2):
                        for f in range(c.nf):
                            dve_step(c, i * 2 + r, h, f)
            dve_add_kept(c)

        def dve_ffn_added(c):
            with V.loop(c.E // 2, 0) as i:
                for r in range(2):
                    e = i * 2 + r
                    for h in range(2):
                        dve.wait_ge(acc_ready.sem, acc_ready.at(e * 2 + h + 1))
                        for t in range(4):
                            bank = psum[4 + 2 * h + t // 2][:, (t % 2) * DM:(t % 2 + 1) * DM]
                            b = 4 * h + t
                            last = dve.scalar_tensor_tensor(x[:, b, :], bank, coef[:, b, bass.ds(e, 1)], x[:, b, :],
                                                            ALU.mult, ALU.add)
                        last.then_inc(acc_done.sem, 1)
            dve.wait_ge(acc_done.sem, acc_done.at(2 * c.E))

        def sp_ring(c):
            with sp.Fori(1, c.E // 2) as i:
                for r in range(2):
                    e = i * 2 + r
                    sp.wait_ge(acc_ready.sem, acc_ready.at(2 * e - 2))
                    c.load(r, e)

        coef_cols = small[:, 576:960].bitcast(BF16).rearrange("p (b e) -> p b e", b=B)
        coef_rest = small[:, 256:416].rearrange("p (b e) -> p b e", b=B)
        coef_parts = arena_b[0:96, 0:512].bitcast(BF16)

        def dve_coef_parts(E):
            dve.memset(coef_cols, 0.0).then_inc(dve_own, V.up())
            dve.wait_ge(dve_own, V.now())
            rest = coef[:, :, 0:E]
            for part in range(3):
                cols = coef_cols[:, :, 32 * part:32 * part + E]
                dve.tensor_copy(cols, rest).then_inc(dve_own, V.up())
                dve.wait_ge(dve_own, V.now())
                if part < 2:
                    dve.tensor_tensor(coef_rest[:, :, 0:E], rest, cols, ALU.subtract).then_inc(dve_own, V.up())
                    dve.wait_ge(dve_own, V.now())
                    rest = coef_rest[:, :, 0:E]
            dve.sem_inc(aux5_ready.sem, 1)
            for i in range(2):
                dve.wait_ge(proj_ready.sem, proj_ready.at(i + 1))
                dve.tensor_copy(coef_parts[:, i * 512:(i + 1) * 512], SC[i][0:96, :]).then_inc(slice_ready.sem, 1)

        def pe_coef_parts():
            pe.wait_ge(aux5_ready.sem, aux5_ready.at(1))
            for b in range(B):
                last = pe.matmul(SC[b // 4][0:96, (b % 4) * P:(b % 4 + 1) * P], coef_cols[:, b, :], ident16[:, :],
                                 start=True, stop=True)
                if b % 4 == 3:
                    last.then_inc(proj_ready.sem, 1)

        W4 = 3 * DM
        codes = [arena_a[:, 2048 + r * W4:2048 + (r + 1) * W4].bitcast(I32) for r in range(2)]
        scales = [arena_a[:, 3584 + r * W4:3584 + (r + 1) * W4] for r in range(2)]
        mags = arena_a[:, 5120:6656]
        sgns = arena_a[:, 6656:8192]
        tops = arena_a[:, 8192:9728]
        sfac = arena_a[:, 9728:11264]
        wq4 = [arena_a[:, 11264 + r * 1536:11264 + (r + 1) * 1536] for r in range(2)]
        lows = arena_a[:, 14336:15872]
        minus6 = small[:, 976:977]

        def dve_dequant(i, r, piece, first=False):
            m, g, j = mags.bitcast(I32), sgns.bitcast(I32), i * 2 + r
            if piece == 0:
                dve.wait_ge(loaded["w5" + "ab"[r]], (i + 1) * 32)
                dve.wait_ge(scale_ready.sem, scale_ready.at(j))
                dve.tensor_scalar(m[:, 0:W4], codes[r], 7, None, ALU.bitwise_and).then_inc(dve_own, V.up())
                dve.tensor_scalar(m[:, W4:2 * W4], codes[r], 4, 7, ALU.logical_shift_right,
                                  ALU.bitwise_and).then_inc(dve_own, V.up())
                dve.tensor_scalar(g[:, 0:W4], codes[r], 8, None, ALU.bitwise_and)
                dve.tensor_scalar(g[:, W4:2 * W4], codes[r], 4, 8, ALU.logical_shift_right,
                                  ALU.bitwise_and).then_inc(codes_ready.sem, 1)
            elif piece == 1:
                dve.wait_ge(dve_own, V.now())
                dve.scalar_tensor_tensor(lows, m, 4.0, m, ALU.max, ALU.add).then_inc(dve_own, V.up())
            elif piece == 2:
                dve.wait_ge(dve_own, V.now())
                dve.wait_ge(top_ready.sem, top_ready.at(j + 1))
                dve.scalar_tensor_tensor(lows, lows, 0.5, tops, ALU.mult, ALU.add).then_inc(dve_own, V.up())
            else:
                dve.wait_ge(dve_own, V.now())
                dve.wait_ge(scale_ready.sem, scale_ready.at(j + 1))
                if not first:
                    dve.wait_ge(acc_ready.sem, acc_ready.at(j * 2 - 2))
                dve.scalar_tensor_tensor(wq4[r], lows, 2.0, sfac, ALU.subtract, ALU.mult).then_inc(weights_ready.sem, 1)

        def act_signs(j):
            act.wait_ge(codes_ready.sem, codes_ready.at(j + 1))
            act.wait_ge(weights_ready.sem, weights_ready.at(j))
            act.activation(tops, mags.bitcast(I32), ACT.Relu, bias=minus6).then_inc(top_ready.sem, 1)
            act.activation(sfac, sgns.bitcast(I32), ACT.Copy, scale=-0.25, bias=1.0).then_inc(sign_ready.sem, 1)

        def act_codes_ffn():
            act_signs(0)
            act_norm(5)
            with A.loop(3, 0) as i:
                for r in range(2):
                    for f in range(s5.nf):
                        act_step(s5, i * 2 + r, 0, f)
                    act_signs(i * 2 + r + 1)
                    for f in range(s5.nf):
                        act_step(s5, i * 2 + r, 1, f)
            for f in range(s5.nf):
                act_step(s5, 6, 0, f)
            act_signs(7)
            for h, e in ((1, 6), (0, 7), (1, 7)):
                for f in range(s5.nf):
                    act_step(s5, e, h, f)

        def dve_codes_ffn():
            def tile(e, i, r, first=False):
                for h in range(2):
                    for f in range(s5.nf):
                        dve_step(s5, e, h, f)
                        if i is not None:
                            dve_dequant(i, r, h * s5.nf + f, first)

            tile(0, 0, 1, True)
            with V.loop(3, 8) as i:
                tile(i * 2 + 1, i + 1, 0)
                tile(i * 2 + 2, i + 1, 1)
            tile(7, None, 0)
            dve_add_kept(s5)

        def pool_signed_scales():
            with G.loop(4, 0) as i:
                for r in range(2):
                    pool.wait_ge(sign_ready.sem, sign_ready.at(i * 2 + r + 1))
                    pool.tensor_tensor(sfac.rearrange("p (l n) -> p l n", l=2), sfac.rearrange("p (l n) -> p l n", l=2),
                                       scales[r].unsqueeze(1).to_broadcast([P, 2, W4]),
                                       ALU.mult).then_inc(scale_ready.sem, 1)

        xc = [work[:, k * 1024:(k + 1) * 1024].rearrange("p (b t) -> p b t", b=B) for k in range(DC)]
        dx = rows_(arena_b, 12288, 2, 1024)
        NT = B * P
        sp_, sn_, dl_, da_, bu_, hh_ = (work[0:64, 2048 + k * NT:2048 + (k + 1) * NT] for k in range(6))
        wB = rows_(arena_b, 8192, 2, 64)
        wC = rows_(arena_b, 8320, 2, 64)
        wD = rows_(arena_b, 8448, 2, 64)
        wIn = rows_(arena_b, 8576, 2, 64)
        wOut = arena_b[0:64, 8704:8960]
        cw = small[:, 544:552].rearrange("p (c k) -> p c k", c=DC)
        cbias = small[:, 552:554]
        dskip = small[:, 554:556]
        alog = small[0:64, 556:557]
        nega = small[0:64, 557:558]

        def dve_scan():
            dve.wait_ge(loaded["w9"], 16 * 9)
            dve.wait_ge(xnt_done.sem, xnt_done.at(B))
            xk = [xnT[:, k, :].rearrange("p (b t) -> p b t", b=B) for k in range(DC)]
            for k in range(DC):
                dve.tensor_scalar(xc[k], xk[k], cw[:, k, 3:4], cbias[:, k:k + 1], ALU.mult,
                                  ALU.add).then_inc(dve_own, V.up())
            for d in range(1, 4):
                dve.wait_ge(dve_own, V.now())
                for k in range(DC):
                    dve.scalar_tensor_tensor(xc[k][:, :, d:P], xk[k][:, :, 0:P - d], cw[:, k, 3 - d:4 - d],
                                             xc[k][:, :, d:P], ALU.mult, ALU.add).then_inc(dve_own, V.up())
            dve.wait_ge(dve_own, V.now())
            dve.sem_inc(aux3_ready.sem, 1)
            for k in range(DC):
                dve.tensor_scalar(dx[:, k, :], xc[k].rearrange("p b t -> p (b t)"), dskip[:, k:k + 1], None,
                                  ALU.mult).then_inc(dve_own, V.up())
            dve.wait_ge(aux_ready.sem, aux_ready.at(3))
            for i in range(2):
                half = slice(i * 512, (i + 1) * 512)
                dve.tensor_scalar(sp_[:, half], psum[4 + i][0:64, :], 0.0, None, ALU.max).then_inc(dve_own, V.up())
                dve.tensor_scalar(sn_[:, half], psum[4 + i][0:64, :], 0.0, None, ALU.min).then_inc(dve_own, V.up())
            dve.wait_ge(dve_own, V.now())
            dve.tensor_tensor(sn_, sn_, sp_, ALU.subtract).then_inc(aux4_ready.sem, 1)
            dve.wait_ge(aux5_ready.sem, aux5_ready.at(1))
            dve.tensor_tensor(dl_, dl_, sp_, ALU.add).then_inc(dve_own, V.up())
            dve.wait_ge(dve_own, V.now())
            dve.sem_inc(aux6_ready.sem, 1)
            for i in range(2):
                half = slice(i * 512, (i + 1) * 512)
                dve.tensor_tensor(bu_[:, half], dl_[:, half], psum[i][0:64, :], ALU.mult).then_inc(dve_own, V.up())
            dve.wait_ge(dve_own, V.now())
            dve.wait_ge(aux2_ready.sem, aux2_ready.at(1))
            for i in range(2):
                half = slice(i * 512, (i + 1) * 512)
                dve.tensor_tensor(bu_[:, half], bu_[:, half], psum[6 + i][0:64, :], ALU.mult).then_inc(dve_own, V.up())
            dve.wait_ge(aux5_ready.sem, aux5_ready.at(2))
            dve.memset(da_.rearrange("p (b t) -> p b t", b=B)[:, :, 0:1], 0.0).then_inc(dve_own, V.up())
            dve.wait_ge(dve_own, V.now())
            dve.tensor_tensor_scan(hh_, da_, bu_, 0.0, ALU.mult, ALU.add).then_inc(dve_own, V.up())
            dve.wait_ge(dve_own, V.now())
            for i in range(2):
                half = slice(i * 512, (i + 1) * 512)
                last = dve.tensor_tensor(hh_[:, half], hh_[:, half], psum[2 + i][0:64, :], ALU.mult)
                last.then_inc(slice_ready.sem, 1)
            for b in range(B):
                dve.wait_ge(out_ready.sem, out_ready.at(b + 1))
                dve.tensor_tensor(x[:, b, :], x[:, b, :], psum[b % 4][:, 0:DM], ALU.add).then_inc(out_done.sem, 1)

        def act_scan():
            act.wait_ge(loaded["w9"], 16 * 9)
            act.activation(nega, alog, ACT.Exp).then_inc(act_own, A.up())
            act.wait_ge(act_own, A.now())
            act.activation(nega, nega, ACT.Copy, scale=-1.0).then_inc(act_own, A.up())
            act.wait_ge(act_own, A.now())
            act.wait_ge(aux4_ready.sem, aux4_ready.at(1))
            act.activation(sn_, sn_, ACT.Exp).then_inc(act_own, A.up())
            act.wait_ge(act_own, A.now())
            act.activation(dl_, sn_, ACT.Ln, bias=1.0).then_inc(aux5_ready.sem, 1)
            act.wait_ge(aux6_ready.sem, aux6_ready.at(1))
            act.activation(da_, dl_, ACT.Exp, scale=nega).then_inc(aux5_ready.sem, 1)

        def pe_scan():
            pe.wait_ge(loaded["w9"], 16 * 9)
            for n, w in enumerate((wB, wC, wD)):
                for i in range(2):
                    for k in range(DC):
                        last = pe.matmul(psum[2 * n + i][0:64, :], w[:, k, :], xnT[:, k, i * 512:(i + 1) * 512],
                                         start=(k == 0), stop=(k == DC - 1))
                last.then_inc(aux_ready.sem, 1)
            pe.wait_ge(aux3_ready.sem, aux3_ready.at(1))
            for i in range(2):
                for k in range(DC):
                    last = pe.matmul(psum[6 + i][0:64, :], wIn[:, k, :],
                                     work[:, k * 1024 + i * 512:k * 1024 + (i + 1) * 512],
                                     start=(k == 0), stop=(k == DC - 1))
            last.then_inc(aux2_ready.sem, 1)
            pe.wait_ge(slice_ready.sem, slice_ready.at(2))
            for b in range(B):
                if b >= 4:
                    pe.wait_ge(out_done.sem, out_done.at(b - 3))
                toks = slice(b * P, (b + 1) * P)
                pe.matmul(psum[b % 4][:, 0:DM], hh_[:, toks], wOut, start=True, stop=False, skip_group_check=True)
                for k in range(DC):
                    last = pe.matmul(psum[b % 4][:, k * P:(k + 1) * P], dx[:, k, toks], ident[:, :],
                                     start=False, stop=(k == DC - 1), skip_group_check=True)
                last.then_inc(out_ready.sem, 1)

        bqT, bkT = small[:, 32:48], small[:, 48:64]
        bo0, bv0 = small[:, 256:512], work[:, 7168:9216]
        s0 = Attention(wq=rows_(arena_a, 0, 2, 2048), wk=rows_(arena_a, 4096, 2, 2048), wv=rows_(arena_a, 8192, 2, 2048),
                 wo=rows_(arena_a, 12288, 16, DM), bq=bqT, bk=bkT, bv=bv0, bo=bo0, causal=True,
                 scale=128 ** -0.5, w="w0", nw=8)

        wts1 = [(rows_(ar, 0, 2, DM), rows_(ar, 512, 2, DM), rows_(ar, 1024, 2, 64), rows_(ar, 1152, 2, DM))
                for ar in (arena_b, arena_a)]
        s1 = Attention(wq=wts1[0][0], wk=wts1[0][1], wv=wts1[0][2], wo=wts1[0][3], bq=small[:, 560:562],
                 bk=small[:, 562:564], bv=small[:, 564:628], bo=small[:, 640:896], cross=True, scale=8 ** -0.5,
                 w="w1", nw=10)
        s3 = Attention(wq=wts1[1][0], wk=wts1[1][1], wv=wts1[1][2], wo=wts1[1][3], causal=True, scale=8 ** -0.5,
                 w="w3", nw=4)
        wts5 = [w.rearrange("p (l m n) -> p l m n", l=2, m=3) for w in wq4]
        s5 = FeedForward(E=8, nf=2, gated=True, func=ACT.Gelu_apprx_tanh, keep=True,
                 up=[lambda g, f, k, w=w: w[:, k, g, f::2] for w in wts5], down=[w[:, :, 2, :] for w in wts5],
                 arrived=lambda eng, i, par: eng.wait_ge(weights_ready.sem, weights_ready.at(i * 2 + par + 1)))
        s6 = Attention(wq=rows_(arena_b, 0, 2, 2048), wk=rows_(arena_b, 4096, 2, 512), wv=rows_(arena_b, 5120, 2, 512),
                 wo=rows_(arena_b, 6144, 16, DM), cos=arena_b[:, 10240:10368], sin=arena_b[:, 10368:10496],
                 gqa=True, causal=True, rope=True, scale=128 ** -0.5, w="w6", nw=6)
        s7 = Attention(wq=s0.wq, wk=s0.wk, wv=s0.wv, wo=s0.wo, cross=True, scale=128 ** -0.5, w="w7", nw=4)
        fc1 = [rows_(arena_b, 4096 * r, 2, 1024) for r in range(2)]
        fc2 = [rows_(arena_b, 4096 * r + 2048, 8, DM) for r in range(2)]
        b2e, gatew8 = arena_b[0:8, 9216:9472], rows_(arena_b, 9472, 2, 8)
        gateb8, alpha8 = small[:, 960:968], small[:, 968:976]
        s8 = FeedForward(E=8, nf=8, gated=False, func=ACT.Gelu, bias=small[:, 896:960],
                 up=[lambda g, f, k, w=w: w[:, k, f * P:(f + 1) * P] for w in fc1], down=fc2,
                 arrived=lambda eng, i, par: eng.wait_ge(loaded["w8" + "ab"[par]], (i + 1) * 32),
                 load=lambda r, e: load_expert(fc1, "fc1", fc2, "fc2", "w8", r, e))
        wts11 = [arena_a[:, 1536 * r:1536 * (r + 1)] for r in range(2)]
        w13 = [w[:, 0:1024].rearrange("p (g k n) -> p g k n", g=2, k=DC) for w in wts11]
        w2 = [rows_(w, 1024, 2, DM) for w in wts11]
        gatew11, sgate11 = rows_(arena_a, 4096, 2, 16), rows_(arena_a, 4128, 2, 1)
        chunk_experts = arena_a[0:96, 8192:8192 + 28 * P]
        chunk_experts16 = arena_b[0:96, 1024:1024 + 14 * P].bitcast(BF16)
        s11 = FeedForward(E=14, nf=2, gated=True, func=ACT.Silu, keep=True,
                  up=[lambda g, f, k, w=w: w[:, g, k, f * P:(f + 1) * P] for w in w13], down=w2,
                  coef_rows=lambda e, f: chunk_experts16[:, bass.ds((e * 2 + f) * P, P)],
                  arrived=lambda eng, i, par: eng.wait_ge(loaded["w11" + "ab"[par]], (i + 1) * 16),
                  load=lambda r, e: load_tile(wts11, "tiles11", "w11", r, e))

        def load_tile(dst, name, landed, r, e):
            src = D[name][e] if isinstance(e, int) else D[name][bass.ds(e, 1)].rearrange("e p n -> (e p) n")
            sp.dma_start(dst[r], src).then_inc(loaded[landed + "ab"[r]], 16)

        def load_expert(ups, up_name, downs, down_name, landed, r, e):
            for dst, name in ((ups[r], up_name), (downs[r], down_name)):
                src = D[name][e] if isinstance(e, int) else D[name][bass.ds(e, 1)].rearrange("e p k n -> (e p) k n")
                sp.dma_start(dst, src).then_inc(loaded[landed + "ab"[r]], 16)

        def n(k, *which):
            return {w: k for w in which}

        units = ("scores_ready", "max_ready", "exp_done", "probsT_ready", "probsT_done")
        softmax = units + ("recip_ready", "probs_ready")
        norm = n(1, "var_ready", "std_ready") | n(B, "xn_ready", "xnt_ready", "xnt_done")
        attn128 = norm | n(4 * B, *softmax, "mix_ready", "mix_done", "out_ready", "out_done") \
            | n(12 * B, "proj_ready", "proj_done") | n(B, "slice_ready")
        attn8 = norm | n(8 * B, *units, "mix_ready", "kpad_ready") \
            | n(B, "slice_ready", "mix_done", "aux_ready", "aux_done", "out_ready", "out_done") \
            | n(2 * B, "proj_ready") | n(3 * B, "proj_done")
        route = n(1, "aux2_ready", "aux3_ready", "aux4_ready")

        def ffn(c):
            return n(2 * c.E * c.nf, "up_ready", "hidden_done", *(["gate_ready"] if c.gated else [])) \
                | n(2 * c.E, "acc_ready") | n(2 if c.keep else 2 * c.E, "acc_done")

        steps = {
            0: attn128,
            1: attn8 | n(1, "aux2_ready"),
            2: norm | route | n(1, "aux_ready", "aux5_ready", "aux6_ready") | n(2, "aux_done") | n(3, "slice_ready")
            | n(5, "proj_ready") | n(4, "proj_done") | n(1, "out_ready") | n(16, "out_done")
            | n(32, "scores_ready", "mix_done", "probs_ready", "mix_ready"),
            3: attn8,
            4: norm | n(2, *softmax, "out_ready") | n(1, "aux2_ready") | n(B, "out_done"),
            5: norm | ffn(s5) | n(8, "codes_ready", "top_ready", "sign_ready", "scale_ready", "weights_ready"),
            6: attn128 | n(8 * B, "aux_ready", "aux2_ready"),
            7: attn128,
            8: norm | route | n(1, "aux5_ready", "aux6_ready", "slice_ready", "out_ready") | n(B, "out_done") | ffn(s8),
            9: norm | n(3, "aux_ready") | n(1, "aux2_ready", "aux3_ready", "aux4_ready", "aux6_ready")
            | n(2, "aux5_ready", "slice_ready") | n(B, "out_ready", "out_done"),
            10: n(1, "var_ready", "std_ready") | n(B, "xn_ready", "slice_ready", "mix_done", "out_ready", "out_done")
            | n(8 * B, *units, "mix_ready", "kpad_ready"),
            11: norm | route | n(1, "aux_ready", "aux5_ready", "aux6_ready") | n(2, "proj_ready", "slice_ready")
            | ffn(s11),
        }
        bases, total = {}, {t.sem.name: 0 for t in tallies}
        for s in stages:
            bases[s] = dict(total)
            for n, k in steps[s].items():
                total[n] += k
        done_before = {s: k for k, s in enumerate(stages)}

        def enter(eng, s):
            for t in tallies:
                t.base = bases[s][t.sem.name]
            if done_before[s]:
                eng.wait_ge(stage_done.sem, done_before[s] + 1)

        block = ctx.enter_context(nc.Block())

        @block.sync
        def _(sp_eng):
            def load(landed, *pairs):
                if landed[0] == "w" and int(landed.strip("wab")) not in stages and pairs[0][1] != "mask_pair":
                    return
                for dst, name in pairs:
                    sp.dma_start(dst, name if not isinstance(name, str) else D[name]).then_inc(loaded[landed], 16)

            def after(s):
                if s in done_before:
                    sp.wait_ge(stage_done.sem, done_before[s] + 2)

            def every(name):
                return D[name].partition_broadcast(P)

            load("x", (x[:, :, :], D["x"].rearrange("b t d -> t b d")))
            load("const", (ident[:, :], "ident"), (xn2[:, 0, 0:P], "causal"),
                 (heads8[:, :], "heads8"), (heads16[:, :], "heads16"), (tri[:, :, :], every("tri")),
                 (iotaf[:, :], every("iotaf")), (iotap[:, :], "iotap"))
            if 0 in stages:
                load("w0", (s0.bq, "bqT"), (s0.bk, "bkT"), (s0.bv, every("bv0")), (s0.bo, every("bo0")),
                     (s0.wq, "wq0"), (s0.wk, "wk0"), (s0.wv, "wv0"), (s0.wo, "wo0"))
            load("ctx", (ctxn[:, :, :], D["ctx"].rearrange("b t d -> t b d")), (ctxT[:, :, :], "ctxT"))
            if 1 in stages:
                load("w1", (s1.wq, "wq1"), (s1.wk, "wk1"), (s1.wv, "wv1"), (s1.wo, "wo1"), (s1.bq, "bq1"),
                     (s1.bk, "bk1"), (s1.bv, every("bv1")), (s1.bo, every("bo1")))
            load("w1", (pair_mask[:, :], "mask_pair"), (row_mask[:, :, :], every("mask_row")))
            if 2 in stages:
                load("w2", (WT, "WT"), (atoms, "atoms"), (slots, "importance"), (eaw, "eaw"), (gatewT, "gatew2"),
                     (rowsi, "slot_rows"))
            after(0)
            load("w3", (s3.wq, "wq3"), (s3.wk, "wk3"), (s3.wv, "wv3"), (s3.wo, "wo3"))
            if 5 in stages:
                for r in range(2):
                    load("w5" + "ab"[r], (codes[r], D["codes"][r]), (scales[r], D["scales"][r]))
            after(1)
            if 2 in stages:
                load("w2", (colsi, every("slot_cols")))
            after(2)
            if 6 in stages:
                load("w6", (s6.wq, "wq6"), (s6.wk, "wk6"), (s6.wv, "wv6"), (s6.wo, "wo6"), (s6.cos, "cosT"),
                     (s6.sin, "sinT"))
            if 5 in stages:
                enter(sp, 5)
                with sp.Fori(1, 4) as i:
                    for r in range(2):
                        j = i * 2 + r
                        sp.wait_ge(scale_ready.sem, scale_ready.at(j - 1))
                        for dst, name in ((codes[r], "codes"), (scales[r], "scales")):
                            sp.dma_start(dst, D[name][bass.ds(j, 1)].rearrange("e p n -> (e p) n")
                                         ).then_inc(loaded["w5" + "ab"[r]], 16)
            after(5)
            if 7 in stages:
                load("w7", (s7.wq, "wq7"), (s7.wk, "wk7"), (s7.wv, "wv7"), (s7.wo, "wo7"))
            after(6)
            load("w8", (b2e, "b2e"), (gatew8, "gatew8"), (gateb8, every("gateb8")), (alpha8, every("alpha8")),
                 (s8.bias, "b1T"))
            if 8 in stages:
                for r in range(2):
                    s8.load(r, r)
            load("w9", (wB, "wB9"), (wC, "wC9"), (wD, "wD9"), (wIn, "wIn9"), (wOut, "wOut9"), (cw, "cw9"),
                 (cbias, "cb9"), (dskip, "dskip9"), (alog, "alog9"))
            after(7)
            load("w11", (gatew11, "gatew11"), (sgate11, "sgate11"), (chunk_experts, "chunk_experts"))
            if 11 in stages:
                for r in range(2):
                    s11.load(r, r)
            for s, c in ((8, s8), (11, s11)):
                if s in stages:
                    enter(sp, s)
                    sp_ring(c)
            sp.wait_ge(stage_done.sem, len(stages) + 1)
            sp.dma_start(out.rearrange("b t d -> t b d"), x[:, :, :]).then_inc(stored, 16)
            sp.wait_ge(stored, 16)

        @block.gpsimd
        def _(pool_eng):
            for t in tallies:
                pool.sem_inc(t.sem, t.credit)
            pool.sem_inc(credits_given, 1)
            pool.wait_ge(loaded["const"], 16 * 7)
            pool.wait_ge(loaded["ctx"], 32)
            for s in stages:
                enter(pool, s)
                if s in (0, 6, 7):
                    pool_attn128(s, {0: s0, 6: s6, 7: s7}[s])
                elif s in (1, 3):
                    pool_small(s, {1: s1, 3: s3}[s])
                elif s == 4:
                    pool_memory(s)
                elif s == 5:
                    pool_signed_scales()
                elif s == 10:
                    pool_small(s, None)
                elif s == 11:
                    pool.wait_ge(loaded["w11"], 48)
                    pool.tensor_copy(chunk_experts16, chunk_experts).then_inc(aux_ready.sem, 1)

        @block.scalar
        def _(act_eng):
            act.wait_ge(credits_given, 1)
            for s in stages:
                enter(act, s)
                if s == 2:
                    act_slots_prepare()
                if s != 5:
                    act_norm(s, natural if s == 10 else None)
                if s in (0, 6, 7):
                    act_attn128(s, {0: s0, 6: s6, 7: s7}[s])
                elif s in (1, 3):
                    act_small(s, {1: s1, 3: s3}[s])
                elif s == 2:
                    act_route(8)
                    act_slots()
                elif s == 4:
                    act_memory(s)
                elif s == 5:
                    act_codes_ffn()
                elif s == 8:
                    act.wait_ge(loaded["w8"], 16 * 5)
                    act_route(8)
                    act_ffn(s8)
                elif s == 9:
                    act_scan()
                elif s == 10:
                    act_small(s, None)
                elif s == 11:
                    act.wait_ge(aux2_ready.sem, aux2_ready.at(1))
                    act.activation(coef[:, :, 16:20], PJ[1][:, 0:B].unsqueeze(2).to_broadcast([P, B, 4]),
                                   ACT.Sigmoid).then_inc(aux6_ready.sem, 1)
                    act_route(16)
                    act_ffn(s11)

        @block.vector
        def _(dve_eng):
            dve.wait_ge(credits_given, 1)
            dve.wait_ge(loaded["const"], 16 * 7)
            dve.tensor_copy(ident16[:, :], ident[:, :]).then_inc(masks16_ready, 1)
            dve.tensor_copy(causal16[:, :], xn2[:, 0, 0:P]).then_inc(masks16_ready, 1)
            dve.wait_ge(loaded["x"], 16)
            for s in stages:
                enter(dve, s)
                if s == 1:
                    dve.wait_ge(loaded["w1"], 16 * 10)
                    dve.tensor_tensor(mask16[:, :, :], row_mask[:, :, :],
                                      pair_mask[:, :].unsqueeze(1).to_broadcast([P, B, P]),
                                      ALU.max).then_inc(dve_own, V.up())
                    dve.wait_ge(dve_own, V.now())
                    dve.tensor_scalar(mask16[:, :, :], mask16[:, :, :], NEG, None, ALU.mult).then_inc(aux2_ready.sem, 1)
                elif s == 2:
                    dve_slots_prepare()
                elif s == 4:
                    dve.wait_ge(loaded["w1"], 16 * (10 if 1 in stages else 2))
                    dve.tensor_scalar(mask16[:, :, :], row_mask[:, :, :], -NEG, NEG, ALU.mult,
                                      ALU.add).then_inc(aux2_ready.sem, 1)
                    dve.tensor_reduce(valid, row_mask[:, :, :], AX, ALU.max).then_inc(dve_own, V.up())
                elif s == 5:
                    dve.memset(minus6, -6.0)
                    for piece in range(4):
                        dve_dequant(0, 0, piece, first=True)
                elif s == 0:
                    dve.wait_ge(loaded["w0"], 16 * 8)
                elif s == 6:
                    dve.wait_ge(loaded["w6"], 16 * 6)
                dve_norm(s, natural if s == 10 else None)
                if s in (0, 6, 7):
                    dve_attn128(s, {0: s0, 6: s6, 7: s7}[s])
                    dve.wait_ge(out_done.sem, out_done.at(4 * B))
                elif s in (1, 3):
                    dve_small(s, {1: s1, 3: s3}[s])
                    dve.wait_ge(out_done.sem, out_done.at(B))
                elif s == 2:
                    dve_route(8, 2, clip=50.0)
                    dve_slots()
                    dve.wait_ge(out_done.sem, out_done.at(2 * B))
                elif s == 4:
                    dve_memory(s)
                    dve.wait_ge(out_done.sem, out_done.at(B))
                elif s == 5:
                    dve_codes_ffn()
                elif s == 8:
                    dve.wait_ge(loaded["w8"], 16 * 5)
                    dve_route(8, 2, bias=gateb8, alpha=alpha8)
                    dve.sem_inc(aux5_ready.sem, 1)
                    dve.wait_ge(aux6_ready.sem, aux6_ready.at(1))
                    for i in range(2):
                        dve.tensor_copy(coefT[:, i * 512:(i + 1) * 512], SC[i][0:8, :]).then_inc(dve_own, V.up())
                    dve.wait_ge(dve_own, V.now())
                    dve.sem_inc(slice_ready.sem, 1)
                    dve.wait_ge(out_ready.sem, out_ready.at(1))
                    for b in range(B):
                        bank = (ZP, OP, PJ[0], PJ[1])[b // 2]
                        dve.tensor_tensor(x[:, b, :], x[:, b, :], bank[:, (b % 2) * DM:(b % 2 + 1) * DM],
                                          ALU.add).then_inc(out_done.sem, 1)
                    dve.wait_ge(out_done.sem, out_done.at(B))
                    dve_ffn_added(s8)
                elif s == 9:
                    dve_scan()
                    dve.wait_ge(out_done.sem, out_done.at(B))
                elif s == 10:
                    dve_small(s, None)
                    dve.wait_ge(out_done.sem, out_done.at(B))
                elif s == 11:
                    dve_route(16, 4, over_all=True)
                    dve.wait_ge(aux6_ready.sem, aux6_ready.at(1))
                    dve_coef_parts(20)
                    dve_ffn_kept(s11)
                dve.sem_inc(stage_done.sem, 1)

        @block.tensor
        def _(pe_eng):
            pe.wait_ge(credits_given, 1)
            pe.wait_ge(masks16_ready, 2)
            pe.wait_ge(loaded["const"], 16 * 7)
            pe.wait_ge(loaded["ctx"], 32)
            for s in stages:
                enter(pe, s)
                if s == 2:
                    pe.wait_ge(loaded["w2"], 16 * 7)
                    pe_slots_prepare()
                if s != 10:
                    pe_norm(s, 2 if s == 5 else 1)
                    pe.wait_ge(xnt_done.sem, xnt_done.at(B))
                if s in (0, 6, 7):
                    pe_attn128(s, {0: s0, 6: s6, 7: s7}[s])
                elif s in (1, 3):
                    if s == 1:
                        pe.wait_ge(aux2_ready.sem, aux2_ready.at(1))
                    pe_small(s, {1: s1, 3: s3}[s])
                elif s == 2:
                    pe_route(8, gatewT)
                    pe_slots()
                elif s == 4:
                    pe_memory(s)
                elif s == 5:
                    pe_ffn(s5)
                elif s == 8:
                    pe.wait_ge(loaded["w8"], 16 * 5)
                    pe_route(8, gatew8)
                    pe_coefT(8)
                    pe.wait_ge(slice_ready.sem, slice_ready.at(1))
                    for b in range(B):
                        bank = (ZP, OP, PJ[0], PJ[1])[b // 2]
                        last = pe.matmul(bank[:, (b % 2) * DM:(b % 2 + 1) * DM], coefT[:, b * P:(b + 1) * P], b2e,
                                         start=True, stop=True)
                    last.then_inc(out_ready.sem, 1)
                    pe.wait_ge(out_done.sem, out_done.at(B))
                    pe_ffn(s8)
                elif s == 9:
                    pe_scan()
                elif s == 10:
                    pe_small(s, None)
                elif s == 11:
                    pe.wait_ge(loaded["w11"], 48)
                    pe_route(16, gatew11, sgate11)
                    pe.wait_ge(aux3_ready.sem, aux3_ready.at(1))
                    pe.wait_ge(aux6_ready.sem, aux6_ready.at(1))
                    pe_coef_parts()
                    pe.wait_ge(slice_ready.sem, slice_ready.at(2))
                    pe.wait_ge(aux_ready.sem, aux_ready.at(1))
                    pe_ffn(s11)


def layouts(I):
    c = np.ascontiguousarray

    def kxn(w):
        return c(w.reshape(-1, P, w.shape[-1]).transpose(1, 0, 2))

    def col(v, n):
        return c(v.reshape(n, P).T)

    d = {"x": I["x"], "ctx": I["ctx_2048"], "ctxT": kxn(I["ctx_2048"].reshape(B * P, DM).T)}
    d["mask_pair"], d["mask_row"] = I["mask_SxS2_bc0"], I["mask_BxS2_bk0"]
    d["bqT"], d["bkT"] = c(I["L0_attn_b_Q"].T), c(I["L0_attn_b_K"].T)
    d["bv0"], d["bo0"] = I["L0_attn_b_V"].reshape(-1), I["L0_attn_b_O"]
    for n, k in (("wq0", "W_Q"), ("wk0", "W_K"), ("wv0", "W_V")):
        d[n] = kxn(I["L0_attn_" + k].transpose(1, 0, 2).reshape(DM, -1))
    d["wo0"] = c(I["L0_attn_W_O"].transpose(1, 0, 2))
    rep = np.arange(DM) // 32 * 8 + np.arange(DM) % 8
    for s, p in (("1", "L0_xattn_"), ("3", "L1_attn_")):
        d["wq" + s], d["wk" + s] = kxn(I[p + "Wq"].T), kxn(I[p + "Wk"][rep].T)
        d["wv" + s], d["wo" + s] = kxn(I[p + "Wv"].T), kxn(I[p + "Wo"].T)
    d["bq1"], d["bk1"] = col(I["L0_xattn_bq"], 2), col(I["L0_xattn_bk"][rep], 2)
    d["bv1"], d["bo1"] = I["L0_xattn_bv"], I["L0_xattn_bo"]
    d["WT"], d["atoms"], d["importance"] = kxn(I["L0_ffn_W"].T), I["L0_ffn_atoms"], I["L0_ffn_importance"]
    d["eaw"], d["gatew2"] = I["L0_ffn_expert_atom_weights"], kxn(I["L0_ffn_gate_w"].T)
    d["slot_cols"], d["slot_rows"] = I["L0_ffn_mask_idx"], col(I["L0_ffn_mask_idx"], 16)
    def tiles(gate, up, down):
        g, u = (w.reshape(8, DM, P).transpose(0, 2, 1) for w in (gate, up))
        return c(np.stack([g, u, down.reshape(DM, 8, P).transpose(1, 2, 0)], axis=2).reshape(8, P, 3 * DM))

    d["codes"] = tiles(*(I[f"L1_ffn_{k}_W_packed"] for k in ("gate", "up", "down")))
    d["scales"] = tiles(*(np.repeat(I[f"L1_ffn_{k}_scales"], 16, axis=1) for k in ("gate", "up", "down")))
    for n in "qkv":
        d[f"w{n}6"], d[f"w{n}7"] = kxn(I["L2_attn_w_" + n]), kxn(I["L2_xattn_W" + n])
    d["wo6"], d["wo7"] = kxn(I["L2_attn_w_o"]), kxn(I["L2_xattn_Wo"])
    d["fc1"] = c(I["L2_ffn_fc1_w"].reshape(8, DC, P, 1024).transpose(0, 2, 1, 3))
    d["fc2"] = c(I["L2_ffn_fc2_w"].reshape(8, 8, P, DM).transpose(0, 2, 1, 3))
    d["b1T"], d["b2e"] = col(I["L2_ffn_fc1_b"].reshape(-1), 64), I["L2_ffn_fc2_b"]
    d["gatew8"], d["gateb8"], d["alpha8"] = kxn(I["L2_ffn_gate_w"]), I["L2_ffn_gate_b"], I["L2_ffn_alpha"]
    wx = I["L3_attn_Wxproj"]
    d["wB9"], d["wC9"] = kxn(wx[0:64].T), kxn(wx[64:128].T)
    d["wD9"] = kxn(np.repeat(wx[128:129], 64, axis=0).T)
    d["wIn9"], d["wOut9"] = kxn(I["L3_attn_Winproj"].T), c(I["L3_attn_Woutproj"].T)
    d["cw9"] = c(I["L3_attn_conv_w"].reshape(DC, P, 4).transpose(1, 0, 2))
    d["cb9"], d["dskip9"] = col(I["L3_attn_conv_b"], 2), col(I["L3_attn_D"], 2)
    d["alog9"] = I["L3_attn_A_log"].reshape(64, 1)
    w13, w2 = I["L3_ffn_w13"], I["L3_ffn_w2"]
    sgu, sd = I["L3_ffn_shared_gate_up_w"], I["L3_ffn_shared_down_w"]
    sh13 = sgu.reshape(2, 4, 176, DM).transpose(1, 0, 2, 3).reshape(4, 352, DM)
    sh2 = sd.reshape(DM, 4, 176).transpose(1, 0, 2)
    w13, w2 = np.concatenate([w13, sh13]), np.concatenate([w2, sh2])
    pad = ((0, 28 * P - 20 * 176), (0, 0))
    gu = [np.pad(w13[:, g * 176:(g + 1) * 176].reshape(-1, DM), pad).reshape(14, DM, DC, P).transpose(0, 3, 2, 1)
          for g in range(2)]
    dn = np.pad(w2.transpose(0, 2, 1).reshape(-1, DM), pad).reshape(14, 2, P, DM).transpose(0, 2, 1, 3)
    d["tiles11"] = c(np.concatenate([t.reshape(14, P, -1) for t in (*gu, dn)], axis=2))
    owner = np.where(np.arange(28 * P) < 20 * 176, np.arange(28 * P) // 176, -1)
    d["chunk_experts"] = (np.arange(96)[:, None] % 32 == owner).astype(np.float32)
    d["gatew11"], d["sgate11"] = kxn(I["L3_ffn_gate_w"].T), kxn(I["L3_ffn_sgate_w"].T)
    t = np.arange(P)
    d["ident"] = np.eye(P, dtype=np.float32)
    d["causal"] = np.where(t[None, :] <= t[:, None], 0.0, NEG).astype(np.float32)
    d["heads8"] = (t[:, None] // 8 == np.arange(16)).astype(np.float32)
    d["heads16"] = (t[:, None] // 16 == np.arange(8)).astype(np.float32)
    d["tri"] = np.tril(np.ones((16, 16), np.float32), -1)
    d["iotaf"] = np.arange(DM, dtype=np.float32)
    d["iotap"] = np.stack([t, t + P], 1).astype(np.float32)
    inv = 1.0 / np.float32(10000.0) ** (np.arange(0, P, 2, dtype=np.float32) / np.float32(P))
    ang = np.outer(np.arange(P, dtype=np.float32), inv).astype(np.float32)
    d["cosT"] = c(np.concatenate([np.cos(ang), np.cos(ang)], 1).T.astype(np.float32))
    d["sinT"] = c(np.concatenate([-np.sin(ang), np.sin(ang)], 1).T.astype(np.float32))
    return d


STAGES = tuple(range(12))


def kernel(**inputs):
    import concourse.bacc as bacc
    from concourse.bass_utils import run_bass_kernel_spmd

    nc = bacc.Bacc("TRN2", target_bir_lowering=False, num_devices=1)
    arrays = layouts({k: np.asarray(v) for k, v in inputs.items()})
    D = {n: nc.dram_tensor("in_" + n, a.shape, mybir.dt.from_np(a.dtype), kind="ExternalInput").ap()
         for n, a in arrays.items()}
    out = nc.dram_tensor("out", (B, P, DM), F32, kind="ExternalOutput").ap()
    build(nc, D, out, STAGES)
    got = run_bass_kernel_spmd(nc, [{"in_" + n: a for n, a in arrays.items()}], core_ids=[0])
    return got.results[0]["out"]
```

```python
from contextlib import ExitStack, contextmanager

import numpy as np

import concourse.bass as bass
from concourse import mybir

F32 = mybir.dt.float32
BF16 = mybir.dt.bfloat16
I32 = mybir.dt.int32
U8 = mybir.dt.uint8
ALU = mybir.AluOpType
ACT = mybir.ActivationFunctionType
AX = mybir.AxisListType.X

P = 128
B = 8
DM = 256
DC = DM // P
EPS = 1e-5
NEG = -1e30
BIG = 3e38


class Tally:

    def __init__(self, sem, credit):
        self.sem, self.credit, self.base = sem, credit, 0

    def at(self, steps):
        return steps + (self.credit + self.base)


class Own:

    def __init__(self, eng, sem):
        self.eng, self.sem, self.start, self.k = eng, sem, 0, 0

    def up(self):
        self.k += 1
        return 1

    def now(self):
        return self.start + self.k

    @contextmanager
    def loop(self, count, per):
        base = self.start + self.k
        with self.eng.Fori(0, count) as i:
            self.start, self.k = (i * per + base if per else base), 0
            yield i
            assert self.k == per, (self.eng, self.k, per)
        self.start, self.k = base + count * per, 0


class Attention:

    def __init__(self, w, nw, wq, wk, wv, wo, scale, bq=None, bk=None, bv=None, bo=None, cos=None, sin=None,
                 causal=False, cross=False, gqa=False, rope=False):
        self.w, self.nw = w, nw
        self.wq, self.wk, self.wv, self.wo = wq, wk, wv, wo
        self.bq, self.bk, self.bv, self.bo = bq, bk, bv, bo
        self.cos, self.sin, self.scale = cos, sin, scale
        self.causal, self.cross, self.gqa, self.rope = causal, cross, gqa, rope
        self.nh, self.ns, self.per = (4, 1, 4) if gqa else (2, 2, 8)
        self.lead, self.near = (3, 2) if rope else (1, 1)


class FeedForward:

    def __init__(self, E, nf, gated, func, up, down, arrived, load=None, bias=None, keep=False, coef_rows=None):
        self.E, self.nf, self.gated, self.func, self.keep, self.coef_rows = E, nf, gated, func, keep, coef_rows
        self.up, self.down, self.arrived, self.load, self.bias = up, down, arrived, load, bias


def build(nc, D, out, stages):
    ctx = ExitStack()
    with ctx:
        def sb(name, shape, dt=F32):
            return ctx.enter_context(nc.sbuf_tensor(name, shape, dt))

        def sem(name):
            return ctx.enter_context(nc.semaphore(name))

        x = sb("x", [P, B, DM])
        ctxn = sb("ctxn", [P, B, DM])
        ctxT = sb("ctxT", [P, DC, B * P])
        xnT = sb("xnT", [P, DC, B * P])
        arena_a = sb("arena_a", [P, 16384])
        arena_b = sb("arena_b", [P, 16384])
        work = sb("work", [P, 9216])
        scrap = sb("scrap", [P, 1])
        ident = sb("ident", [P, P])
        ident16 = sb("ident16", [P, P], BF16)
        causal16 = sb("causal16", [P, P], BF16)
        bn = sb("bn", [P, B, 6])
        stat = sb("stat", [P, 6, B])
        small = sb("small", [P, 1024])

        pair_mask = sb("pair_mask", [P, P], U8)
        row_mask = sb("row_mask", [P, B, P], U8)

        psum = [ctx.enter_context(nc.psum_tensor(f"bank{i}", [P, 512], F32)) for i in range(8)]

        tallies = []

        def tally(name, credit=1):
            tallies.append(Tally(sem(name), credit))
            return tallies[-1]

        var_ready = tally("var_ready")
        std_ready = tally("std_ready")
        xn_ready = tally("xn_ready")
        xnt_ready = tally("xnt_ready", 4)
        xnt_done = tally("xnt_done", 4)
        slice_ready = tally("slice_ready")
        proj_ready = tally("proj_ready")
        proj_done = tally("proj_done", 3)
        scores_ready = tally("scores_ready", 2)
        max_ready = tally("max_ready")
        exp_done = tally("exp_done", 2)
        recip_ready = tally("recip_ready")
        probs_ready = tally("probs_ready")
        probsT_ready = tally("probsT_ready")
        probsT_done = tally("probsT_done")
        mix_ready = tally("mix_ready")
        mix_done = tally("mix_done")
        out_ready = tally("out_ready")
        out_done = tally("out_done")
        kpad_ready = tally("kpad_ready")
        aux_ready = tally("aux_ready")
        aux_done = tally("aux_done")
        aux2_ready = tally("aux2_ready")
        aux3_ready = tally("aux3_ready")
        aux4_ready = tally("aux4_ready")
        aux5_ready = tally("aux5_ready")
        aux6_ready = tally("aux6_ready")
        up_ready = tally("up_ready")
        gate_ready = tally("gate_ready")
        hidden_done = tally("hidden_done", 2)
        acc_ready = tally("acc_ready")
        acc_done = tally("acc_done", 2)
        codes_ready = tally("codes_ready")
        scale_ready = tally("scale_ready")
        top_ready = tally("top_ready")
        sign_ready = tally("sign_ready")
        weights_ready = tally("weights_ready")
        stage_done = tally("stage_done")
        loaded = {s: sem(f"loaded_{s}") for s in
                  ("x", "const", "rest", "ctx", "w0", "w0_0", "w0_1", "w0_2", "w0_3", "w1", "w2", "w3", "w5a", "w5b", "w6", "w7", "w8", "w8a", "w8b", "w9", "w11", "w11a", "w11b")}
        stored = sem("stored")
        passed = sem("passed")
        slot_numbers = sem("slot_numbers")
        one_hot_ready = sem("one_hot_ready")
        masks16_ready = sem("masks16_ready")
        credits_given = sem("credits_given")
        dve_own, act_own, pool_own = sem("dve_own"), sem("act_own"), sem("pool_own")
        pe, act, dve, pool, sp = nc.tensor, nc.scalar, nc.vector, nc.gpsimd, nc.sync
        V, A, G = Own(dve, dve_own), Own(act, act_own), Own(pool, pool_own)

        def stand_alone(eng):
            eng.sem_inc(passed, 1)

        def rows_(v, off, k, n):
            return v[:, off:off + k * n].rearrange("p (k n) -> p k n", k=k)

        xn4 = work[:, 5120:6144].rearrange("p (r n) -> p r n", r=4)

        def dve_stats(b, n=1):
            for t in range(n):
                dve.bn_stats(bn[:, b + t, :], x[:, b + t, :]).then_inc(dve_own, V.up())

        takes_stats = (0, 1, 3, 6, 7, 10)

        def dve_norm(s, natural=None):
            if done_before[s] == 0 or stages[done_before[s] - 1] not in takes_stats:
                with V.loop(B // 4, 4) as i:
                    for q in range(4):
                        dve_stats(i * 4 + q)
            dve.wait_ge(dve_own, V.now())
            mean, var, rstd, diff, sq, std = (stat[:, k, :] for k in range(6))
            dve.tensor_tensor(diff, bn[:, :, 1], bn[:, :, 4], ALU.subtract).then_inc(dve_own, V.up())
            dve.tensor_tensor(mean, bn[:, :, 1], bn[:, :, 4], ALU.add).then_inc(dve_own, V.up())
            dve.tensor_tensor(var, bn[:, :, 2], bn[:, :, 5], ALU.add).then_inc(dve_own, V.up())
            dve.wait_ge(dve_own, V.now())
            dve.tensor_tensor(sq, diff, diff, ALU.mult).then_inc(dve_own, V.up())
            dve.tensor_scalar(mean, mean, 0.5, None, ALU.mult).then_inc(dve_own, V.up())
            dve.tensor_scalar(var, var, 1.0 / DM, EPS, ALU.mult, ALU.add).then_inc(dve_own, V.up())
            dve.wait_ge(dve_own, V.now())
            dve.scalar_tensor_tensor(var, sq, 0.25, var, ALU.mult, ALU.add).then_inc(var_ready.sem, 1)
            dve.wait_ge(std_ready.sem, std_ready.at(1))
            dve.reciprocal(rstd, std).then_inc(dve_own, V.up())
            dve.wait_ge(dve_own, V.now())
            with V.loop(B // 4, 0) as i:
                for q in range(4):
                    b = i * 4 + q
                    if natural is None:
                        dve.wait_ge(xnt_ready.sem, xnt_ready.at(b - 3))
                        dst = xn4[:, q, :]
                    else:
                        dst = natural[:, b, :]
                    dve.tensor_scalar(dst, x[:, b, :], stat[:, 0, bass.ds(b, 1)], stat[:, 2, bass.ds(b, 1)],
                                      ALU.subtract, ALU.mult).then_inc(xn_ready.sem, 1)

        def act_norm(s, natural=None):
            act.wait_ge(var_ready.sem, var_ready.at(1))
            act.activation(stat[:, 5, :], stat[:, 1, :], ACT.Sqrt).then_inc(std_ready.sem, 1)
            if natural is None:
                with A.loop(B // 4, 0) as i:
                    for q in range(4):
                        b = i * 4 + q
                        act.wait_ge(xnt_ready.sem, xnt_ready.at(b + 1))
                        stand_alone(act)
                        act.activation(xnT[:, :, bass.ds(b * P, P)],
                                       psum[3 + q][:, 0:DM].rearrange("p (c t) -> p c t", c=DC),
                                       ACT.Copy).then_inc(xnt_done.sem, 1)

        def pe_norm(s, step=1):
            with pe.Fori(0, B // 4) as i:
                for q in range(4):
                    b = i * 4 + q
                    pe.wait_ge(xn_ready.sem, xn_ready.at(b + 1))
                    pe.wait_ge(xnt_done.sem, xnt_done.at(b - 3))
                    for c in range(DC):
                        rows = xn4[:, q, c::2] if step == 2 else xn4[:, q, c * P:(c + 1) * P]
                        last = pe.transpose(psum[3 + q][:, c * P:(c + 1) * P], rows, ident[:, :])
                    last.then_inc(xnt_ready.sem, 1)

        SC, TP, ZP, OP, PJ = psum[0:2], psum[2], psum[3], psum[4], psum[5:8]
        QG = work[:, 0:512].rearrange("p (j t) -> p j t", j=4)
        KG = work[:, 512:1024].rearrange("p (j t) -> p j t", j=4)
        QG2 = work[:, 7168:7680].rearrange("p (j t) -> p j t", j=4)
        KG2 = work[:, 7680:7808].rearrange("p (j t) -> p j t", j=1)
        VG = work[:, 1024:2048].rearrange("p (r n) -> p r n", r=2)
        VG4 = work[:, 1024:1536].rearrange("p (r n) -> p r n", r=4)
        PR = work[:, 2048:3072].rearrange("p (r n) -> p r n", r=2)
        PT = work[:, 3072:3584].rearrange("p (j t) -> p j t", j=4)
        ZS = work[:, 3584:4096]
        xb = work[:, 4096:4352].rearrange("p (c t) -> p c t", c=DC)
        cb = work[:, 4352:4608].rearrange("p (c t) -> p c t", c=DC)
        RT = [work[:, o:o + 512].rearrange("p (j t) -> p j t", j=4) for o in (4608, 6144)]
        KP = work[:, 5120:6144].rearrange("p (r n) -> p r n", r=2)
        nmax = small[:, 0:8].rearrange("p (r j) -> p r j", r=2)
        smax = small[:, 8:16].rearrange("p (r j) -> p r j", r=2)
        sums = small[:, 16:24].rearrange("p (r j) -> p r j", r=2)
        rsum = small[:, 24:32].rearrange("p (r j) -> p r j", r=2)

        def dve_max(u, r, nh, scale):
            dve.wait_ge(scores_ready.sem, scores_ready.at(u + 1))
            dve.tensor_reduce(nmax[:, r, 0:nh], SC[r][:, :].rearrange("p (j t) -> p j t", j=nh), AX, ALU.max,
                              negate=True).then_inc(dve_own, V.up())
            dve.wait_ge(dve_own, V.now())
            dve.tensor_scalar(smax[:, r, 0:nh], nmax[:, r, 0:nh], scale, None, ALU.mult).then_inc(max_ready.sem, 1)

        def act_exp(u, r, nh, scale, into=None):
            act.wait_ge(max_ready.sem, max_ready.at(u + 1))
            w = 512 // nh
            for j in range(nh):
                cols = slice(j * w, (j + 1) * w)
                last = act.activation(PR[:, r, cols], SC[r][:, cols], ACT.Exp, bias=smax[:, r, j:j + 1],
                                      scale=scale, accum_out=(sums[:, r, j:j + 1] if into is None else into[:, j:j + 1]))
            last.then_inc(exp_done.sem, 1)

        def dve_recip(u, r, nh):
            dve.wait_ge(exp_done.sem, exp_done.at(u + 1))
            dve.reciprocal(rsum[:, r, 0:nh], sums[:, r, 0:nh]).then_inc(recip_ready.sem, 1)

        def pool_normalise(u, r, nh):
            pool.wait_ge(recip_ready.sem, recip_ready.at(u + 1))
            w = 512 // nh
            probs = PR[:, r, :].rearrange("p (j t) -> p j t", j=nh)
            pool.tensor_tensor(probs, probs, rsum[:, r, 0:nh].unsqueeze(2).to_broadcast([P, nh, w]),
                               ALU.mult).then_inc(probs_ready.sem, 1)

        def pe_probsT(u, r):
            pe.wait_ge(probs_ready.sem, probs_ready.at(u + 1))
            pe.wait_ge(probsT_done.sem, probsT_done.at(u))
            for j in range(4):
                last = pe.transpose(TP[:, j * P:(j + 1) * P], PR[:, r, j * P:(j + 1) * P], ident[:, :])
            last.then_inc(probsT_ready.sem, 1)

        def dve_probsT(u):
            dve.wait_ge(probsT_ready.sem, probsT_ready.at(u + 1))
            dve.tensor_copy(work[:, 3072:3584], TP[:, :]).then_inc(probsT_done.sem, 1)

        x_pair = work[:, 4096:4608].rearrange("p (c t) -> p c t", c=DC)
        c_rows = work[:, 6656:7168].rearrange("p (c t) -> p c t", c=DC)

        def x_rows(c):
            return x_pair if c.ns == 2 else xb

        def heads_qk(c, n, g):
            if c.rope and g % 2:
                return QG2 if n == 0 else KG2
            return QG if n == 0 else KG

        def pe_attn128(s, c):
            xs_, src = x_rows(c), (c_rows if c.cross else x_rows(c))

            def project(b, u, g, n):
                if s == 0 and n == 0:
                    pe.wait_ge(loaded[f"w0_{g // 2}"], 16 * 4)
                if n == 0 and g == 0:
                    pe.wait_ge(slice_ready.sem, slice_ready.at(b + 1))
                pe.wait_ge(proj_done.sem, proj_done.at(u * 3 + n - 2))
                w, v = (c.wk, src) if n else (c.wq, xs_)
                nt = c.ns * P
                for j in range(1 if n and c.gqa else c.nh):
                    h = g if n and c.gqa else c.nh * g + j
                    for k in range(DC):
                        last = pe.matmul(PJ[n][:, j * nt:(j + 1) * nt], w[:, k, h * P:(h + 1) * P],
                                         v[:, k, :], start=(k == 0), stop=(k == DC - 1))
                last.then_inc(proj_ready.sem, 1)

            def values(u, g):
                pe.wait_ge(proj_done.sem, proj_done.at(u * 3))
                nv = P if c.gqa else c.nh * P
                for t in range(c.ns):
                    for k in range(DC):
                        last = pe.matmul(PJ[2][:, t * nv:(t + 1) * nv], src[:, k, t * P:(t + 1) * P],
                                         c.wv[:, k, g * nv:(g + 1) * nv], start=(k == 0), stop=(k == DC - 1))
                last.then_inc(proj_ready.sem, 1)

            def scores(u, g):
                pe.wait_ge(proj_done.sem, proj_done.at(u * 3 + 2))
                pe.wait_ge(exp_done.sem, exp_done.at(u - 1))
                if c.causal:
                    pe.matmul(SC[g % 2][:, :].rearrange("p (j t) -> p j t", j=4), ident16[:, :],
                              causal16[:, :].unsqueeze(1).to_broadcast([P, 4, P]), start=True, stop=False,
                              skip_group_check=True)
                q, kk = heads_qk(c, 0, g), heads_qk(c, 1, g)
                for j in range(4):
                    last = pe.matmul(SC[g % 2][:, j * P:(j + 1) * P], q[:, j, :], kk[:, 0 if c.gqa else j, :],
                                     start=not c.causal, stop=True, skip_group_check=True)
                last.then_inc(scores_ready.sem, 1)

            def step(b, g, last=False):
                u, near, far = b * c.per + g, (g + c.near) % c.per, (g + c.lead) % c.per
                projects, scored = not (last and g + c.lead >= c.per), not (last and g + c.near >= c.per)
                if projects:
                    project(b + 1, u + c.lead, far, 0)
                    if not c.rope:
                        project(b + 1, u + c.lead, far, 1)
                pe_probsT(u, g % 2)
                if projects:
                    if c.rope:
                        project(b + 1, u + c.lead, far, 1)
                    else:
                        values(u + c.lead, far)
                pe.wait_ge(proj_done.sem, proj_done.at(u * 3 + 3))
                pe.wait_ge(probsT_done.sem, probsT_done.at(u + 1))
                pe.wait_ge(mix_done.sem, mix_done.at(u))
                for j in range(4):
                    at = (j % c.ns * c.nh + j // c.ns) * P
                    vals = VG4[:, g, :] if c.gqa else VG[:, g % 2, at:at + P]
                    mm = pe.matmul(ZP[:, j * P:(j + 1) * P], vals, PT[:, j, :], start=True, stop=True)
                mm.then_inc(mix_ready.sem, 1)
                if projects and c.rope:
                    values(u + c.lead, far)
                if scored:
                    scores(u + c.near, near)
                pe.wait_ge(mix_done.sem, mix_done.at(u + 1))
                pe.wait_ge(out_done.sem, out_done.at(u))
                for t in range(c.ns):
                    for j in range(c.nh):
                        part = (j * c.ns + t) * P
                        mm = pe.matmul(OP[:, t * DM:(t + 1) * DM], ZS[:, part:part + P], c.wo[:, c.nh * g + j, :],
                                       start=(j == 0), stop=(j == c.nh - 1))
                mm.then_inc(out_ready.sem, 1)

            if s != 0:
                pe.wait_ge(loaded[c.w], 16 * c.nw)
            for u in range(c.lead):
                project(0, u, u, 0)
                project(0, u, u, 1)
                values(u, u)
            for u in range(c.near):
                scores(u, u)
            with pe.Fori(0, B // c.ns - 1) as b:
                for g in range(c.per):
                    step(b, g)
            for g in range(c.per):
                step(B // c.ns - 1, g, last=True)

        def dve_attn128(s, c):
            if s == 0:
                dve.wait_ge(loaded["w0"], 16 * 4)
            elif c.rope:
                dve.wait_ge(loaded[c.w], 16 * c.nw)
            if c.bo is not None:
                dve.wait_ge(xn_ready.sem, xn_ready.at(B))
                dve.tensor_tensor(x[:, :, :], x[:, :, :], c.bo.unsqueeze(1).to_broadcast([P, B, DM]),
                                  ALU.add).then_inc(dve_own, V.up())
                dve.wait_ge(dve_own, V.now())

            def qk(n, g):
                return (heads_qk(c, n, g), *((c.bq, 4) if n == 0 else (c.bk, 1 if c.gqa else 4)))

            def copy_qk(u, g, n):
                dst, bias, nj = qk(n, g)
                dve.wait_ge(proj_ready.sem, proj_ready.at(u * 3 + n + 1))
                bank = PJ[n][:, 0:nj * P].rearrange("p (j t) -> p j t", j=nj)
                if c.rope:
                    dve.wait_ge(scores_ready.sem, scores_ready.at(u - 1))
                    dve.wait_ge(aux2_ready.sem, aux2_ready.at(u * 2 + n + 1))
                    dve.tensor_tensor(dst[:, 0:nj, :], bank, c.cos.unsqueeze(1).to_broadcast([P, nj, P]),
                                      ALU.mult).then_inc(dve_own, V.up())
                elif bias is None:
                    dve.tensor_copy(dst[:, 0:nj, :], bank).then_inc(proj_done.sem, 1)
                else:
                    heads = "p j t -> p (j t)"
                    dve.tensor_tensor(dst[:, 0:nj, :].rearrange(heads).rearrange("p (h n) -> p h n", h=c.nh),
                                      bank.rearrange(heads).rearrange("p (h n) -> p h n", h=c.nh),
                                      bias[:, c.nh * g:c.nh * g + c.nh].unsqueeze(2).to_broadcast([P, c.nh, c.ns * P]),
                                      ALU.add).then_inc(proj_done.sem, 1)

            def add_rotated(u, g):
                dve.wait_ge(dve_own, V.now())
                for n in range(2):
                    dst, _, nj = qk(n, g)
                    dve.wait_ge(aux_ready.sem, aux_ready.at(u * 2 + n + 1))
                    dve.tensor_tensor(dst[:, 0:nj, :], dst[:, 0:nj, :], RT[n][:, 0:nj, :],
                                      ALU.add).then_inc(proj_done.sem, 1)

            def copy_values(u, g):
                dve.wait_ge(proj_ready.sem, proj_ready.at(u * 3 + 3))
                nv = P if c.gqa else c.nh * P
                bank = PJ[2][:, 0:nv * c.ns]
                if c.bv is None:
                    dve.tensor_copy(VG4[:, g, :] if c.gqa else VG[:, g % 2, :], bank).then_inc(proj_done.sem, 1)
                else:
                    seqs = "p (t n) -> p t n"
                    dve.tensor_tensor(VG[:, g % 2, :].rearrange(seqs, t=c.ns), bank.rearrange(seqs, t=c.ns),
                                      c.bv[:, g * nv:(g + 1) * nv].unsqueeze(1).to_broadcast([P, c.ns, nv]),
                                      ALU.add).then_inc(proj_done.sem, 1)

            def step(b, g, last=False):
                u, near, far = b * c.per + g, (g + c.near) % c.per, (g + c.lead) % c.per
                projects, scored = not (last and g + c.lead >= c.per), not (last and g + c.near >= c.per)
                if projects and not c.rope:
                    copy_qk(u + c.lead, far, 0)
                    copy_qk(u + c.lead, far, 1)
                dve_probsT(u)
                if projects:
                    if c.rope:
                        copy_qk(u + c.lead, far, 0)
                        copy_qk(u + c.lead, far, 1)
                        add_rotated(u + c.lead, far)
                    copy_values(u + c.lead, far)
                if scored:
                    dve_max(u + c.near, near % 2, 4, c.scale)
                    dve_recip(u + c.near, near % 2, 4)
                dve.wait_ge(out_ready.sem, out_ready.at(u + 1))
                seqs = x[:, bass.ds(b * c.ns, c.ns), :]
                dve.tensor_tensor(seqs, seqs, OP[:, 0:c.ns * DM].rearrange("p (t n) -> p t n", t=c.ns),
                                  ALU.add).then_inc(out_done.sem, 1)
                if g == c.per - 1:
                    dve.wait_ge(out_done.sem, out_done.at((b + 1) * c.per))
                    dve_stats(b * c.ns, c.ns)
                if last and s == 0 and 2 in stages and g < 2:
                    dve_slot_numbers(g)

            for u in range(c.lead):
                copy_qk(u, u, 0)
                copy_qk(u, u, 1)
                if c.rope:
                    add_rotated(u, u)
                copy_values(u, u)
            for u in range(c.near):
                dve_max(u, u, 4, c.scale)
                dve_recip(u, u, 4)
            with V.loop(B // c.ns - 1, c.per * (3 if c.rope else 1) + c.ns) as b:
                for g in range(c.per):
                    step(b, g)
            for g in range(c.per):
                step(B // c.ns - 1, g, last=True)

        def act_attn128(s, c):
            def rotate(u, n):
                nj = 1 if n else 4
                act.wait_ge(proj_ready.sem, proj_ready.at(u * 3 + n + 1))
                act.wait_ge(proj_done.sem, proj_done.at(u * 3 + n - 2))
                act.activation(RT[n][0:64, 0:nj, :], PJ[n][64:128, 0:nj * P].rearrange("p (j t) -> p j t", j=nj),
                               ACT.Copy)
                act.activation(RT[n][64:128, 0:nj, :], PJ[n][0:64, 0:nj * P].rearrange("p (j t) -> p j t", j=nj),
                               ACT.Copy).then_inc(aux2_ready.sem, 1)

            def step(b, g, last=False):
                u, near = b * c.per + g, (g + c.near) % c.per
                rotates = c.rope and not (last and g + c.lead >= c.per)
                if rotates:
                    rotate(u + c.lead, 0)
                    rotate(u + c.lead, 1)
                act.wait_ge(mix_ready.sem, mix_ready.at(u + 1))
                act.activation(ZS, ZP[:, :], ACT.Copy).then_inc(mix_done.sem, 1)
                if not (last and g + c.near >= c.per):
                    act_exp(u + c.near, near % 2, 4, c.scale)

            if c.rope:
                for u in range(c.lead):
                    rotate(u, 0)
                    rotate(u, 1)
            for u in range(c.near):
                act_exp(u, u, 4, c.scale)
            with A.loop(B // c.ns - 1, 0) as b:
                for g in range(c.per):
                    step(b, g)
            for g in range(c.per):
                step(B // c.ns - 1, g, last=True)

        def pool_attn128(s, c):
            def slices(b):
                toks = bass.ds(b * c.ns * P, c.ns * P)
                if c.cross:
                    pool.tensor_copy(c_rows, ctxT[:, :, toks]).then_inc(pool_own, G.up())
                    pool.wait_ge(pool_own, G.now())
                if isinstance(b, int):
                    pool.wait_ge(xnt_done.sem, xnt_done.at(c.ns))
                pool.tensor_copy(x_rows(c), xnT[:, :, toks]).then_inc(slice_ready.sem, 1)

            def times_sines(u):
                for n, nj in ((0, 4), (1, 1)):
                    pool.wait_ge(aux2_ready.sem, aux2_ready.at(u * 2 + n + 1))
                    pool.tensor_tensor(RT[n][:, 0:nj, :], RT[n][:, 0:nj, :], c.sin.unsqueeze(1).to_broadcast([P, nj, P]),
                                       ALU.mult).then_inc(aux_ready.sem, 1)

            slices(0)
            if c.rope:
                for u in range(c.lead):
                    times_sines(u)
            for u in range(c.near):
                pool_normalise(u, u, 4)
            with G.loop(B // c.ns - 1, 1 if c.cross else 0) as b:
                for g in range(c.per):
                    if c.rope:
                        times_sines(b * c.per + g + c.lead)
                    if g == c.per - 1 - c.lead:
                        pool.wait_ge(proj_ready.sem, proj_ready.at((b + 1) * 3 * c.per))
                        slices(b + 1)
                    pool_normalise(b * c.per + g + c.near, (g + c.near) % 2, 4)
            for g in range(c.per - c.near):
                u = (B // c.ns - 1) * c.per + g
                if c.rope and g + c.lead < c.per:
                    times_sines(u + c.lead)
                pool_normalise(u + c.near, (g + c.near) % 2, 4)

        QB = work[:, 6656:6912].rearrange("p (c t) -> p c t", c=2)
        KB = work[:, 6912:7168].rearrange("p (c t) -> p c t", c=2)
        VB = work[:, 7168:7232]
        ZB = work[:, 7232:7488]
        ZT = work[:, 7488:7744].rearrange("p (c t) -> p c t", c=2)
        PT2 = [work[:, o:o + 512].rearrange("p (j t) -> p j t", j=4) for o in (3072, 7744)]
        heads8 = sb("heads8", [P, 16])
        heads16 = sb("heads16", [P, 8])
        mask16 = sb("mask16", [P, B, P], BF16)
        SC4, SH = (psum[0], psum[1], psum[4], psum[6]), psum[7]
        PR4 = work[:, 0:2048].rearrange("p (r n) -> p r n", r=4)
        nmax4 = work[:, 8320:8336].rearrange("p (r j) -> p r j", r=4)
        smax4 = work[:, 8336:8352].rearrange("p (r j) -> p r j", r=4)
        sums32 = work[:, 8256:8288]
        rsum32 = work[:, 8288:8320]
        natural = xnT[:, :, :].rearrange("p c n -> p (c n)").rearrange("p (b d) -> p b d", b=B)

        def pe_small(s, c):
            def project(b, first):
                if c is None:
                    return
                pe.wait_ge(slice_ready.sem, slice_ready.at(b + 1))
                src = cb if c.cross else xb
                pe.wait_ge(proj_done.sem, proj_done.at(b * 3 - 1))
                for n, (w, v) in enumerate(((c.wq, xb), (c.wk, src))):
                    for m in range(2):
                        for k in range(DC):
                            last = pe.matmul(PJ[0][:, (2 * n + m) * P:(2 * n + m + 1) * P],
                                             w[:, k, m * P:(m + 1) * P], v[:, k, :],
                                             start=(k == 0), stop=(k == DC - 1))
                last.then_inc(proj_ready.sem, 1)
                if not first:
                    pe.wait_ge(out_done.sem, out_done.at(b - 1))
                for k in range(DC):
                    last = pe.matmul(SH[:, 0:64], src[:, k, :], c.wv[:, k, :], start=(k == 0), stop=(k == DC - 1))
                last.then_inc(proj_ready.sem, 1)

            def scores(b, g, first):
                u = b * 8 + g
                if c is not None:
                    pe.wait_ge(proj_done.sem, proj_done.at(b * 3 + 2))
                pe.wait_ge(kpad_ready.sem, kpad_ready.at(u + 1))
                if not first or g >= 4:
                    pe.wait_ge(exp_done.sem, exp_done.at(u - 3))
                if c is None:
                    for m in range(2):
                        last = pe.matmul(SC4[g % 4][:, m * DM:(m + 1) * DM].unsqueeze(1), KP[:, g % 2, m * P:(m + 1) * P],
                                         ctxn[:, bass.ds(b, 1), :], start=True, stop=True)
                    last.then_inc(scores_ready.sem, 1)
                    return
                mask = causal16[:, :].unsqueeze(1) if c.causal else mask16[:, bass.ds(b, 1), :]
                pe.matmul(SC4[g % 4][:, :].rearrange("p (j t) -> p j t", j=4), ident16[:, :],
                          mask.to_broadcast([P, 4, P]), start=True, stop=False)
                pe.matmul(SC4[g % 4][:, :], QB[:, g // 4, :], KP[:, g % 2, :],
                          start=False, stop=True).then_inc(scores_ready.sem, 1)

            def transposed(b, g):
                u = b * 8 + g
                pe.wait_ge(exp_done.sem, exp_done.at(u + 1))
                pe.wait_ge(probsT_done.sem, probsT_done.at(u))
                for j in range(4):
                    last = pe.transpose(TP[:, j * P:(j + 1) * P], PR4[:, g % 4, j * P:(j + 1) * P], ident[:, :])
                last.then_inc(probsT_ready.sem, 1)

            def mix(b, g):
                u = b * 8 + g
                pe.wait_ge(probsT_done.sem, probsT_done.at(u + 1))
                if g == 0:
                    pe.wait_ge(mix_done.sem, mix_done.at(b))
                    if c is not None:
                        pe.wait_ge(proj_done.sem, proj_done.at(b * 3 + 3))
                for j in range(4):
                    if c is None:
                        m, k = j // 2, j % 2
                        last = pe.matmul(ZP[:, m * P + 16 * g:m * P + 16 * g + 16], PT2[g % 2][:, j, :],
                                         ctxT[:, k, bass.ds(b * P + 16 * g, 16)], start=(k == 0), stop=(k == 1))
                    else:
                        h = 4 * g + j
                        last = pe.matmul(ZP[:, h * 8:h * 8 + 8], PT2[g % 2][:, j, :], VB[:, g * 8:g * 8 + 8],
                                         start=True, stop=True)
                last.then_inc(mix_ready.sem, 1)

            def result_transposed(b):
                pe.wait_ge(mix_done.sem, mix_done.at(b + 1))
                pe.wait_ge(out_done.sem, out_done.at(b))
                if c is not None and b is not last_seq:
                    pe.wait_ge(proj_done.sem, proj_done.at(b * 3 + 6))
                for k in range(2):
                    last = pe.transpose(SH[:, k * P:(k + 1) * P], ZB[:, k * P:(k + 1) * P], ident[:, :])
                last.then_inc(out_ready.sem if c is None else aux_ready.sem, 1)

            def output(b):
                if c is None:
                    return
                pe.wait_ge(aux_done.sem, aux_done.at(b + 1))
                for k in range(2):
                    last = pe.matmul(SH[:, 0:DM], ZT[:, k, :], c.wo[:, k, :], start=(k == 0), stop=(k == 1))
                last.then_inc(out_ready.sem, 1)

            def earlier(b, g, n):
                return (b, g - n) if g >= n else (b - 1, g + 8 - n)

            def body(b, first=False):
                project(b, first)
                for g in range(8):
                    if not first or g >= 3:
                        transposed(*earlier(b, g, 3))
                    if not first or g >= 4:
                        mix(*earlier(b, g, 4))
                    if not first and g == 4:
                        result_transposed(b - 1)
                    if not first and g == 5:
                        output(b - 1)
                    scores(b, g, first)

            last_seq = B - 1
            if c is not None:
                pe.wait_ge(loaded[c.w], 16 * c.nw)
            body(0, first=True)
            with pe.Fori(0, B - 1) as i:
                body(i + 1)
            for g in (5, 6, 7):
                transposed(last_seq, g)
                mix(last_seq, g - 1)
            mix(last_seq, 7)
            result_transposed(last_seq)
            output(last_seq)

        def dve_small(s, c):
            nh = 2 if c is None else 4
            scale = 0.25 if c is None else c.scale
            dve.wait_ge(xn_ready.sem, xn_ready.at(B))
            if c is not None and c.bo is not None:
                dve.tensor_tensor(x[:, :, :], x[:, :, :], c.bo.unsqueeze(1).to_broadcast([P, B, DM]),
                                  ALU.add).then_inc(dve_own, V.up())
                dve.wait_ge(dve_own, V.now())

            def copy_qk(b):
                dve.wait_ge(proj_ready.sem, proj_ready.at(b * 2 + 1))
                for n, (dst, bias) in enumerate(((QB, c.bq), (KB, c.bk))):
                    bank = PJ[0][:, 2 * n * P:2 * (n + 1) * P].rearrange("p (c t) -> p c t", c=2)
                    if bias is None:
                        dve.tensor_copy(dst, bank).then_inc(proj_done.sem, 1)
                    else:
                        dve.tensor_tensor(dst, bank, bias.unsqueeze(2).to_broadcast([P, 2, P]),
                                          ALU.add).then_inc(proj_done.sem, 1)

            def copy_values(b):
                dve.wait_ge(proj_ready.sem, proj_ready.at(b * 2 + 2))
                if c.bv is None:
                    dve.tensor_copy(VB, SH[:, 0:64]).then_inc(proj_done.sem, 1)
                else:
                    dve.tensor_tensor(VB, SH[:, 0:64], c.bv, ALU.add).then_inc(proj_done.sem, 1)

            def copy_transposed(u, g):
                dve.wait_ge(probsT_ready.sem, probsT_ready.at(u + 1))
                dve.tensor_copy(PT2[g % 2].rearrange("p j t -> p (j t)"), TP[:, :]).then_inc(probsT_done.sem, 1)

            def maxima(u, g):
                r = g % 4
                dve.wait_ge(scores_ready.sem, scores_ready.at(u + 1))
                dve.tensor_reduce(nmax4[:, r, 0:nh], SC4[r][:, :].rearrange("p (j t) -> p j t", j=nh), AX, ALU.max,
                                  negate=True).then_inc(dve_own, V.up())
                dve.wait_ge(dve_own, V.now())
                dve.tensor_scalar(smax4[:, r, 0:nh], nmax4[:, r, 0:nh], scale, None,
                                  ALU.mult).then_inc(max_ready.sem, 1)

            def invert_sums(b):
                dve.wait_ge(exp_done.sem, exp_done.at(b * 8 + 8))
                dve.reciprocal(rsum32[:, 0:8 * nh], sums32[:, 0:8 * nh]).then_inc(dve_own, V.up())

            def divide(b):
                dve.wait_ge(mix_ready.sem, mix_ready.at(b * 8 + 8))
                dve.wait_ge(dve_own, V.now())
                if c is None:
                    view = "p (m h n) -> p m h n"
                    dve.tensor_tensor(ZB.rearrange(view, m=2, h=8), ZP[:, 0:DM].rearrange(view, m=2, h=8),
                                      rsum32[:, 0:16].rearrange("p (h m) -> p m h", m=2).unsqueeze(3)
                                      .to_broadcast([P, 2, 8, 16]), ALU.mult).then_inc(mix_done.sem, 1)
                else:
                    view = "p (h n) -> p h n"
                    dve.tensor_tensor(ZB.rearrange(view, h=32), ZP[:, 0:DM].rearrange(view, h=32),
                                      rsum32.unsqueeze(2).to_broadcast([P, 32, 8]), ALU.mult).then_inc(mix_done.sem, 1)

            def copy_result(b):
                if c is not None:
                    dve.wait_ge(aux_ready.sem, aux_ready.at(b + 1))
                    dve.tensor_copy(ZT, SH[:, 0:DM].rearrange("p (c t) -> p c t", c=2)).then_inc(aux_done.sem, 1)

            def add_out(b):
                dve.wait_ge(out_ready.sem, out_ready.at(b + 1))
                dve.tensor_tensor(x[:, b, :], x[:, b, :], SH[:, 0:DM],
                                  ALU.add).then_inc(out_done.sem, 1)

            def body(b, first=False):
                if c is not None:
                    copy_qk(b)
                if not first:
                    invert_sums(b - 1)
                for g in range(8):
                    if not first or g >= 3:
                        copy_transposed(b * 8 + g - 3, g - 3)
                    if not first and g == 3:
                        divide(b - 1)
                    if c is not None and g == 3:
                        copy_values(b)
                    if not first and g == 4:
                        copy_result(b - 1)
                    if not first and g == 5:
                        add_out(b - 1)
                    if not first and g == 6:
                        dve.wait_ge(out_done.sem, out_done.at(b))
                        dve_stats(b - 1)
                    maxima(b * 8 + g, g)

            body(0, first=True)
            with V.loop(B - 1, 10) as i:
                body(i + 1)
            last_seq = B - 1
            for g in (5, 6, 7):
                copy_transposed(last_seq * 8 + g, g)
            invert_sums(last_seq)
            divide(last_seq)
            copy_result(last_seq)
            add_out(last_seq)
            dve.wait_ge(out_done.sem, out_done.at(B))
            dve_stats(last_seq)

        def act_small(s, c):
            nh = 2 if c is None else 4
            scale, w = 0.25 if c is None else c.scale, 512 // nh
            with A.loop(B, 0) as b:
                for g in range(8):
                    act.wait_ge(max_ready.sem, max_ready.at(b * 8 + g + 1))
                    for j in range(nh):
                        cols = slice(j * w, (j + 1) * w)
                        last = act.activation(PR4[:, g % 4, cols], SC4[g % 4][:, cols], ACT.Exp,
                                              bias=smax4[:, g % 4, j:j + 1], scale=scale,
                                              accum_out=sums32[:, g * nh + j:g * nh + j + 1])
                    last.then_inc(exp_done.sem, 1)

        def pool_small(s, c):
            def slices(b):
                if c.cross:
                    pool.tensor_copy(cb, ctxT[:, :, bass.ds(b * P, P)]).then_inc(pool_own, G.up())
                    pool.wait_ge(pool_own, G.now())
                pool.tensor_copy(xb, xnT[:, :, bass.ds(b * P, P)]).then_inc(slice_ready.sem, 1)

            def kpad(b, g):
                if c is not None and g == 0:
                    pool.wait_ge(proj_done.sem, proj_done.at(b * 3 + 2))
                pool.wait_ge(scores_ready.sem, scores_ready.at(b * 8 + g - 1))
                if c is None:
                    if g == 0:
                        pool.wait_ge(xn_ready.sem, xn_ready.at(b + 1))
                    stand_alone(pool)
                    pool.tensor_tensor(KP[:, g % 2, 0:DM], natural[:, b, :], heads16[:, g:g + 1].to_broadcast([P, DM]),
                                       ALU.mult).then_inc(kpad_ready.sem, 1)
                else:
                    pool.tensor_tensor(KP[:, g % 2, :].rearrange("p (j t) -> p j t", j=4),
                                       KB[:, g // 4, :].unsqueeze(1).to_broadcast([P, 4, P]),
                                       heads8[:, 4 * (g % 4):4 * (g % 4) + 4].unsqueeze(2).to_broadcast([P, 4, P]),
                                       ALU.mult).then_inc(kpad_ready.sem, 1)

            if c is not None:
                pool.wait_ge(xnt_done.sem, xnt_done.at(1))
                slices(0)
            with G.loop(B - 1, 1 if c is not None and c.cross else 0) as b:
                for g in range(8):
                    kpad(b, g)
                    if g == 5 and c is not None:
                        pool.wait_ge(proj_ready.sem, proj_ready.at(b * 2 + 2))
                        slices(b + 1)
            for g in range(8):
                kpad(B - 1, g)

        valid = small[:, 64:72]

        def pe_memory(s):
            pe.wait_ge(aux2_ready.sem, aux2_ready.at(1))
            for u in range(2):
                for j in range(4):
                    b = 4 * u + j
                    for k in range(DC):
                        pe.matmul(SC[u][:, j * P:(j + 1) * P], xnT[:, k, b * P:(b + 1) * P],
                                  ctxT[:, k, b * P:(b + 1) * P], start=(k == 0), stop=False)
                    last = pe.matmul(SC[u][:, j * P:(j + 1) * P], ident16[:, :], mask16[:, b, :],
                                     start=False, stop=True)
                last.then_inc(scores_ready.sem, 1)
            for u in range(2):
                pe_probsT(u, u)
                pe.wait_ge(probsT_done.sem, probsT_done.at(u + 1))
                for half in range(2):
                    bank = (ZP, OP, PJ[0], PJ[1])[2 * u + half]
                    for j in range(2):
                        b = 4 * u + 2 * half + j
                        last = pe.matmul(bank[:, j * DM:(j + 1) * DM], PT[:, 2 * half + j, :], ctxn[:, b, :],
                                         start=True, stop=True)
                last.then_inc(out_ready.sem, 1)

        def dve_memory(s):
            for u in range(2):
                dve_max(u, u, 4, DM ** -0.5)
            for u in range(2):
                dve_recip(u, u, 4)
            for u in range(2):
                dve_probsT(u)
            for u in range(2):
                dve.wait_ge(out_ready.sem, out_ready.at(u + 1))
                for half in range(2):
                    bank = (ZP, OP, PJ[0], PJ[1])[2 * u + half]
                    for j in range(2):
                        b = 4 * u + 2 * half + j
                        dve.scalar_tensor_tensor(x[:, b, :], bank[:, j * DM:(j + 1) * DM], valid[:, b:b + 1],
                                                 x[:, b, :], ALU.mult, ALU.add).then_inc(out_done.sem, 1)

        def act_memory(s):
            for u in range(2):
                act_exp(u, u, 4, DM ** -0.5)

        def pool_memory(s):
            for u in range(2):
                pool_normalise(u, u, 4)

        lg = work[:, 7296:7424].rearrange("p (b e) -> p b e", b=B)
        coef = small[:, 96:256].rearrange("p (b e) -> p b e", b=B)
        tri = rows_(arena_b, 15360, 16, 16)
        pair = work[:, 0:2048]
        tied = work[:, 2048:4096]
        rank = work[:, 7424:7552].rearrange("p (b e) -> p b e", b=B)
        peak = small[:, 72:80]
        denom = small[:, 80:88]

        def pe_route(E, w, sgate=None):
            for b in range(B):
                for k in range(DC):
                    last = pe.matmul(PJ[0][:, b * E:(b + 1) * E], xnT[:, k, b * P:(b + 1) * P], w[:, k, :],
                                     start=(k == 0), stop=(k == DC - 1))
            if sgate is not None:
                for b in range(B):
                    for k in range(DC):
                        last = pe.matmul(PJ[1][:, b:b + 1], xnT[:, k, b * P:(b + 1) * P], sgate[:, k, :],
                                         start=(k == 0), stop=(k == DC - 1))
            last.then_inc(aux2_ready.sem, 1)

        def dve_route(E, k, clip=None, bias=None, alpha=None, over_all=False):
            dve.wait_ge(aux2_ready.sem, aux2_ready.at(1))
            L = lg[:, :, 0:E]
            bank = PJ[0][:, 0:B * E].rearrange("p (b e) -> p b e", b=B)
            if clip is not None:
                dve.tensor_scalar(L, bank, clip, -clip, ALU.min, ALU.max).then_inc(dve_own, V.up())
            elif bias is not None:
                dve.tensor_tensor(L, bank, bias.unsqueeze(1).to_broadcast([P, B, E]), ALU.add).then_inc(dve_own, V.up())
            else:
                dve.tensor_copy(L, bank).then_inc(dve_own, V.up())
            dve.wait_ge(dve_own, V.now())
            four = [P, B, E, E]
            pairs, ties = (t[:, 0:B * E * E].rearrange("p (b e j) -> p b e j", b=B, e=E) for t in (pair, tied))
            other, own = L.unsqueeze(2).to_broadcast(four), L.unsqueeze(3).to_broadcast(four)
            flat = [t[:, 0:B * E * E] for t in (pair, tied)]
            dve.tensor_tensor(pairs, other, own, ALU.is_gt).then_inc(dve_own, V.up())
            dve.tensor_tensor(ties, other, own, ALU.is_equal).then_inc(dve_own, V.up())
            dve.tensor_reduce(peak, L, AX, ALU.max).then_inc(dve_own, V.up())
            dve.wait_ge(dve_own, V.now())
            dve.tensor_tensor(ties, ties, tri[:, 0:E, 0:E].unsqueeze(1).to_broadcast(four),
                              ALU.mult).then_inc(dve_own, V.up())
            dve.tensor_tensor(L, L, peak.unsqueeze(2).to_broadcast([P, B, E]), ALU.subtract).then_inc(aux3_ready.sem, 1)
            dve.wait_ge(dve_own, V.now())
            dve.tensor_tensor(flat[0], flat[0], flat[1], ALU.add).then_inc(dve_own, V.up())
            dve.wait_ge(dve_own, V.now())
            R = rank[:, :, 0:E]
            dve.tensor_reduce(R, pairs, AX, ALU.add).then_inc(dve_own, V.up())
            dve.wait_ge(dve_own, V.now())
            dve.tensor_scalar(R, R, float(k), None, ALU.is_lt).then_inc(dve_own, V.up())
            dve.wait_ge(aux4_ready.sem, aux4_ready.at(1))
            if over_all:
                dve.tensor_reduce(denom, L, AX, ALU.add).then_inc(dve_own, V.up())
            dve.wait_ge(dve_own, V.now())
            C = coef[:, :, 0:E]
            dve.tensor_tensor(C, L, R, ALU.mult).then_inc(dve_own, V.up())
            dve.wait_ge(dve_own, V.now())
            if not over_all:
                dve.tensor_reduce(denom, C, AX, ALU.add).then_inc(dve_own, V.up())
                dve.wait_ge(dve_own, V.now())
            dve.reciprocal(denom, denom).then_inc(dve_own, V.up())
            dve.wait_ge(dve_own, V.now())
            dve.tensor_tensor(C, C, denom.unsqueeze(2).to_broadcast([P, B, E]), ALU.mult).then_inc(dve_own, V.up())
            dve.wait_ge(dve_own, V.now())
            if alpha is not None:
                dve.tensor_tensor(C, C, alpha.unsqueeze(1).to_broadcast([P, B, E]), ALU.mult).then_inc(dve_own, V.up())
                dve.wait_ge(dve_own, V.now())

        def act_route(E):
            act.wait_ge(aux3_ready.sem, aux3_ready.at(1))
            act.activation(lg[:, :, 0:E], lg[:, :, 0:E], ACT.Exp).then_inc(aux4_ready.sem, 1)

        coefT = work[0:B, 8192:9216]

        def pe_coefT(E, banks):
            pe.wait_ge(aux5_ready.sem, aux5_ready.at(1))
            for b in range(B):
                last = pe.transpose(banks[b // 4][0:E, (b % 4) * P:(b % 4 + 1) * P], coef[:, b, 0:E], ident[:, :])
            last.then_inc(aux6_ready.sem, 1)

        NS = 2048
        gatewT = rows_(arena_b, 14848, 2, 8)
        WT = rows_(arena_b, 2048, 2, DM)
        atoms = arena_b[0:64, 2560:4608]
        slots = arena_b[0:8, 4608:6656]
        gather = rows_(arena_b, 6656, 2, NS)
        scatter = rows_(arena_b, 10752, 16, DM)
        eaw = arena_b[0:8, 14864:14928]
        eawT = arena_b[0:64, 14928:14936]
        colsi = arena_b[:, 10752:12800].bitcast(I32)
        colsf = gather[:, 1, :]
        rowsi = small[:, 512:528].bitcast(I32)
        rowsf = small[:, 528:544]
        iotaf = arena_b[:, 15104:15360]
        iotap = sb("iotap", [P, 2])
        em = small[0:8, 88:92]
        xv = work[:, 4096:5120].rearrange("p (r n) -> p r n", r=2)
        xg = work[:, 5120:6144].rearrange("p (r n) -> p r n", r=2)

        def dve_slot_numbers(piece):
            if piece == 0:
                dve.wait_ge(loaded["w2"], 16 * 7)
                dve.tensor_scalar(rowsi, rowsi, 8, None, ALU.arith_shift_right).then_inc(dve_own, V.up())
                dve.tensor_scalar(colsi, colsi, DM - 1, None, ALU.bitwise_and).then_inc(dve_own, V.up())
            else:
                dve.wait_ge(dve_own, V.now())
                dve.tensor_copy(rowsf, rowsi).then_inc(slot_numbers, 1)
                dve.tensor_copy(colsf, colsi).then_inc(slot_numbers, 1)

        def pool_gather():
            pool.wait_ge(slot_numbers, 2)
            for k in range(DC):
                last = pool.tensor_scalar(gather[:, k, :], colsf, iotap[:, k:k + 1], None, ALU.is_equal)
            last.then_inc(one_hot_ready, 1)

        def pool_scatter():
            pool.wait_ge(one_hot_ready, 1)
            for i in range(NS // P):
                last = pool.tensor_scalar(scatter[:, i, :], iotaf[:, :], rowsf[:, i:i + 1], None, ALU.is_equal)
            last.then_inc(one_hot_ready, 1)

        def dve_slots_prepare():
            dve.wait_ge(loaded["w2"], 16 * 7)
            dve.tensor_reduce(em[:, 0:1], eaw, AX, ALU.max, negate=True).then_inc(aux_ready.sem, 1)
            dve.wait_ge(aux_done.sem, aux_done.at(1))
            dve.reciprocal(em[:, 2:3], em[:, 1:2]).then_inc(dve_own, V.up())
            dve.wait_ge(dve_own, V.now())
            dve.tensor_scalar(eaw, eaw, em[:, 2:3], None, ALU.mult).then_inc(slice_ready.sem, 1)
            dve.wait_ge(proj_ready.sem, proj_ready.at(1))
            dve.tensor_copy(eawT, TP[0:64, 0:8]).then_inc(slice_ready.sem, 1)
            dve.wait_ge(aux_done.sem, aux_done.at(2))
            for i in range(4):
                dve.wait_ge(proj_ready.sem, proj_ready.at(i + 2))
                dve.tensor_tensor(slots[:, i * 512:(i + 1) * 512], (SC[0], SC[1], TP, ZP)[i][0:8, :],
                                  slots[:, i * 512:(i + 1) * 512], ALU.mult).then_inc(proj_done.sem, 1)

        def act_slots_prepare():
            act.wait_ge(aux_ready.sem, aux_ready.at(1))
            act.activation(eaw, eaw, ACT.Exp, bias=em[:, 0:1], accum_out=em[:, 1:2]).then_inc(aux_done.sem, 1)
            act.activation(slots, slots, ACT.Sigmoid).then_inc(aux_done.sem, 1)

        def pe_slots_prepare():
            pe.wait_ge(slice_ready.sem, slice_ready.at(1))
            pe.transpose(TP[0:64, 0:8], eaw, ident[0:8, 0:8]).then_inc(proj_ready.sem, 1)
            pe.wait_ge(slice_ready.sem, slice_ready.at(2))
            for i in range(4):
                pe.matmul((SC[0], SC[1], TP, ZP)[i][0:8, :], eawT, atoms[:, i * 512:(i + 1) * 512],
                          start=True, stop=True).then_inc(proj_ready.sem, 1)
            pe.wait_ge(proj_done.sem, proj_done.at(4))

        def pe_slots():
            for b in range(B):
                bank = (ZP, OP, PJ[1], PJ[2])[b // 2]
                for k in range(DC):
                    last = pe.matmul(bank[:, (b % 2) * DM:(b % 2 + 1) * DM], xnT[:, k, b * P:(b + 1) * P],
                                     WT[:, k, :], start=(k == 0), stop=(k == DC - 1))
            last.then_inc(out_ready.sem, 1)
            pe_coefT(8, (TP, PJ[0]))
            pe.wait_ge(one_hot_ready, 2)
            GX, VL, ACC = (psum[0], psum[1]), (psum[2], psum[3]), psum[4:6]

            def scatter_out(h, i):
                u = h * 16 + i
                pe.wait_ge(probs_ready.sem, probs_ready.at(u + 1))
                for t in range(4):
                    last = pe.matmul(ACC[t // 2][:, (t % 2) * DM:(t % 2 + 1) * DM], xg[:, i % 2, t * P:(t + 1) * P],
                                     scatter[:, i, :], start=(i == 0 and t % 2 == 0), stop=(i == 15),
                                     skip_group_check=True)
                last.then_inc(mix_ready.sem, 1)

            with pe.Fori(0, 2) as h:
                for i in range(16):
                    u = h * 16 + i
                    if i >= 2:
                        pe.wait_ge(probs_ready.sem, probs_ready.at(u - 1))
                    for k in range(DC):
                        pe.matmul(GX[i % 2][:, :], gather[:, k, i * P:(i + 1) * P],
                                  xnT[:, k, bass.ds(h * 512, 512)], start=(k == 0), stop=(k == DC - 1))
                    if i == 0:
                        pe.wait_ge(slice_ready.sem, slice_ready.at(3))
                        pe.wait_ge(out_done.sem, out_done.at(B + h * 4))
                    pe.matmul(VL[i % 2][:, :], slots[:, i * P:(i + 1) * P],
                              coefT[:, bass.ds(h * 512, 512)], start=True, stop=True).then_inc(scores_ready.sem, 1)
                    if i:
                        scatter_out(h, i - 1)
                scatter_out(h, 15)

        def act_slots():
            with A.loop(16, 0) as v:
                for r in range(2):
                    u = v * 2 + r
                    act.wait_ge(scores_ready.sem, scores_ready.at(u + 1))
                    act.activation(xv[:, r, :], psum[2 + r][:, :], ACT.Copy).then_inc(mix_done.sem, 1)

        def dve_slots():
            dve.sem_inc(aux5_ready.sem, 1)
            dve.wait_ge(aux6_ready.sem, aux6_ready.at(1))
            for i in range(2):
                dve.tensor_copy(coefT[:, i * 512:(i + 1) * 512], (TP, PJ[0])[i][0:8, :]).then_inc(dve_own, V.up())
            dve.wait_ge(dve_own, V.now())
            dve.sem_inc(slice_ready.sem, 1)
            dve.wait_ge(out_ready.sem, out_ready.at(1))
            for b in range(B):
                bank = (ZP, OP, PJ[1], PJ[2])[b // 2]
                dve.tensor_tensor(x[:, b, :], x[:, b, :], bank[:, (b % 2) * DM:(b % 2 + 1) * DM],
                                  ALU.add).then_inc(out_done.sem, 1)
            with V.loop(2, 0) as h:
                with V.loop(8, 0) as v:
                    for r in range(2):
                        u = h * 16 + v * 2 + r
                        dve.wait_ge(mix_done.sem, mix_done.at(u + 1))
                        dve.tensor_tensor(xg[:, r, :], psum[r][:, :], xv[:, r, :], ALU.mult).then_inc(probs_ready.sem, 1)
                dve.wait_ge(mix_ready.sem, mix_ready.at((h + 1) * 16))
                for t in range(4):
                    dve.tensor_tensor(x[:, bass.ds(h * 4 + t, 1), :], x[:, bass.ds(h * 4 + t, 1), :],
                                      psum[4 + t // 2][:, (t % 2) * DM:(t % 2 + 1) * DM].unsqueeze(1),
                                      ALU.add).then_inc(out_done.sem, 1)

        hid = work[:, 4096:5120].rearrange("p (r n) -> p r n", r=2)
        gat = work[:, 5120:6144].rearrange("p (r n) -> p r n", r=2)

        def pe_ffn(c):
            def down(r, e, h, f, first):
                v = (e * 2 + h) * c.nf + f
                if f == 0 and not c.keep:
                    pe.wait_ge(acc_done.sem, acc_done.at(e * 2 + h - 1))
                pe.wait_ge(hidden_done.sem, hidden_done.at(v + 1))
                opens = f == 0 and (not c.keep or first)
                for t in range(4):
                    bank = psum[4 + 2 * h + t // 2]
                    last = pe.matmul(bank[:, (t % 2) * DM:(t % 2 + 1) * DM], hid[:, f % 2, t * P:(t + 1) * P],
                                     c.down[r][:, f, :], start=(opens and t % 2 == 0), stop=(f == c.nf - 1),
                                     skip_group_check=True)
                if f == c.nf - 1:
                    last.then_inc(acc_ready.sem, 1)

            def tile(e, i, r, first):
                c.arrived(pe, i, r)
                for h in range(2):
                    for f in range(c.nf):
                        v = (e * 2 + h) * c.nf + f
                        pe.wait_ge(hidden_done.sem, hidden_done.at(v - 1))
                        if c.coef_rows is not None:
                            chunk, toks = c.coef_rows(e, f), slice(h * 512, (h + 1) * 512)
                        for g in range(2 if c.gated else 1):
                            bank = psum[2 * g + f % 2]
                            if g == 1 and c.coef_rows is not None:
                                pe.wait_ge(hidden_done.sem, hidden_done.at(v))
                                bank = psum[2]
                            for k in range(DC):
                                last = pe.matmul(bank[:, :], c.up[r](g, f, k), xnT[:, k, h * 512:(h + 1) * 512],
                                                 start=(k == 0), stop=(k == DC - 1))
                        if c.coef_rows is not None:
                            if first and v == 0:
                                pe_coef_parts()
                            last = pe.matmul(psum[3][:, :], chunk, coef_parts[0:96, toks], start=True, stop=True)
                        last.then_inc(up_ready.sem, 1)
                        if (h, f) != (0, 0):
                            down(r, e, *((h, f - 1) if f else (h - 1, c.nf - 1)), first)
                down(r, e, 1, c.nf - 1, first)

            peeled = 1 if c.keep else 0
            for e in range(2 * peeled):
                tile(e, 0, e, e == 0)
            with pe.Fori(peeled, c.E // 2) as i:
                for r in range(2):
                    tile(i * 2 + r, i, r, False)

        def act_step(c, e, h, f):
            v = (e * 2 + h) * c.nf + f
            act.wait_ge(up_ready.sem, up_ready.at(v + 1))
            if c.gated:
                act.activation(gat[:, f % 2, :], psum[f % 2][:, :], c.func).then_inc(gate_ready.sem, 1)
            else:
                stand_alone(act)
                act.activation(hid[:, f % 2, :], psum[f % 2][:, :], c.func,
                               bias=c.bias[:, bass.ds(e * c.nf + f, 1)]).then_inc(hidden_done.sem, 1)

        def act_ffn(c):
            with A.loop(c.E // 2, 0) as i:
                for r in range(2):
                    for h in range(2):
                        for f in range(c.nf):
                            act_step(c, i * 2 + r, h, f)

        def dve_step(c, e, h, f):
            v = (e * 2 + h) * c.nf + f
            dve.wait_ge(gate_ready.sem, gate_ready.at(v + 1))
            if c.coef_rows is None:
                dve.tensor_tensor(hid[:, f % 2, :], gat[:, f % 2, :], psum[2 + f % 2][:, :],
                                  ALU.mult).then_inc(hidden_done.sem, 1)
            else:
                dve.tensor_tensor(hid[:, f % 2, :], gat[:, f % 2, :], psum[2][:, :], ALU.mult).then_inc(dve_own, V.up())
                dve.wait_ge(dve_own, V.now())
                dve.tensor_tensor(hid[:, f % 2, :], hid[:, f % 2, :], psum[3][:, :],
                                  ALU.mult).then_inc(hidden_done.sem, 1)

        def dve_add_kept(c):
            for h in range(2):
                dve.wait_ge(acc_ready.sem, acc_ready.at(2 * c.E - 1 + h))
                for t in range(4):
                    last = dve.tensor_tensor(x[:, 4 * h + t, :], x[:, 4 * h + t, :],
                                             psum[4 + 2 * h + t // 2][:, (t % 2) * DM:(t % 2 + 1) * DM], ALU.add)
                last.then_inc(acc_done.sem, 1)
            dve.wait_ge(acc_done.sem, acc_done.at(2))

        def dve_ffn_kept(c):
            with V.loop(c.E // 2, 4 * c.nf) as i:
                for r in range(2):
                    for h in range(2):
                        for f in range(c.nf):
                            dve_step(c, i * 2 + r, h, f)
            dve_add_kept(c)

        def dve_ffn_added(c):
            with V.loop(c.E // 2, 0) as i:
                for r in range(2):
                    e = i * 2 + r
                    for h in range(2):
                        dve.wait_ge(acc_ready.sem, acc_ready.at(e * 2 + h + 1))
                        for t in range(4):
                            bank = psum[4 + 2 * h + t // 2][:, (t % 2) * DM:(t % 2 + 1) * DM]
                            b = 4 * h + t
                            last = dve.scalar_tensor_tensor(x[:, b, :], bank, coef[:, b, bass.ds(e, 1)], x[:, b, :],
                                                            ALU.mult, ALU.add)
                        last.then_inc(acc_done.sem, 1)

        def pe_output_bias():
            pe_coefT(8, psum[2:4])
            pe.wait_ge(slice_ready.sem, slice_ready.at(1))
            pe.wait_ge(acc_done.sem, acc_done.at(2 * s8.E - 1))
            for b in range(B):
                bank = (psum[0], psum[1], psum[4], psum[5])[b // 2]
                pe.matmul(bank[:, (b % 2) * DM:(b % 2 + 1) * DM], coefT[:, b * P:(b + 1) * P], b2e,
                          start=True, stop=True).then_inc(out_ready.sem, 1)

        def dve_output_bias():
            dve.wait_ge(aux6_ready.sem, aux6_ready.at(1))
            for i in range(2):
                dve.tensor_copy(coefT[:, i * 512:(i + 1) * 512], psum[2 + i][0:8, :]).then_inc(dve_own, V.up())
            dve.wait_ge(dve_own, V.now())
            dve.sem_inc(slice_ready.sem, 1)
            dve.wait_ge(acc_done.sem, acc_done.at(2 * s8.E))
            for i in range(4):
                dve.wait_ge(out_ready.sem, out_ready.at(2 * i + 2))
                pair_ = x[:, 2 * i:2 * i + 2, :]
                dve.tensor_tensor(pair_, pair_, (psum[0], psum[1], psum[4], psum[5])[i][:, :]
                                  .rearrange("p (t n) -> p t n", t=2), ALU.add).then_inc(out_done.sem, 1)
            dve.wait_ge(out_done.sem, out_done.at(4))

        def sp_ring(c):
            with sp.Fori(1, c.E // 2) as i:
                for r in range(2):
                    e = i * 2 + r
                    sp.wait_ge(acc_ready.sem, acc_ready.at(2 * e - 2))
                    c.load(r, e)

        coef_cols = small[:, 576:960].bitcast(BF16).rearrange("p (b e) -> p b e", b=B)
        coef_rest = small[:, 256:416].rearrange("p (b e) -> p b e", b=B)
        coef_parts = arena_b[0:96, 0:512].bitcast(BF16)

        def dve_coef_parts(E):
            dve.memset(coef_cols, 0.0).then_inc(dve_own, V.up())
            dve.wait_ge(dve_own, V.now())
            rest = coef[:, :, 0:E]
            for part in range(3):
                cols = coef_cols[:, :, 32 * part:32 * part + E]
                dve.tensor_copy(cols, rest).then_inc(dve_own, V.up())
                dve.wait_ge(dve_own, V.now())
                if part < 2:
                    dve.tensor_tensor(coef_rest[:, :, 0:E], rest, cols, ALU.subtract).then_inc(dve_own, V.up())
                    dve.wait_ge(dve_own, V.now())
                    rest = coef_rest[:, :, 0:E]
            dve.sem_inc(aux5_ready.sem, 1)
            for i in range(2):
                dve.wait_ge(proj_ready.sem, proj_ready.at(i + 1))
                dve.tensor_copy(coef_parts[:, i * 512:(i + 1) * 512], PJ[i + 1][0:96, :]).then_inc(slice_ready.sem, 1)

        def pe_coef_parts():
            pe.wait_ge(aux5_ready.sem, aux5_ready.at(1))
            for b in range(B):
                last = pe.matmul(PJ[b // 4 + 1][0:96, (b % 4) * P:(b % 4 + 1) * P], coef_cols[:, b, :], ident16[:, :],
                                 start=True, stop=True)
                if b % 4 == 3:
                    last.then_inc(proj_ready.sem, 1)
            pe.wait_ge(slice_ready.sem, slice_ready.at(2))
            pe.wait_ge(aux_ready.sem, aux_ready.at(1))

        W4 = 3 * DM
        codes = [arena_a[:, 2048 + r * W4:2048 + (r + 1) * W4].bitcast(I32) for r in range(2)]
        scales = [arena_a[:, 3584 + r * W4:3584 + (r + 1) * W4] for r in range(2)]
        mags = arena_a[:, 5120:6656]
        sgns = arena_a[:, 6656:8192]
        tops = arena_a[:, 8192:9728]
        sfac = arena_a[:, 9728:11264]
        wq4 = [arena_a[:, 11264 + r * 1536:11264 + (r + 1) * 1536] for r in range(2)]
        lows = arena_a[:, 14336:15872]
        minus6 = small[:, 976:977]

        def dve_dequant(i, r, piece, first=False):
            m, g, j = mags.bitcast(I32), sgns.bitcast(I32), i * 2 + r
            if piece == 0:
                dve.wait_ge(loaded["w5" + "ab"[r]], (i + 1) * 32)
                dve.wait_ge(scale_ready.sem, scale_ready.at(j))
                dve.tensor_scalar(m[:, 0:W4], codes[r], 7, None, ALU.bitwise_and).then_inc(dve_own, V.up())
                dve.tensor_scalar(m[:, W4:2 * W4], codes[r], 4, 7, ALU.logical_shift_right,
                                  ALU.bitwise_and).then_inc(dve_own, V.up())
                dve.tensor_scalar(g[:, 0:W4], codes[r], 8, None, ALU.bitwise_and)
                dve.tensor_scalar(g[:, W4:2 * W4], codes[r], 4, 8, ALU.logical_shift_right,
                                  ALU.bitwise_and).then_inc(codes_ready.sem, 1)
            elif piece == 1:
                dve.wait_ge(dve_own, V.now())
                dve.scalar_tensor_tensor(lows, m, 4.0, m, ALU.max, ALU.add).then_inc(dve_own, V.up())
            elif piece == 2:
                dve.wait_ge(dve_own, V.now())
                dve.wait_ge(top_ready.sem, top_ready.at(j + 1))
                dve.scalar_tensor_tensor(lows, lows, 0.5, tops, ALU.mult, ALU.add).then_inc(dve_own, V.up())
            else:
                dve.wait_ge(dve_own, V.now())
                dve.wait_ge(scale_ready.sem, scale_ready.at(j + 1))
                if not first:
                    dve.wait_ge(acc_ready.sem, acc_ready.at(j * 2 - 2))
                dve.scalar_tensor_tensor(wq4[r], lows, 2.0, sfac, ALU.subtract, ALU.mult).then_inc(weights_ready.sem, 1)

        def act_signs(j):
            act.wait_ge(codes_ready.sem, codes_ready.at(j + 1))
            act.wait_ge(weights_ready.sem, weights_ready.at(j))
            act.activation(tops, mags.bitcast(I32), ACT.Relu, bias=minus6).then_inc(top_ready.sem, 1)
            act.activation(sfac, sgns.bitcast(I32), ACT.Copy, scale=-0.25, bias=1.0).then_inc(sign_ready.sem, 1)

        def act_codes_ffn():
            act_signs(0)
            act_norm(5)
            with A.loop(3, 0) as i:
                for r in range(2):
                    for f in range(s5.nf):
                        act_step(s5, i * 2 + r, 0, f)
                    act_signs(i * 2 + r + 1)
                    for f in range(s5.nf):
                        act_step(s5, i * 2 + r, 1, f)
            for f in range(s5.nf):
                act_step(s5, 6, 0, f)
            act_signs(7)
            for h, e in ((1, 6), (0, 7), (1, 7)):
                for f in range(s5.nf):
                    act_step(s5, e, h, f)

        def dve_codes_ffn():
            def tile(e, i, r, first=False):
                for h in range(2):
                    for f in range(s5.nf):
                        dve_step(s5, e, h, f)
                        if i is not None:
                            dve_dequant(i, r, h * s5.nf + f, first)

            tile(0, 0, 1, True)
            with V.loop(3, 8) as i:
                tile(i * 2 + 1, i + 1, 0)
                tile(i * 2 + 2, i + 1, 1)
            tile(7, None, 0)
            dve_add_kept(s5)

        def pool_signed_scales():
            with G.loop(4, 0) as i:
                for r in range(2):
                    pool.wait_ge(sign_ready.sem, sign_ready.at(i * 2 + r + 1))
                    pool.tensor_tensor(sfac.rearrange("p (l n) -> p l n", l=2), sfac.rearrange("p (l n) -> p l n", l=2),
                                       scales[r].unsqueeze(1).to_broadcast([P, 2, W4]),
                                       ALU.mult).then_inc(scale_ready.sem, 1)

        xc = [work[:, k * 1024:(k + 1) * 1024].rearrange("p (b t) -> p b t", b=B) for k in range(DC)]
        dx = rows_(arena_b, 12288, 2, 1024)
        NT = B * P
        sp_, sn_, dl_, da_, bu_, hh_ = (work[0:64, 2048 + k * NT:2048 + (k + 1) * NT] for k in range(6))
        wB = rows_(arena_b, 8192, 2, 64)
        wC = rows_(arena_b, 8320, 2, 64)
        wD = rows_(arena_b, 8448, 2, 64)
        wIn = rows_(arena_b, 8576, 2, 64)
        wOut = arena_b[0:64, 8704:8960]
        cw = small[:, 544:552].rearrange("p (c k) -> p c k", c=DC)
        cbias = small[:, 552:554]
        dskip = small[:, 554:556]
        alog = small[0:64, 556:557]
        nega = small[0:64, 557:558]

        def dve_scan():
            dve.wait_ge(loaded["w9"], 16 * 9)
            dve.wait_ge(xnt_done.sem, xnt_done.at(B))
            xk = [xnT[:, k, :].rearrange("p (b t) -> p b t", b=B) for k in range(DC)]
            for k in range(DC):
                dve.tensor_scalar(xc[k], xk[k], cw[:, k, 3:4], cbias[:, k:k + 1], ALU.mult,
                                  ALU.add).then_inc(dve_own, V.up())
            for d in range(1, 4):
                dve.wait_ge(dve_own, V.now())
                for k in range(DC):
                    dve.scalar_tensor_tensor(xc[k][:, :, d:P], xk[k][:, :, 0:P - d], cw[:, k, 3 - d:4 - d],
                                             xc[k][:, :, d:P], ALU.mult, ALU.add).then_inc(dve_own, V.up())
            dve.wait_ge(dve_own, V.now())
            dve.sem_inc(aux3_ready.sem, 1)
            for k in range(DC):
                dve.tensor_scalar(dx[:, k, :], xc[k].rearrange("p b t -> p (b t)"), dskip[:, k:k + 1], None,
                                  ALU.mult).then_inc(dve_own, V.up())
            dve.wait_ge(aux_ready.sem, aux_ready.at(3))
            for i in range(2):
                half = slice(i * 512, (i + 1) * 512)
                dve.tensor_scalar(sp_[:, half], psum[4 + i][0:64, :], 0.0, None, ALU.max).then_inc(dve_own, V.up())
                dve.tensor_scalar(sn_[:, half], psum[4 + i][0:64, :], 0.0, None, ALU.min).then_inc(dve_own, V.up())
            dve.wait_ge(dve_own, V.now())
            dve.tensor_tensor(sn_, sn_, sp_, ALU.subtract).then_inc(aux4_ready.sem, 1)
            dve.wait_ge(aux5_ready.sem, aux5_ready.at(1))
            dve.tensor_tensor(dl_, dl_, sp_, ALU.add).then_inc(dve_own, V.up())
            dve.wait_ge(dve_own, V.now())
            dve.sem_inc(aux6_ready.sem, 1)
            for i in range(2):
                half = slice(i * 512, (i + 1) * 512)
                dve.tensor_tensor(bu_[:, half], dl_[:, half], psum[i][0:64, :], ALU.mult).then_inc(dve_own, V.up())
            dve.wait_ge(dve_own, V.now())
            dve.wait_ge(aux2_ready.sem, aux2_ready.at(1))
            for i in range(2):
                half = slice(i * 512, (i + 1) * 512)
                dve.tensor_tensor(bu_[:, half], bu_[:, half], psum[6 + i][0:64, :], ALU.mult).then_inc(dve_own, V.up())
            dve.wait_ge(aux5_ready.sem, aux5_ready.at(2))
            dve.memset(da_.rearrange("p (b t) -> p b t", b=B)[:, :, 0:1], 0.0).then_inc(dve_own, V.up())
            dve.wait_ge(dve_own, V.now())
            dve.tensor_tensor_scan(hh_, da_, bu_, 0.0, ALU.mult, ALU.add).then_inc(dve_own, V.up())
            dve.wait_ge(dve_own, V.now())
            for i in range(2):
                half = slice(i * 512, (i + 1) * 512)
                last = dve.tensor_tensor(hh_[:, half], hh_[:, half], psum[2 + i][0:64, :], ALU.mult)
                last.then_inc(slice_ready.sem, 1)
            for b in range(B):
                dve.wait_ge(out_ready.sem, out_ready.at(b + 1))
                dve.tensor_tensor(x[:, b, :], x[:, b, :], psum[b % 4][:, 0:DM], ALU.add).then_inc(out_done.sem, 1)

        def act_scan():
            act.wait_ge(loaded["w9"], 16 * 9)
            act.activation(nega, alog, ACT.Exp).then_inc(act_own, A.up())
            act.wait_ge(act_own, A.now())
            act.activation(nega, nega, ACT.Copy, scale=-1.0).then_inc(act_own, A.up())
            act.wait_ge(act_own, A.now())
            act.wait_ge(aux4_ready.sem, aux4_ready.at(1))
            act.activation(sn_, sn_, ACT.Exp).then_inc(act_own, A.up())
            act.wait_ge(act_own, A.now())
            act.activation(dl_, sn_, ACT.Ln, bias=1.0).then_inc(aux5_ready.sem, 1)
            act.wait_ge(aux6_ready.sem, aux6_ready.at(1))
            act.activation(da_, dl_, ACT.Exp, scale=nega).then_inc(aux5_ready.sem, 1)

        def pe_scan():
            pe.wait_ge(loaded["w9"], 16 * 9)
            for n, w in enumerate((wB, wC, wD)):
                for i in range(2):
                    for k in range(DC):
                        last = pe.matmul(psum[2 * n + i][0:64, :], w[:, k, :], xnT[:, k, i * 512:(i + 1) * 512],
                                         start=(k == 0), stop=(k == DC - 1))
                last.then_inc(aux_ready.sem, 1)
            pe.wait_ge(aux3_ready.sem, aux3_ready.at(1))
            for i in range(2):
                for k in range(DC):
                    last = pe.matmul(psum[6 + i][0:64, :], wIn[:, k, :],
                                     work[:, k * 1024 + i * 512:k * 1024 + (i + 1) * 512],
                                     start=(k == 0), stop=(k == DC - 1))
            last.then_inc(aux2_ready.sem, 1)
            pe.wait_ge(slice_ready.sem, slice_ready.at(2))
            for b in range(B):
                if b >= 4:
                    pe.wait_ge(out_done.sem, out_done.at(b - 3))
                toks = slice(b * P, (b + 1) * P)
                pe.matmul(psum[b % 4][:, 0:DM], hh_[:, toks], wOut, start=True, stop=False, skip_group_check=True)
                for k in range(DC):
                    last = pe.matmul(psum[b % 4][:, k * P:(k + 1) * P], dx[:, k, toks], ident[:, :],
                                     start=False, stop=(k == DC - 1), skip_group_check=True)
                last.then_inc(out_ready.sem, 1)

        bqT, bkT = small[:, 32:48], small[:, 48:64]
        bo0, bv0 = small[:, 256:512], work[:, 7168:9216]
        s0 = Attention(wq=rows_(arena_a, 0, 2, 2048), wk=rows_(arena_a, 4096, 2, 2048), wv=rows_(arena_a, 8192, 2, 2048),
                 wo=rows_(arena_a, 12288, 16, DM), bq=bqT, bk=bkT, bv=bv0, bo=bo0, causal=True,
                 scale=128 ** -0.5, w="w0", nw=8)

        wts1 = [(rows_(ar, 0, 2, DM), rows_(ar, 512, 2, DM), rows_(ar, 1024, 2, 64), rows_(ar, 1152, 2, DM))
                for ar in (arena_b, arena_a)]
        s1 = Attention(wq=wts1[0][0], wk=wts1[0][1], wv=wts1[0][2], wo=wts1[0][3], bq=small[:, 560:562],
                 bk=small[:, 562:564], bv=small[:, 564:628], bo=small[:, 640:896], cross=True, scale=8 ** -0.5,
                 w="w1", nw=10)
        s3 = Attention(wq=wts1[1][0], wk=wts1[1][1], wv=wts1[1][2], wo=wts1[1][3], causal=True, scale=8 ** -0.5,
                 w="w3", nw=4)
        wts5 = [w.rearrange("p (l m n) -> p l m n", l=2, m=3) for w in wq4]
        s5 = FeedForward(E=8, nf=2, gated=True, func=ACT.Gelu_apprx_tanh, keep=True,
                 up=[lambda g, f, k, w=w: w[:, k, g, f::2] for w in wts5], down=[w[:, :, 2, :] for w in wts5],
                 arrived=lambda eng, i, par: eng.wait_ge(weights_ready.sem, weights_ready.at(i * 2 + par + 1)))
        s6 = Attention(wq=rows_(arena_b, 0, 2, 2048), wk=rows_(arena_b, 4096, 2, 512), wv=rows_(arena_b, 5120, 2, 512),
                 wo=rows_(arena_b, 6144, 16, DM), cos=arena_b[:, 10240:10368], sin=arena_b[:, 10368:10496],
                 gqa=True, causal=True, rope=True, scale=128 ** -0.5, w="w6", nw=6)
        s7 = Attention(wq=s0.wq, wk=s0.wk, wv=s0.wv, wo=s0.wo, cross=True, scale=128 ** -0.5, w="w7", nw=4)
        fc1 = [rows_(arena_b, 4096 * r, 2, 1024) for r in range(2)]
        fc2 = [rows_(arena_b, 4096 * r + 2048, 8, DM) for r in range(2)]
        b2e, gatew8 = arena_b[0:8, 9216:9472], rows_(arena_b, 9472, 2, 8)
        gateb8, alpha8 = small[:, 960:968], small[:, 968:976]
        s8 = FeedForward(E=8, nf=8, gated=False, func=ACT.Gelu, bias=small[:, 896:960],
                 up=[lambda g, f, k, w=w: w[:, k, f * P:(f + 1) * P] for w in fc1], down=fc2,
                 arrived=lambda eng, i, par: eng.wait_ge(loaded["w8" + "ab"[par]], (i + 1) * 32),
                 load=lambda r, e: load_expert(fc1, "fc1", fc2, "fc2", "w8", r, e))
        wts11 = [arena_a[:, 1536 * r:1536 * (r + 1)] for r in range(2)]
        w13 = [w[:, 0:1024].rearrange("p (g k n) -> p g k n", g=2, k=DC) for w in wts11]
        w2 = [rows_(w, 1024, 2, DM) for w in wts11]
        gatew11, sgate11 = rows_(arena_a, 4096, 2, 16), rows_(arena_a, 4128, 2, 1)
        chunk_experts = arena_a[0:96, 8192:8192 + 28 * P]
        chunk_experts16 = arena_b[0:96, 1024:1024 + 14 * P].bitcast(BF16)
        s11 = FeedForward(E=14, nf=2, gated=True, func=ACT.Silu, keep=True,
                  up=[lambda g, f, k, w=w: w[:, g, k, f * P:(f + 1) * P] for w in w13], down=w2,
                  coef_rows=lambda e, f: chunk_experts16[:, bass.ds((e * 2 + f) * P, P)],
                  arrived=lambda eng, i, par: eng.wait_ge(loaded["w11" + "ab"[par]], (i + 1) * 16),
                  load=lambda r, e: load_tile(wts11, "tiles11", "w11", r, e))

        def load_tile(dst, name, landed, r, e):
            src = D[name][e] if isinstance(e, int) else D[name][bass.ds(e, 1)].rearrange("e p n -> (e p) n")
            sp.dma_start(dst[r], src).then_inc(loaded[landed + "ab"[r]], 16)

        def load_expert(ups, up_name, downs, down_name, landed, r, e):
            for dst, name in ((ups[r], up_name), (downs[r], down_name)):
                src = D[name][e] if isinstance(e, int) else D[name][bass.ds(e, 1)].rearrange("e p k n -> (e p) k n")
                sp.dma_start(dst, src).then_inc(loaded[landed + "ab"[r]], 16)

        def n(k, *which):
            return {w: k for w in which}

        units = ("scores_ready", "max_ready", "exp_done", "probsT_ready", "probsT_done")
        softmax = units + ("recip_ready", "probs_ready")
        norm = n(1, "var_ready", "std_ready") | n(B, "xn_ready", "xnt_ready", "xnt_done")
        attn128 = norm | n(4 * B, *softmax, "mix_ready", "mix_done", "out_ready", "out_done") \
            | n(12 * B, "proj_ready", "proj_done")
        attn8 = norm | n(8 * B, *units, "mix_ready", "kpad_ready") \
            | n(B, "slice_ready", "mix_done", "aux_ready", "aux_done", "out_ready", "out_done") \
            | n(2 * B, "proj_ready") | n(3 * B, "proj_done")
        route = n(1, "aux2_ready", "aux3_ready", "aux4_ready")

        def ffn(c):
            return n(2 * c.E * c.nf, "up_ready", "hidden_done", *(["gate_ready"] if c.gated else [])) \
                | n(2 * c.E, "acc_ready") | n(2 if c.keep else 2 * c.E, "acc_done")

        steps = {
            0: attn128 | n(B // s0.ns, "slice_ready"),
            1: attn8 | n(1, "aux2_ready"),
            2: norm | route | n(1, "aux_ready", "aux5_ready", "aux6_ready") | n(2, "aux_done") | n(3, "slice_ready")
            | n(5, "proj_ready") | n(4, "proj_done") | n(1, "out_ready") | n(16, "out_done")
            | n(32, "scores_ready", "mix_done", "probs_ready", "mix_ready"),
            3: attn8,
            4: norm | n(2, *softmax, "out_ready") | n(1, "aux2_ready") | n(B, "out_done"),
            5: norm | ffn(s5) | n(8, "codes_ready", "top_ready", "sign_ready", "scale_ready", "weights_ready"),
            6: attn128 | n(B, "slice_ready") | n(8 * B, "aux_ready", "aux2_ready"),
            7: attn128 | n(B // s7.ns, "slice_ready"),
            8: norm | route | n(1, "aux5_ready", "aux6_ready", "slice_ready") | n(B, "out_ready") | n(4, "out_done")
            | ffn(s8),
            9: norm | n(3, "aux_ready") | n(1, "aux2_ready", "aux3_ready", "aux4_ready", "aux6_ready")
            | n(2, "aux5_ready", "slice_ready") | n(B, "out_ready", "out_done"),
            10: n(1, "var_ready", "std_ready") | n(B, "xn_ready", "mix_done", "out_ready", "out_done")
            | n(8 * B, *units, "mix_ready", "kpad_ready"),
            11: norm | route | n(1, "aux_ready", "aux5_ready", "aux6_ready") | n(2, "proj_ready", "slice_ready")
            | ffn(s11),
        }
        bases, total = {}, {t.sem.name: 0 for t in tallies}
        for s in stages:
            bases[s] = dict(total)
            for n, k in steps[s].items():
                total[n] += k
        rest_at = min(s for s in stages if s) if any(stages) else None
        done_before = {s: k for k, s in enumerate(stages)}

        def enter(eng, s):
            for t in tallies:
                t.base = bases[s][t.sem.name]
            if done_before[s]:
                eng.wait_ge(stage_done.sem, done_before[s] + 1)

        block = ctx.enter_context(nc.Block())

        @block.sync
        def _(sp_eng):
            def load(landed, *pairs):
                if landed[0] == "w" and int(landed.strip("wab")) not in stages and pairs[0][1] != "mask_pair":
                    return
                for dst, name in pairs:
                    sp.dma_start(dst, name if not isinstance(name, str) else D[name]).then_inc(loaded[landed], 16)

            def after(s):
                if s in done_before:
                    sp.wait_ge(stage_done.sem, done_before[s] + 2)

            def every(name):
                return D[name].partition_broadcast(P)

            load("x", (x[:, :, :], D["x"].rearrange("b t d -> t b d")))
            load("const", (ident[:, :], "ident"), (xn4[:, 0, 0:P], "causal"))
            if 0 in stages:
                for g in range(4):
                    cols = slice(g * 512, (g + 1) * 512)
                    for dst, name in ((s0.wq, "wq0"), (s0.wk, "wk0"), (s0.wv, "wv0")):
                        sp.dma_start(dst[:, :, cols], D[name][:, :, cols]).then_inc(loaded[f"w0_{g}"], 16)
                    if g == 0:
                        load("w0", (s0.bq, "bqT"), (s0.bk, "bkT"), (s0.bo, every("bo0")), (s0.bv, every("bv0")))
                    sp.dma_start(s0.wo[:, 4 * g:4 * g + 4, :], D["wo0"][:, 4 * g:4 * g + 4, :]).then_inc(loaded[f"w0_{g}"], 16)
            load("rest", (heads8[:, :], "heads8"), (heads16[:, :], "heads16"), (tri[:, :, :], every("tri")),
                 (iotaf[:, :], every("iotaf")), (iotap[:, :], "iotap"))
            load("ctx", (ctxn[:, :, :], D["ctx"].rearrange("b t d -> t b d")), (ctxT[:, :, :], "ctxT"))
            if 1 in stages:
                load("w1", (s1.wq, "wq1"), (s1.wk, "wk1"), (s1.wv, "wv1"), (s1.wo, "wo1"), (s1.bq, "bq1"),
                     (s1.bk, "bk1"), (s1.bv, every("bv1")), (s1.bo, every("bo1")))
            load("w1", (pair_mask[:, :], "mask_pair"), (row_mask[:, :, :], every("mask_row")))
            if 2 in stages:
                load("w2", (WT, "WT"), (atoms, "atoms"), (slots, "importance"), (eaw, "eaw"), (gatewT, "gatew2"),
                     (rowsi, "slot_rows"), (colsi, every("slot_cols")))
            after(0)
            load("w3", (s3.wq, "wq3"), (s3.wk, "wk3"), (s3.wv, "wv3"), (s3.wo, "wo3"))
            if 5 in stages:
                for r in range(2):
                    load("w5" + "ab"[r], (codes[r], D["codes"][r]), (scales[r], D["scales"][r]))
            after(1)
            after(2)
            if 6 in stages:
                load("w6", (s6.wq, "wq6"), (s6.wk, "wk6"), (s6.wv, "wv6"), (s6.wo, "wo6"), (s6.cos, "cosT"),
                     (s6.sin, "sinT"))
            if 5 in stages:
                enter(sp, 5)
                with sp.Fori(1, 4) as i:
                    for r in range(2):
                        j = i * 2 + r
                        sp.wait_ge(scale_ready.sem, scale_ready.at(j - 1))
                        for dst, name in ((codes[r], "codes"), (scales[r], "scales")):
                            sp.dma_start(dst, D[name][bass.ds(j, 1)].rearrange("e p n -> (e p) n")
                                         ).then_inc(loaded["w5" + "ab"[r]], 16)
            after(5)
            if 7 in stages:
                load("w7", (s7.wq, "wq7"), (s7.wk, "wk7"), (s7.wv, "wv7"), (s7.wo, "wo7"))
            after(6)
            load("w8", (b2e, "b2e"), (gatew8, "gatew8"), (gateb8, every("gateb8")), (alpha8, every("alpha8")),
                 (s8.bias, "b1T"))
            if 8 in stages:
                for r in range(2):
                    s8.load(r, r)
            load("w9", (wB, "wB9"), (wC, "wC9"), (wD, "wD9"), (wIn, "wIn9"), (wOut, "wOut9"), (cw, "cw9"),
                 (cbias, "cb9"), (dskip, "dskip9"), (alog, "alog9"))
            after(7)
            load("w11", (gatew11, "gatew11"), (sgate11, "sgate11"), (chunk_experts, "chunk_experts"))
            if 11 in stages:
                for r in range(2):
                    s11.load(r, r)
            for s, c in ((8, s8), (11, s11)):
                if s in stages:
                    enter(sp, s)
                    sp_ring(c)
            sp.wait_ge(stage_done.sem, len(stages) + 1)
            sp.dma_start(out.rearrange("b t d -> t b d"), x[:, :, :]).then_inc(stored, 16)
            sp.wait_ge(stored, 16)

        @block.gpsimd
        def _(pool_eng):
            for t in tallies:
                pool.sem_inc(t.sem, t.credit)
            pool.sem_inc(credits_given, 1)
            for s in stages:
                if s == rest_at:
                    pool.wait_ge(loaded["rest"], 16 * 5)
                    pool.wait_ge(loaded["ctx"], 32)
                    if 2 in stages:
                        pool_gather()
                if s == 2:
                    pool_scatter()
                enter(pool, s)
                if s in (0, 6, 7):
                    pool_attn128(s, {0: s0, 6: s6, 7: s7}[s])
                elif s in (1, 3):
                    pool_small(s, {1: s1, 3: s3}[s])
                elif s == 4:
                    pool_memory(s)
                elif s == 5:
                    pool_signed_scales()
                elif s == 10:
                    pool_small(s, None)
                elif s == 11:
                    pool.wait_ge(loaded["w11"], 48)
                    pool.tensor_copy(chunk_experts16, chunk_experts).then_inc(aux_ready.sem, 1)

        @block.scalar
        def _(act_eng):
            act.wait_ge(credits_given, 1)
            act.wait_ge(loaded["const"], 32)
            for s in stages:
                act.activation(scrap[:, :], ident[:, 0:1], ACT.Sqrt)
                enter(act, s)
                if s == 2:
                    act_slots_prepare()
                if s != 5:
                    act_norm(s, natural if s == 10 else None)
                if s in (0, 6, 7):
                    act_attn128(s, {0: s0, 6: s6, 7: s7}[s])
                elif s in (1, 3):
                    act_small(s, {1: s1, 3: s3}[s])
                elif s == 2:
                    act_route(8)
                    act_slots()
                elif s == 4:
                    act_memory(s)
                elif s == 5:
                    act_codes_ffn()
                elif s == 8:
                    act.wait_ge(loaded["w8"], 16 * 5)
                    act_route(8)
                    act_ffn(s8)
                elif s == 9:
                    act_scan()
                elif s == 10:
                    act_small(s, None)
                elif s == 11:
                    act.wait_ge(aux2_ready.sem, aux2_ready.at(1))
                    act.activation(coef[:, :, 16:20], PJ[1][:, 0:B].unsqueeze(2).to_broadcast([P, B, 4]),
                                   ACT.Sigmoid).then_inc(aux6_ready.sem, 1)
                    act_route(16)
                    act_ffn(s11)

        @block.vector
        def _(dve_eng):
            dve.wait_ge(credits_given, 1)
            dve.wait_ge(loaded["const"], 32)
            dve.tensor_copy(ident16[:, :], ident[:, :]).then_inc(masks16_ready, 1)
            dve.tensor_copy(causal16[:, :], xn4[:, 0, 0:P]).then_inc(masks16_ready, 1)
            dve.wait_ge(loaded["x"], 16)
            if 2 in stages and 0 not in stages:
                for piece in range(2):
                    dve_slot_numbers(piece)
            for s in stages:
                if s == rest_at:
                    dve.wait_ge(loaded["rest"], 16 * 5)
                enter(dve, s)
                if s == 1:
                    dve.wait_ge(loaded["w1"], 16 * 10)
                    dve.tensor_tensor(mask16[:, :, :], row_mask[:, :, :],
                                      pair_mask[:, :].unsqueeze(1).to_broadcast([P, B, P]),
                                      ALU.max).then_inc(dve_own, V.up())
                    dve.wait_ge(dve_own, V.now())
                    dve.tensor_scalar(mask16[:, :, :], mask16[:, :, :], NEG, None, ALU.mult).then_inc(aux2_ready.sem, 1)
                elif s == 2:
                    dve_slots_prepare()
                elif s == 4:
                    dve.wait_ge(loaded["w1"], 16 * (10 if 1 in stages else 2))
                    dve.tensor_scalar(mask16[:, :, :], row_mask[:, :, :], -NEG, NEG, ALU.mult,
                                      ALU.add).then_inc(aux2_ready.sem, 1)
                    dve.tensor_reduce(valid, row_mask[:, :, :], AX, ALU.max).then_inc(dve_own, V.up())
                elif s == 5:
                    dve.memset(minus6, -6.0)
                    for piece in range(4):
                        dve_dequant(0, 0, piece, first=True)
                dve_norm(s, natural if s == 10 else None)
                if s in (0, 6, 7):
                    dve_attn128(s, {0: s0, 6: s6, 7: s7}[s])
                    dve.wait_ge(out_done.sem, out_done.at(4 * B))
                elif s in (1, 3):
                    dve_small(s, {1: s1, 3: s3}[s])
                    dve.wait_ge(out_done.sem, out_done.at(B))
                elif s == 2:
                    dve_route(8, 2, clip=50.0)
                    dve_slots()
                    dve.wait_ge(out_done.sem, out_done.at(2 * B))
                elif s == 4:
                    dve_memory(s)
                    dve.wait_ge(out_done.sem, out_done.at(B))
                elif s == 5:
                    dve_codes_ffn()
                elif s == 8:
                    dve.wait_ge(loaded["w8"], 16 * 5)
                    dve_route(8, 2, bias=gateb8, alpha=alpha8)
                    dve.sem_inc(aux5_ready.sem, 1)
                    dve_ffn_added(s8)
                    dve_output_bias()
                elif s == 9:
                    dve_scan()
                    dve.wait_ge(out_done.sem, out_done.at(B))
                elif s == 10:
                    dve_small(s, None)
                    dve.wait_ge(out_done.sem, out_done.at(B))
                elif s == 11:
                    dve_route(16, 4, over_all=True)
                    dve.wait_ge(aux6_ready.sem, aux6_ready.at(1))
                    dve_coef_parts(20)
                    dve_ffn_kept(s11)
                dve.sem_inc(stage_done.sem, 1)

        @block.tensor
        def _(pe_eng):
            pe.wait_ge(credits_given, 1)
            pe.wait_ge(masks16_ready, 2)
            pe.wait_ge(loaded["const"], 32)
            for s in stages:
                if s == rest_at:
                    pe.wait_ge(loaded["ctx"], 32)
                enter(pe, s)
                if s == 2:
                    pe.wait_ge(loaded["w2"], 16 * 7)
                    pe_slots_prepare()
                if s != 10:
                    pe_norm(s, 2 if s == 5 else 1)
                    pe.wait_ge(xnt_done.sem, xnt_done.at(B))
                if s in (0, 6, 7):
                    pe_attn128(s, {0: s0, 6: s6, 7: s7}[s])
                elif s in (1, 3):
                    if s == 1:
                        pe.wait_ge(aux2_ready.sem, aux2_ready.at(1))
                    pe_small(s, {1: s1, 3: s3}[s])
                elif s == 2:
                    pe_route(8, gatewT)
                    pe_slots()
                elif s == 4:
                    pe_memory(s)
                elif s == 5:
                    pe_ffn(s5)
                elif s == 8:
                    pe.wait_ge(loaded["w8"], 16 * 5)
                    pe_route(8, gatew8)
                    pe.wait_ge(aux3_ready.sem, aux3_ready.at(1))
                    pe_ffn(s8)
                    pe_output_bias()
                elif s == 9:
                    pe_scan()
                elif s == 10:
                    pe_small(s, None)
                elif s == 11:
                    pe.wait_ge(loaded["w11"], 48)
                    pe_route(16, gatew11, sgate11)
                    pe.wait_ge(aux3_ready.sem, aux3_ready.at(1))
                    pe.wait_ge(aux6_ready.sem, aux6_ready.at(1))
                    pe_ffn(s11)


def layouts(I):
    c = np.ascontiguousarray

    def kxn(w):
        return c(w.reshape(-1, P, w.shape[-1]).transpose(1, 0, 2))

    def col(v, n):
        return c(v.reshape(n, P).T)

    d = {"x": I["x"], "ctx": I["ctx_2048"], "ctxT": kxn(I["ctx_2048"].reshape(B * P, DM).T)}
    d["mask_pair"], d["mask_row"] = I["mask_SxS2_bc0"], I["mask_BxS2_bk0"]
    d["bqT"], d["bkT"] = c(I["L0_attn_b_Q"].T), c(I["L0_attn_b_K"].T)
    d["bv0"], d["bo0"] = I["L0_attn_b_V"].reshape(-1), I["L0_attn_b_O"]
    for n, k in (("wq0", "W_Q"), ("wk0", "W_K"), ("wv0", "W_V")):
        d[n] = kxn(I["L0_attn_" + k].transpose(1, 0, 2).reshape(DM, -1))
    d["wo0"] = c(I["L0_attn_W_O"].transpose(1, 0, 2))
    rep = np.arange(DM) // 32 * 8 + np.arange(DM) % 8
    for s, p in (("1", "L0_xattn_"), ("3", "L1_attn_")):
        d["wq" + s], d["wk" + s] = kxn(I[p + "Wq"].T), kxn(I[p + "Wk"][rep].T)
        d["wv" + s], d["wo" + s] = kxn(I[p + "Wv"].T), kxn(I[p + "Wo"].T)
    d["bq1"], d["bk1"] = col(I["L0_xattn_bq"], 2), col(I["L0_xattn_bk"][rep], 2)
    d["bv1"], d["bo1"] = I["L0_xattn_bv"], I["L0_xattn_bo"]
    d["WT"], d["atoms"], d["importance"] = kxn(I["L0_ffn_W"].T), I["L0_ffn_atoms"], I["L0_ffn_importance"]
    d["eaw"], d["gatew2"] = I["L0_ffn_expert_atom_weights"], kxn(I["L0_ffn_gate_w"].T)
    d["slot_cols"], d["slot_rows"] = I["L0_ffn_mask_idx"], col(I["L0_ffn_mask_idx"], 16)
    def tiles(gate, up, down):
        g, u = (w.reshape(8, DM, P).transpose(0, 2, 1) for w in (gate, up))
        return c(np.stack([g, u, down.reshape(DM, 8, P).transpose(1, 2, 0)], axis=2).reshape(8, P, 3 * DM))

    d["codes"] = tiles(*(I[f"L1_ffn_{k}_W_packed"] for k in ("gate", "up", "down")))
    d["scales"] = tiles(*(np.repeat(I[f"L1_ffn_{k}_scales"], 16, axis=1) for k in ("gate", "up", "down")))
    for n in "qkv":
        d[f"w{n}6"], d[f"w{n}7"] = kxn(I["L2_attn_w_" + n]), kxn(I["L2_xattn_W" + n])
    d["wo6"], d["wo7"] = kxn(I["L2_attn_w_o"]), kxn(I["L2_xattn_Wo"])
    d["fc1"] = c(I["L2_ffn_fc1_w"].reshape(8, DC, P, 1024).transpose(0, 2, 1, 3))
    d["fc2"] = c(I["L2_ffn_fc2_w"].reshape(8, 8, P, DM).transpose(0, 2, 1, 3))
    d["b1T"], d["b2e"] = col(I["L2_ffn_fc1_b"].reshape(-1), 64), I["L2_ffn_fc2_b"]
    d["gatew8"], d["gateb8"], d["alpha8"] = kxn(I["L2_ffn_gate_w"]), I["L2_ffn_gate_b"], I["L2_ffn_alpha"]
    wx = I["L3_attn_Wxproj"]
    d["wB9"], d["wC9"] = kxn(wx[0:64].T), kxn(wx[64:128].T)
    d["wD9"] = kxn(np.repeat(wx[128:129], 64, axis=0).T)
    d["wIn9"], d["wOut9"] = kxn(I["L3_attn_Winproj"].T), c(I["L3_attn_Woutproj"].T)
    d["cw9"] = c(I["L3_attn_conv_w"].reshape(DC, P, 4).transpose(1, 0, 2))
    d["cb9"], d["dskip9"] = col(I["L3_attn_conv_b"], 2), col(I["L3_attn_D"], 2)
    d["alog9"] = I["L3_attn_A_log"].reshape(64, 1)
    w13, w2 = I["L3_ffn_w13"], I["L3_ffn_w2"]
    sgu, sd = I["L3_ffn_shared_gate_up_w"], I["L3_ffn_shared_down_w"]
    sh13 = sgu.reshape(2, 4, 176, DM).transpose(1, 0, 2, 3).reshape(4, 352, DM)
    sh2 = sd.reshape(DM, 4, 176).transpose(1, 0, 2)
    w13, w2 = np.concatenate([w13, sh13]), np.concatenate([w2, sh2])
    pad = ((0, 28 * P - 20 * 176), (0, 0))
    gu = [np.pad(w13[:, g * 176:(g + 1) * 176].reshape(-1, DM), pad).reshape(14, DM, DC, P).transpose(0, 3, 2, 1)
          for g in range(2)]
    dn = np.pad(w2.transpose(0, 2, 1).reshape(-1, DM), pad).reshape(14, 2, P, DM).transpose(0, 2, 1, 3)
    d["tiles11"] = c(np.concatenate([t.reshape(14, P, -1) for t in (*gu, dn)], axis=2))
    owner = np.where(np.arange(28 * P) < 20 * 176, np.arange(28 * P) // 176, -1)
    d["chunk_experts"] = (np.arange(96)[:, None] % 32 == owner).astype(np.float32)
    d["gatew11"], d["sgate11"] = kxn(I["L3_ffn_gate_w"].T), kxn(I["L3_ffn_sgate_w"].T)
    t = np.arange(P)
    d["ident"] = np.eye(P, dtype=np.float32)
    d["causal"] = np.where(t[None, :] <= t[:, None], 0.0, NEG).astype(np.float32)
    d["heads8"] = (t[:, None] // 8 == np.arange(16)).astype(np.float32)
    d["heads16"] = (t[:, None] // 16 == np.arange(8)).astype(np.float32)
    d["tri"] = np.tril(np.ones((16, 16), np.float32), -1)
    d["iotaf"] = np.arange(DM, dtype=np.float32)
    d["iotap"] = np.stack([t, t + P], 1).astype(np.float32)
    inv = 1.0 / np.float32(10000.0) ** (np.arange(0, P, 2, dtype=np.float32) / np.float32(P))
    ang = np.outer(np.arange(P, dtype=np.float32), inv).astype(np.float32)
    d["cosT"] = c(np.concatenate([np.cos(ang), np.cos(ang)], 1).T.astype(np.float32))
    d["sinT"] = c(np.concatenate([-np.sin(ang), np.sin(ang)], 1).T.astype(np.float32))
    return d


STAGES = tuple(range(12))


def kernel(**inputs):
    import concourse.bacc as bacc
    from concourse.bass_utils import run_bass_kernel_spmd

    nc = bacc.Bacc("TRN2", target_bir_lowering=False, num_devices=1)
    arrays = layouts({k: np.asarray(v) for k, v in inputs.items()})
    D = {n: nc.dram_tensor("in_" + n, a.shape, mybir.dt.from_np(a.dtype), kind="ExternalInput").ap()
         for n, a in arrays.items()}
    out = nc.dram_tensor("out", (B, P, DM), F32, kind="ExternalOutput").ap()
    build(nc, D, out, STAGES)
    got = run_bass_kernel_spmd(nc, [{"in_" + n: a for n, a in arrays.items()}], core_ids=[0])
    return got.results[0]["out"]
```
